# Optimizing a Trainium2 kernel written in Bass

```python
import numpy as np
import jax
import jax.numpy as jnp

def _softmax(x, axis=-1):
    return jax.nn.softmax(x, axis=axis)

def _gelu(x):
    return jax.nn.gelu(x, approximate=True)

def _silu(x):
    return jax.nn.silu(x)

def _sigmoid(x):
    return jax.nn.sigmoid(x)

def _layernorm(x, axis=-1, eps=1e-05):
    m = jnp.mean(x, axis=axis, keepdims=True)
    v = jnp.var(x, axis=axis, keepdims=True)
    return (x - m) / jnp.sqrt(v + eps)

def _scatter_add(tgt, idx, src, axis=0):
    return tgt.at[idx].add(src)

def _segment_sum(src, seg, n):
    return jax.ops.segment_sum(src, seg, n)
kernel_name = 'mk_hybrid_d1_jaxref_r8_f5af06'

def setup_inputs(seed: int=0):
    np.random.seed(seed)
    _w = jnp.asarray

    def _L0_attn_a_setup():
        import jax, jax.numpy as jnp
        import numpy as np
        import math
        D_MODEL = 128
        N_HEADS = 16
        HEAD_DIM = D_MODEL // N_HEADS
        FEAT = 16
        WINDOW = 64
        EPS_NORM = 1e-06
        EPS_LIN = 1e-06
        CHUNK = 128

        def rmsnorm(x, w):
            return x * jax.lax.rsqrt(jnp.mean(x * x, axis=-1, keepdims=True) + EPS_NORM) * w

        def taylor_feature_map(x):
            d = x.shape[-1]
            iu, ju = jnp.triu_indices(d)
            scale = jnp.where(iu == ju, 0.5, 1.0 / math.sqrt(2.0)).astype(x.dtype)
            quad = x[..., iu] * x[..., ju] * scale
            ones = jnp.ones(x.shape[:-1] + (1,), dtype=x.dtype)
            return jnp.concatenate([ones, x, quad], axis=-1)

        def linear_attention_causal(q_phi, k_phi, v):
            B, T, H, F = q_phi.shape
            D = v.shape[-1]
            Nc = T // CHUNK
            qc = q_phi.reshape(B, Nc, CHUNK, H, F).transpose(1, 0, 2, 3, 4)
            kc = k_phi.reshape(B, Nc, CHUNK, H, F).transpose(1, 0, 2, 3, 4)
            vc = v.reshape(B, Nc, CHUNK, H, D).transpose(1, 0, 2, 3, 4)
            causal = jnp.tril(jnp.ones((CHUNK, CHUNK), dtype=q_phi.dtype))

            def step(carry, inp):
                kv, ksum = carry
                qb, kb, vb = inp
                A = jnp.einsum('bchf,bshf->bhcs', qb, kb) * causal
                y = jnp.einsum('bhcs,bshd->bchd', A, vb) + jnp.einsum('bchf,bhfd->bchd', qb, kv)
                z = jnp.einsum('bhcs->bch', A) + jnp.einsum('bchf,bhf->bch', qb, ksum)
                kv = kv + jnp.einsum('bshf,bshd->bhfd', kb, vb)
                ksum = ksum + kb.sum(axis=1)
                return ((kv, ksum), y / (z[..., None] + EPS_LIN))
            kv0 = jnp.zeros((B, H, F, D), dtype=q_phi.dtype)
            ks0 = jnp.zeros((B, H, F), dtype=q_phi.dtype)
            _, ys = jax.lax.scan(step, (kv0, ks0), (qc, kc, vc))
            return ys.transpose(1, 0, 2, 3, 4).reshape(B, T, H, D)

        def sliding_window_attention(q, k, v):
            B, T, H, D = q.shape
            scale = 1.0 / math.sqrt(D)
            t = jnp.arange(T)
            allowed = (t[None, :] <= t[:, None]) & (t[None, :] >= t[:, None] - WINDOW)
            scores = jnp.einsum('bqhd,bkhd->bhqk', q, k) * scale
            scores = jnp.where(allowed[None, None], scores, -jnp.inf)
            attn = jax.nn.softmax(scores, axis=-1)
            out = jnp.einsum('bhqk,bkhd->bqhd', attn, v)
            return out.reshape(B, T, H * D)
        key = jax.random.key(seed)
        ks = jax.random.split(key, 7)
        B, T = (2, 256)
        s = 0.02
        return {'x': jax.random.normal(ks[0], (B, T, D_MODEL), jnp.float32), 'norm_w': jnp.ones((D_MODEL,), jnp.float32), 'Wq': jax.random.normal(ks[1], (D_MODEL, D_MODEL), jnp.float32) * s, 'Wk': jax.random.normal(ks[2], (D_MODEL, D_MODEL), jnp.float32) * s, 'Wv': jax.random.normal(ks[3], (D_MODEL, D_MODEL), jnp.float32) * s, 'Wqf': jax.random.normal(ks[4], (HEAD_DIM, FEAT), jnp.float32) * s, 'Wkf': jax.random.normal(ks[5], (HEAD_DIM, FEAT), jnp.float32) * s, 'Wout': jax.random.normal(ks[6], (2 * D_MODEL, D_MODEL), jnp.float32) * s}
    _L0_attn_a_in = _L0_attn_a_setup()

    def _L0_attn_b_setup():
        import jax, jax.numpy as jnp
        import numpy as np
        from jax import lax
        RWKV_K_CLAMP = 60.0
        RWKV_K_EPS = 1e-08
        key = jax.random.key(seed)
        ks = jax.random.split(key, 12)
        B, T, C = (4, 128, 128)
        s = 1.0 / np.sqrt(C)
        return {'xq': jax.random.normal(ks[0], (B, T, C), jnp.float32), 'xk': jax.random.normal(ks[1], (B, T, C), jnp.float32), 'xv': jax.random.normal(ks[2], (B, T, C), jnp.float32), 'time_decay': jax.random.normal(ks[3], (C, 1), jnp.float32) * 0.1, 'time_first': jnp.full((C, 1), np.log(0.3), jnp.float32), 'time_mix_k': jax.random.uniform(ks[4], (1, 1, C), jnp.float32), 'time_mix_v': jax.random.uniform(ks[5], (1, 1, C), jnp.float32), 'time_mix_r': jax.random.uniform(ks[6], (1, 1, C), jnp.float32), 'Wk': jax.random.normal(ks[7], (C, C), jnp.float32) * s, 'Wv': jax.random.normal(ks[8], (C, C), jnp.float32) * s, 'Wr': jax.random.normal(ks[9], (C, C), jnp.float32) * s, 'Wo': jax.random.normal(ks[10], (C, C), jnp.float32) * s}
    _L0_attn_b_in = _L0_attn_b_setup()

    def _L0_ffn_setup():
        import jax, jax.numpy as jnp
        import numpy as np
        B, S, DIM, FFN, E = (4, 256, 128, 512, 8)
        key = jax.random.key(seed)
        k0, k1, k2, k3 = jax.random.split(key, 4)
        scale = 0.02
        return {'hidden_states': jax.random.normal(k0, (B, S, DIM), jnp.float32), 'router_w': jax.random.normal(k1, (DIM, E), jnp.float32) * scale, 'router_b': jnp.zeros((E,), jnp.float32), 'w1': jax.random.normal(k2, (E, DIM, 2 * FFN), jnp.float32) * scale, 'w2': jax.random.normal(k3, (E, FFN, DIM), jnp.float32) * scale}
    _L0_ffn_in = _L0_ffn_setup()
    _d = {'L0_attn_a_x': _L0_attn_a_in['x'], 'L0_attn_a_norm_w': _L0_attn_a_in['norm_w'], 'L0_attn_a_Wq': _L0_attn_a_in['Wq'], 'L0_attn_a_Wk': _L0_attn_a_in['Wk'], 'L0_attn_a_Wv': _L0_attn_a_in['Wv'], 'L0_attn_a_Wqf': _L0_attn_a_in['Wqf'], 'L0_attn_a_Wkf': _L0_attn_a_in['Wkf'], 'L0_attn_a_Wout': _L0_attn_a_in['Wout'], 'L0_attn_b_xk': _L0_attn_b_in['xk'], 'L0_attn_b_xv': _L0_attn_b_in['xv'], 'L0_attn_b_time_decay': _L0_attn_b_in['time_decay'], 'L0_attn_b_time_first': _L0_attn_b_in['time_first'], 'L0_attn_b_time_mix_k': _L0_attn_b_in['time_mix_k'], 'L0_attn_b_time_mix_v': _L0_attn_b_in['time_mix_v'], 'L0_attn_b_time_mix_r': _L0_attn_b_in['time_mix_r'], 'L0_attn_b_Wk': _L0_attn_b_in['Wk'], 'L0_attn_b_Wv': _L0_attn_b_in['Wv'], 'L0_attn_b_Wr': _L0_attn_b_in['Wr'], 'L0_attn_b_Wo': _L0_attn_b_in['Wo'], 'L0_ffn_router_w': _L0_ffn_in['router_w'], 'L0_ffn_router_b': _L0_ffn_in['router_b'], 'L0_ffn_w1': _L0_ffn_in['w1'], 'L0_ffn_w2': _L0_ffn_in['w2']}
    _x0 = _d['L0_attn_a_x']
    _d['L0_attn_a_x'] = jax.random.normal(jax.random.fold_in(jax.random.key(seed), 1), (8, 512, 128), dtype=_x0.dtype)
    del _x0
    return _d

def reference(L0_attn_a_x, L0_attn_a_norm_w, L0_attn_a_Wq, L0_attn_a_Wk, L0_attn_a_Wv, L0_attn_a_Wqf, L0_attn_a_Wkf, L0_attn_a_Wout, L0_attn_b_xk, L0_attn_b_xv, L0_attn_b_time_decay, L0_attn_b_time_first, L0_attn_b_time_mix_k, L0_attn_b_time_mix_v, L0_attn_b_time_mix_r, L0_attn_b_Wk, L0_attn_b_Wv, L0_attn_b_Wr, L0_attn_b_Wo, L0_ffn_router_w, L0_ffn_router_b, L0_ffn_w1, L0_ffn_w2):

    def _L0_attn_a_ref(x, norm_w, Wq, Wk, Wv, Wqf, Wkf, Wout):
        import jax, jax.numpy as jnp
        import numpy as np
        import math
        D_MODEL = 128
        N_HEADS = 16
        HEAD_DIM = D_MODEL // N_HEADS
        FEAT = 16
        WINDOW = 64
        EPS_NORM = 1e-06
        EPS_LIN = 1e-06
        CHUNK = 128

        def rmsnorm(x, w):
            return x * jax.lax.rsqrt(jnp.mean(x * x, axis=-1, keepdims=True) + EPS_NORM) * w

        def taylor_feature_map(x):
            d = x.shape[-1]
            iu, ju = jnp.triu_indices(d)
            scale = jnp.where(iu == ju, 0.5, 1.0 / math.sqrt(2.0)).astype(x.dtype)
            quad = x[..., iu] * x[..., ju] * scale
            ones = jnp.ones(x.shape[:-1] + (1,), dtype=x.dtype)
            return jnp.concatenate([ones, x, quad], axis=-1)

        def linear_attention_causal(q_phi, k_phi, v):
            B, T, H, F = q_phi.shape
            D = v.shape[-1]
            Nc = T // CHUNK
            qc = q_phi.reshape(B, Nc, CHUNK, H, F).transpose(1, 0, 2, 3, 4)
            kc = k_phi.reshape(B, Nc, CHUNK, H, F).transpose(1, 0, 2, 3, 4)
            vc = v.reshape(B, Nc, CHUNK, H, D).transpose(1, 0, 2, 3, 4)
            causal = jnp.tril(jnp.ones((CHUNK, CHUNK), dtype=q_phi.dtype))

            def step(carry, inp):
                kv, ksum = carry
                qb, kb, vb = inp
                A = jnp.einsum('bchf,bshf->bhcs', qb, kb) * causal
                y = jnp.einsum('bhcs,bshd->bchd', A, vb) + jnp.einsum('bchf,bhfd->bchd', qb, kv)
                z = jnp.einsum('bhcs->bch', A) + jnp.einsum('bchf,bhf->bch', qb, ksum)
                kv = kv + jnp.einsum('bshf,bshd->bhfd', kb, vb)
                ksum = ksum + kb.sum(axis=1)
                return ((kv, ksum), y / (z[..., None] + EPS_LIN))
            kv0 = jnp.zeros((B, H, F, D), dtype=q_phi.dtype)
            ks0 = jnp.zeros((B, H, F), dtype=q_phi.dtype)
            _, ys = jax.lax.scan(step, (kv0, ks0), (qc, kc, vc))
            return ys.transpose(1, 0, 2, 3, 4).reshape(B, T, H, D)

        def sliding_window_attention(q, k, v):
            B, T, H, D = q.shape
            scale = 1.0 / math.sqrt(D)
            t = jnp.arange(T)
            allowed = (t[None, :] <= t[:, None]) & (t[None, :] >= t[:, None] - WINDOW)
            scores = jnp.einsum('bqhd,bkhd->bhqk', q, k) * scale
            scores = jnp.where(allowed[None, None], scores, -jnp.inf)
            attn = jax.nn.softmax(scores, axis=-1)
            out = jnp.einsum('bhqk,bkhd->bqhd', attn, v)
            return out.reshape(B, T, H * D)
        B, T, _ = x.shape
        h = rmsnorm(x, norm_w)
        q = (h @ Wq).reshape(B, T, N_HEADS, HEAD_DIM)
        k = (h @ Wk).reshape(B, T, N_HEADS, HEAD_DIM)
        v = (h @ Wv).reshape(B, T, N_HEADS, HEAD_DIM)
        q_phi = taylor_feature_map(q @ Wqf)
        k_phi = taylor_feature_map(k @ Wkf)
        lin = linear_attention_causal(q_phi, k_phi, v).reshape(B, T, D_MODEL)
        win = sliding_window_attention(q, k, v)
        out = jnp.concatenate([lin, win], axis=-1) @ Wout
        return x + out

    def _L0_attn_b_ref(xq, xk, xv, time_decay, time_first, time_mix_k, time_mix_v, time_mix_r, Wk, Wv, Wr, Wo):
        import jax, jax.numpy as jnp
        import numpy as np
        from jax import lax
        RWKV_K_CLAMP = 60.0
        RWKV_K_EPS = 1e-08
        B, T, C = xq.shape
        x = xq
        xx = jnp.pad(x, ((0, 0), (1, 0), (0, 0)))[:, :T]
        k = jnp.einsum('btc,dc->btd', x * time_mix_k + xx * (1 - time_mix_k), Wk)
        v = jnp.einsum('btc,dc->btd', x * time_mix_v + xx * (1 - time_mix_v), Wv)
        r = jnp.einsum('btc,dc->btd', x * time_mix_r + xx * (1 - time_mix_r), Wr)
        sr = jax.nn.sigmoid(r)
        kc = jnp.exp(jnp.minimum(k, RWKV_K_CLAMP)).transpose(0, 2, 1)
        vc = v.transpose(0, 2, 1)
        kv = kc * vc
        curve = jnp.arange(T - 1, dtype=jnp.float32) - (T - 2)
        time_w = jnp.concatenate([jnp.exp(time_decay) * curve[None, :], time_first], axis=-1)
        w = jnp.exp(time_w)[:, None, :]

        def dconv(a):
            ap = jnp.pad(a, ((0, 0), (0, 0), (T - 1, 0)))
            return lax.conv_general_dilated(ap, w, (1,), 'VALID', feature_group_count=C, dimension_numbers=('NCH', 'OIH', 'NCH'))
        wkv = dconv(kv)
        wk = dconv(kc) + RWKV_K_EPS
        out = sr * (wkv / wk).transpose(0, 2, 1)
        return jnp.einsum('btc,dc->btd', out, Wo)

    def _L0_ffn_ref(hidden_states, router_w, router_b, w1, w2):
        import jax, jax.numpy as jnp
        import numpy as np
        B, S, DIM, FFN, E = (4, 256, 128, 512, 8)
        b, s, d = hidden_states.shape
        x = hidden_states.reshape(-1, d)
        logits = x @ router_w + router_b
        route = jax.nn.softmax(logits, axis=1)
        max_prob = jnp.max(route, axis=1, keepdims=True)
        max_ind = jnp.argmax(route, axis=1)
        out = jnp.zeros_like(x)
        num_experts = w1.shape[0]
        for e in range(num_experts):
            h = x @ w1[e]
            a, g = jnp.split(h, 2, axis=1)
            y = jax.nn.silu(a) * g @ w2[e]
            out = jnp.where((max_ind == e)[:, None], y, out)
        out = out * max_prob
        return out.reshape(b, s, d)
    x = L0_attn_a_x
    x = x + _L0_attn_a_ref(_layernorm(x, axis=-1), L0_attn_a_norm_w, L0_attn_a_Wq, L0_attn_a_Wk, L0_attn_a_Wv, L0_attn_a_Wqf, L0_attn_a_Wkf, L0_attn_a_Wout)
    x = x + _L0_ffn_ref(_layernorm(x, axis=-1), L0_ffn_router_w, L0_ffn_router_b, L0_ffn_w1, L0_ffn_w2)
    x = x + _L0_attn_b_ref(_layernorm(x, axis=-1), L0_attn_b_xk, L0_attn_b_xv, L0_attn_b_time_decay, L0_attn_b_time_first, L0_attn_b_time_mix_k, L0_attn_b_time_mix_v, L0_attn_b_time_mix_r, L0_attn_b_Wk, L0_attn_b_Wv, L0_attn_b_Wr, L0_attn_b_Wo)
    x = x + _L0_ffn_ref(_layernorm(x, axis=-1), L0_ffn_router_w, L0_ffn_router_b, L0_ffn_w1, L0_ffn_w2)
    return x

_drawn_inputs = setup_inputs


def setup_inputs(seed=0):
    import zlib

    import numpy as np

    out = dict(_drawn_inputs(seed))
    spreads = {'L0_attn_a_norm_w': (1.0, 0.6),
     'L0_attn_b_time_first': (-1.2039728164672852, 0.6),
     'L0_ffn_router_b': (0.0, 0.8)}
    factors = {'L0_attn_a_Wq': 8.0,
     'L0_attn_a_Wk': 8.0,
     'L0_attn_a_Wv': 8.0,
     'L0_attn_a_Wqf': 8.0,
     'L0_attn_a_Wkf': 8.0,
     'L0_attn_a_Wout': 8.0,
     'L0_attn_b_time_decay': 7.039,
     'L0_ffn_router_w': 8.0,
     'L0_ffn_w1': 8.0,
     'L0_ffn_w2': 8.0}
    for name, (base, spread) in spreads.items():
        noise = np.random.default_rng([zlib.crc32(name.encode()), seed]).standard_normal(out[name].shape)
        drawn = base * np.exp(spread * noise) if base else spread * noise
        out[name] = jnp.asarray(drawn.astype(out[name].dtype))
    for name, factor in factors.items():
        out[name] = (out[name] * factor).astype(out[name].dtype)
    return out
```

```python
import concourse.bass as bass
from concourse import mybir
from contextlib import ExitStack

F32 = mybir.dt.float32
BF16 = mybir.dt.bfloat16
I32 = mybir.dt.int32
U32 = mybir.dt.uint32
ALU = mybir.AluOpType
ACT = mybir.ActivationFunctionType
AX = mybir.AxisListType

P = 128
B = 8
T = 512
TPB = T // P
NT = B * TPB
H = 16
HD = P // H
FEAT = 16
WIN = 64
NW = T // WIN
NP = H // 2
PARTS = 3
ROWS = 6 * HD
BIAS = 2 * ROWS
SROWS = BIAS + 2 * PARTS
NEG = -1.0e30
E = 8
FFN = 512
KF = FFN // P
SLOTS = NT + E - 1
EPS_LN = 1e-5
EPS_RMS = 1e-6
EPS_LIN = 1e-6
EPS_RWKV = 1e-8
K_CLAMP = 60.0
PRODUCTS = [(0, 0), (0, 1), (0, 2), (1, 0), (1, 1), (2, 0)]


class Chain:

    def __init__(self, engine, sem):
        self.engine, self.sem, self.base, self.n = engine, sem, 0, 0

    def at(self, base):
        self.base, self.n = base, 0

    def link(self, ins):
        self.n += 1
        ins.then_inc(self.sem, 1)
        self.engine.wait_ge(self.sem, self.base + self.n)


def layernorm_stats(nc, ch, x, stats, mv):
    for t in range(NT - 1):
        nc.vector.bn_stats(stats[:, t, :], x[:, t, :])
    ch.link(nc.vector.bn_stats(stats[:, NT - 1, :], x[:, NT - 1, :]))
    for t in range(NT):
        last = nc.vector.bn_aggr(mv[:, t, :], stats[:, t, :])
    return last


def build(nc, x_in, norm_w, Wq, Wk, Wv, Wqf, Wkf, Wout, xk_in, xv_in, time_decay, time_first,
          mix_k, mix_v, mix_r, Wk_b, Wv_b, Wr_b, Wo_b, router_w, router_b, w1, w2, out):
    x_tiles = x_in.rearrange("b (t p) d -> p (b t) d", p=P)
    out_tiles = out.rearrange("b (t p) d -> p (b t) d", p=P)
    parts_dram = nc.dram_tensor("parts_dram", (3, B, PARTS, P, T), BF16).ap()
    v_dram = nc.dram_tensor("v_dram", (B, P, NW, P), F32).ap()
    negmax_dram = nc.dram_tensor("negmax_dram", (B, 2, PARTS, NP * NW, WIN), BF16).ap()
    xs_dram = nc.dram_tensor("xs_dram", (SLOTS * P, P), F32).ap()
    ys_dram = nc.dram_tensor("ys_dram", (SLOTS * P, P), F32).ap()
    with ExitStack() as ctx:
        def sb(name, shape, dt=F32):
            return ctx.enter_context(nc.sbuf_tensor(name, shape, dt))

        X = sb("X", [P, NT, P])
        ident = sb("ident", [P, P])
        identb = sb("identb", [P, P], BF16)
        mv = sb("mv", [P, NT, 2])
        rstd = sb("rstd", [P, NT])
        stats = sb("stats", [P, NT, 6])
        half = sb("half", [P, NT])
        slot_idx = sb("slot_idx", [P, NT], U32)
        expert = sb("expert", [1, SLOTS], I32)
        pmax = sb("pmax", [P, NT])
        build_prep(nc, x_tiles, norm_w, Wq, Wk, Wv, Wqf, Wkf, X, ident, identb, mv, rstd, stats, half,
                   parts_dram, v_dram)
        with nc.sbuf_tensor("Y", [P, B, 2, T], F32) as Y:
            build_attention(nc, ident, identb, Y, parts_dram, v_dram, negmax_dram)
            build_outproj(nc, X, Y, Wout, xs_dram)
        w1s = sb("w1s", [P, E, 2 * FFN])
        w2s = sb("w2s", [P, E, KF, P])
        xn = sb("xn", [P, NT, P])
        first = (w1, w2, w1s, w2s)
        for name in ("ffn1", "ffn2"):
            build_route(nc, name, X, xn, ident, mv, rstd, stats, half, router_w, router_b, slot_idx, expert, pmax,
                        xs_dram, first)
            build_experts(nc, name, ident, w1s, w2s, expert, xs_dram, ys_dram)
            if name == "ffn1":
                build_combine(nc, name, X, xn, slot_idx, pmax, ys_dram, None)
                build_rwkv(nc, X, xn, ident, mv, rstd, stats, half, time_decay, time_first, mix_k, mix_v, mix_r,
                           Wk_b, Wv_b, Wr_b, Wo_b)
            else:
                build_combine(nc, name, X, xn, slot_idx, pmax, ys_dram, out_tiles)
            first = None


def build_attention(nc, ident, identb, Y, parts_dram, v_dram, negmax_dram):
    LIN = [[(0, 0)], [(1, 0)], [(2, 0), (3, 2 * P)]]
    NL = 4 * len(LIN)
    NU = NL + 4
    LOADS = 6 * len(PRODUCTS) + 1
    with ExitStack() as ctx:
        def sb(name, shape, dt=F32):
            return ctx.enter_context(nc.sbuf_tensor(name, shape, dt))

        def sem(name):
            return ctx.enter_context(nc.semaphore(name))

        def both(name):
            return [sem(name + "_even"), sem(name + "_odd")]

        sc = ctx.enter_context(nc.psum_tensor("scores", [P, 2, 1024], F32))
        acc = ctx.enter_context(nc.psum_tensor("acc", [P, 2, 2, T], F32))
        qs = [sb(f"qs{u}", [SROWS, 2, NP, T], BF16) for u in range(2)]
        ks = [sb(f"ks{u}", [SROWS, NP, WIN + T], BF16) for u in range(2)]
        k2s = [sb(f"k2s{u}", [BIAS, NP, T], BF16) for u in range(2)]
        v = [sb(f"v{u}", [P, NW, P]) for u in range(2)]
        vpad = [sb(f"vpad{u}", [P, NW, 4, 4, 32]) for u in range(2)]
        ones = sb("ones", [P, 4, 32])
        prob = sb("prob", [P, 2, 2, 1024])
        maskq = sb("maskq", [P, NW, P], BF16)
        maskk = sb("maskk", [P, NW * 2, WIN], BF16)
        mx = sb("mx", [P, 2, NP, NW])
        nm = sb("nm", [NP * NW, 2, PARTS, P], BF16)
        nr = sb("nr", [NP * NW, P])
        den = sb("den", [P, T])
        rden = sb("rden", [P, T])
        loaded, nm_stored, nm_loaded = both("loaded"), both("negmax_stored"), both("negmax_loaded")
        vpad_s = both("vpad_ready")
        zero_s, const_s, pch, vch = sem("zeroed"), sem("consts"), sem("pool_steps"), sem("dve_steps")
        masked_s = sem("lin_masked")
        sp_go, pool_go, pe_go = sem("sp_goes"), sem("pool_goes"), sem("pe_goes")
        mjob, tjob, ujob = sem("max_scores"), sem("max_transposed"), sem("scores_ready")
        maxed, split_s, exped, pv_s = sem("max_done"), sem("negmax_ready"), sem("weights_ready"), sem("unit_summed")
        norm_s = (sem("lin_normalised"), sem("win_normalised"))
        block = ctx.enter_context(nc.Block())

        @block.sync
        def _(sp):
            sp.wait_ge(zero_s, 1)
            with sp.Fori(0, B // 2) as i:
                for u in range(2):
                    b = i * 2 + u
                    sp.wait_ge(pv_s, b * NU)
                    sp.sem_inc(sp_go, 1)
                    sp.wait_ge(vpad_s[u], i * 4)
                    sp.sem_inc(sp_go, 1)
                    for hh in range(2):
                        for c, (kp, qp) in enumerate(PRODUCTS):
                            lo = hh * ROWS + c * HD
                            for dst, which, part in ((qs[u][lo:lo + HD, hh, :, :], 0, qp),
                                                     (ks[u][lo:lo + HD, :, WIN:], 1, kp),
                                                     (k2s[u][lo:lo + HD, :, :], 2, kp)):
                                sp.dma_start(dst, parts_dram[which, bass.ds(b, 1), part, 64 * hh:64 * hh + 64, :]
                                             .rearrange("b (h d) t -> (b d) h t", d=HD)).then_inc(loaded[u], 16)
                    sp.dma_start(v[u][:], v_dram[bass.ds(b, 1)].rearrange("b p w n -> p (b w) n")).then_inc(loaded[u], 16)

        @block.gpsimd
        def _(pool):
            ch = Chain(pool, pch)
            for u in range(2):
                ch.link(nc.gpsimd.memset(qs[u][:], 0.0))
                ch.link(nc.gpsimd.memset(ks[u][0:BIAS, :, 0:WIN], 0.0))
                ch.link(nc.gpsimd.memset(ks[u][BIAS:SROWS, :, :], 1.0))
            pool.sem_inc(zero_s, 1)
            for u in range(2):
                ch.link(nc.gpsimd.memset(vpad[u][:], 0.0))
            ch.link(nc.gpsimd.memset(ones[:], 0.0))
            for j in range(4):
                nc.gpsimd.memset(ones[:, j, HD * j:HD * j + HD], 1.0).then_inc(const_s, 1)
            ch.link(nc.gpsimd.memset(maskq[:], 0.0))
            ch.link(nc.gpsimd.memset(maskk[:], 0.0))
            for lo in (0, WIN):
                m = maskq[lo:lo + WIN, :, :]
                ch.link(nc.gpsimd.affine_select(out=m, in_=m, compare_op=ALU.is_ge, fill=NEG, base=0,
                                                pattern=[[0, NW], [1, P]], channel_multiplier=-1))
                ch.link(nc.gpsimd.affine_select(out=m, in_=m, compare_op=ALU.is_ge, fill=NEG, base=WIN,
                                                pattern=[[0, NW], [-1, P]], channel_multiplier=1))
            ch.link(nc.gpsimd.affine_select(out=maskk[:], in_=maskk[:], compare_op=ALU.is_ge, fill=NEG, base=0,
                                            pattern=[[0, NW * 2], [-1, WIN]], channel_multiplier=1))
            ch.link(nc.gpsimd.affine_select(out=maskk[:], in_=maskk[:], compare_op=ALU.is_ge, fill=NEG, base=WIN,
                                            pattern=[[0, NW * 2], [1, WIN]], channel_multiplier=-1))
            ch.link(nc.gpsimd.memset(maskq[:, 0, 0:WIN], NEG))
            nc.gpsimd.memset(maskk[0:WIN, 0:2, :], NEG).then_inc(const_s, 1)
            with pool.Fori(0, B // 2) as i:
                for u in range(2):
                    pool.wait_ge(loaded[u], i * (16 * LOADS) + 16 * LOADS)
                    pool.wait_ge(pv_s, i * (2 * NU) + u * NU)
                    pool.sem_inc(pool_go, 1)
                    for j in range(4):
                        nc.gpsimd.tensor_copy(vpad[u][:, :, :, j, HD * j:HD * j + HD].rearrange("p w g d -> p (w g) d"),
                                              v[u][:].rearrange("p w (g j d) -> p (w g) j d", g=4, j=4)[:, :, j, :])\
                            .then_inc(vpad_s[u], 1)
                    for n in range(NL):
                        for a in range(2):
                            pool.wait_ge(exped, i * (4 * NU) + 2 * u * NU + 2 * n + a + 1)
                            pool.sem_inc(pool_go, 1)
                            for kc, col in LIN[n % len(LIN)]:
                                m = prob[:, n % 2, a, :].rearrange("p (h n) -> p h n", h=2)[:, :, col:col + P]
                                k = nc.gpsimd.affine_select(out=m, in_=m, compare_op=ALU.is_ge, fill=0.0, base=0,
                                                            pattern=[[0, 2], [1, P]], channel_multiplier=-1)
                            k.then_inc(masked_s, 1)

        @block.scalar
        def _(act):
            with act.Fori(0, B // 2) as i:
                for u in range(2):
                    b = i * 2 + u
                    for n in range(NU):
                        for a in range(2):
                            act.wait_ge(ujob, i * (4 * NU) + 2 * u * NU + 2 * n + a + 1)
                            act.wait_ge(pv_s, i * (2 * NU) + (u + 1) * NU + n - 1)
                            if n < NL:
                                w = max(col + (TPB - kc) * P for kc, col in LIN[n % len(LIN)])
                                nc.scalar.activation(prob[:, n % 2, a, :].rearrange("p (h n) -> p h n", h=2)[:, :, 0:w],
                                                     sc[:, a, :].rearrange("p (h n) -> p h n", h=2)[:, :, 0:w],
                                                     ACT.Square, bias=1.0).then_inc(exped, 1)
                            else:
                                nc.scalar.activation(prob[:, n % 2, a, :], sc[:, a, :], ACT.Exp,
                                                     scale=float(HD) ** -0.5).then_inc(exped, 1)
                        if n == 0:
                            act.wait_ge(split_s, i * 2 + u + 1)
                            for hh in range(2):
                                act.dma_start(negmax_dram[bass.ds(b, 1), hh].rearrange("b c k q -> k (b c) q"),
                                              nm[:, u, :, WIN * hh:WIN * hh + WIN]).then_inc(nm_stored[u], 16)
                        if n == 4:
                            act.wait_ge(nm_stored[u], i * 32 + 32)
                            for hh in range(2):
                                lo = BIAS + PARTS * hh
                                act.dma_start(qs[u][lo:lo + PARTS, hh, :, :].rearrange("c p t -> c (p t)"),
                                              negmax_dram[bass.ds(b, 1), hh].rearrange("b c k q -> (b c) (k q)"))\
                                    .then_inc(nm_loaded[u], 16)

        @block.vector
        def _(dve):
            ch = Chain(dve, vch)
            with dve.Fori(0, B // 2) as i:
                ch.at(i * 14)
                for u in range(2):
                    b = i * 2 + u
                    for m in range(NP):
                        dve.wait_ge(mjob, i * (2 * NP) + u * NP + m + 1)
                        nc.vector.tensor_reduce(mx[:, u, m, :], sc[:, m % 2, :].rearrange("p (w k) -> p w k", w=NW),
                                                AX.X, ALU.max, negate=True).then_inc(maxed, 1)
                    dve.wait_ge(tjob, b + 1)
                    dve.wait_ge(nm_stored[u], i * 32)
                    tr = sc[0:NP * NW, 1, 0:P]
                    ch.link(nc.vector.tensor_copy(nm[:, u, 0, :], tr))
                    ch.link(nc.vector.tensor_tensor(nr[:], tr, nm[:, u, 0, :], ALU.subtract))
                    ch.link(nc.vector.tensor_copy(nm[:, u, 1, :], nr[:]))
                    nc.vector.tensor_tensor(nm[:, u, 2, :], nr[:], nm[:, u, 1, :], ALU.subtract).then_inc(split_s, 1)
                    for k in range(2):
                        dve.wait_ge(pv_s, i * (2 * NU) + (u + 1) * NU + (NL, NU)[k])
                        ch.link(nc.vector.tensor_scalar(den[:], acc[:, k, 1, :], EPS_LIN if k == 0 else 0.0, None, ALU.add))
                        ch.link(nc.vector.reciprocal(rden[:], den[:]))
                        nc.vector.tensor_tensor(Y[:, bass.ds(b, 1), k, :].rearrange("p a t -> p (a t)"),
                                                acc[:, k, 0, :], rden[:], ALU.mult).then_inc(norm_s[k], 1)

        @block.tensor
        def _(pe):
            pe.wait_ge(const_s, 5)
            pe.sem_inc(pv_s, NU)

            def lin_scores(u, j, slot, a):
                p = j + 4 * a
                for kc, col in LIN[slot]:
                    for hh in range(2):
                        at = T * hh + col
                        mm = nc.tensor.matmul(sc[:, a, at:at + T - P * kc], k2s[u][:, p, P * kc:P * kc + P],
                                              qs[u][0:BIAS, hh, p, P * kc:], start=True, stop=True)
                return mm

            def win_scores(u, j, a):
                p = j + 4 * a
                for f in range(2):
                    nc.tensor.matmul(sc[:, a, T * f:T * f + T], identb[:], maskk[:, NW * f:NW * f + NW, :],
                                     start=True, stop=False,
                                             skip_group_check=True)
                    for w in range(4 * f, 4 * f + 4):
                        mm = nc.tensor.matmul(sc[:, a, P * w:P * w + P], ks[u][:, p, WIN * w:WIN * w + P],
                                              qs[u][:, :, p, WIN * w:WIN * w + WIN], start=False,
                                              stop=True, skip_group_check=True)
                return mm

            def sums(u, n):
                if n < NL:
                    j, todo = n // len(LIN), [(2 * kc + 1, P * kc, T - P * kc, [T * hh + col for hh in range(2)])
                                              for kc, col in LIN[n % len(LIN)]]
                    k, opens = 0, n == 0
                else:
                    j, todo = n - NL, [(w, WIN * w, WIN, [P * w + WIN * hh for hh in range(2)]) for w in range(NW)]
                    k, opens = 1, n == NL
                for x, (w, col, width, at) in enumerate(todo):
                    for which in range(2):
                        for a in range(2):
                            for hh in range(2):
                                g = a + 2 * hh
                                lhsT = ones[:, j, :] if which else vpad[u][:, w, g, j, :]
                                mm = nc.tensor.matmul(acc[32 * g:32 * g + 32, k, which, col:col + width], lhsT,
                                                      prob[:, n % 2, a, at[hh]:at[hh] + width],
                                                      start=opens and x == 0, stop=True,
                                                      skip_group_check=True)
                return mm

            with pe.Fori(0, B // 2) as i:
                for u in range(2):
                    b = i * 2 + u
                    pe.wait_ge(loaded[u], i * (16 * LOADS) + 16 * LOADS)
                    pe.wait_ge(exped, i * (4 * NU) + 2 * u * NU)
                    for m in range(NP):
                        if m >= 2:
                            pe.wait_ge(maxed, i * (2 * NP) + u * NP + m - 1)
                        for f in range(2):
                            nc.tensor.matmul(sc[:, m % 2, T * f:T * f + T], identb[:], maskq[:, 4 * f:4 * f + 4, :],
                                             start=True, stop=False,
                                             skip_group_check=True)
                            for w in range(4 * f, 4 * f + 4):
                                for hh in range(2):
                                    mm = nc.tensor.matmul(sc[WIN * hh:WIN * hh + WIN, m % 2, P * w:P * w + P],
                                                          qs[u][0:BIAS, hh, m, WIN * w:WIN * w + WIN],
                                                          ks[u][0:BIAS, m, WIN * w:WIN * w + P],
                                                          start=False, stop=True, skip_group_check=True)
                        mm.then_inc(mjob, 1)
                    pe.wait_ge(maxed, i * (2 * NP) + u * NP + NP)
                    pe.sem_inc(pe_go, 1)
                    nc.tensor.transpose(sc[0:NP * NW, 1, 0:P], mx[:, u, :, :].rearrange("p m w -> p (m w)"), ident[:])\
                        .then_inc(tjob, 1)
                    for n in range(NU + 1):
                        if n < NU:
                            for a in range(2):
                                if n == 0 and a == 1:
                                    pe.wait_ge(split_s, b + 1)
                                if n >= 1:
                                    pe.wait_ge(exped, i * (4 * NU) + 2 * u * NU + 2 * n + a - 1)
                                if n == NL and a == 0:
                                    pe.wait_ge(nm_loaded[u], i * 32 + 32)
                                if n < NL:
                                    lin_scores(u, n // len(LIN), n % len(LIN), a).then_inc(ujob, 1)
                                else:
                                    win_scores(u, n - NL, a).then_inc(ujob, 1)
                        if n >= 1:
                            m = n - 1
                            if m == 0:
                                pe.wait_ge(vpad_s[u], i * 4 + 4)
                                pe.wait_ge(norm_s[0], b)
                            if m == NL:
                                pe.wait_ge(norm_s[1], b)
                            if m < NL:
                                pe.wait_ge(masked_s, i * (4 * NL) + 2 * u * NL + 2 * m + 2)
                            else:
                                pe.wait_ge(exped, i * (4 * NU) + 2 * u * NU + 2 * m + 2)
                            mm = sums(u, m)
                            mm.then_inc(pv_s, 1)


def build_outproj(nc, X, Y, Wout, xs_dram):
    with ExitStack() as ctx:
        wo = ctx.enter_context(nc.sbuf_tensor("wo", [P, 2, P], F32))
        zero = ctx.enter_context(nc.sbuf_tensor("zero", [P, P], F32))
        ps = ctx.enter_context(nc.psum_tensor("out_ps", [P, 2, T], F32))
        w_in, zero_s, cleared, out_s, add_s = (ctx.enter_context(nc.semaphore(n)) for n in (
            "wout_loaded", "zero_tile", "slots_cleared", "out_psum", "out_added"))
        block = ctx.enter_context(nc.Block())

        @block.sync
        def _(sp):
            sp.dma_start(wo[:], Wout.rearrange("(k p) n -> p k n", k=2)).then_inc(w_in, 16)
            sp.wait_ge(zero_s, 1)
            sp.dma_start(xs_dram.rearrange("(s p) d -> p s d", p=P),
                         zero[:].unsqueeze(1).broadcast_to([P, SLOTS, P])).then_inc(cleared, 16)
            sp.wait_ge(cleared, 16)

        @block.tensor
        def _(pe):
            pe.wait_ge(w_in, 16)
            for b in range(B):
                if b >= 2:
                    pe.wait_ge(add_s, b - 1)
                for t in range(TPB):
                    for k in range(2):
                        mm = nc.tensor.matmul(ps[:, b % 2, P * t:P * t + P], Y[:, b, k, P * t:P * t + P], wo[:, k, :],
                                              start=k == 0, stop=k == 1)
                mm.then_inc(out_s, 1)

        @block.vector
        def _(dve):
            nc.vector.memset(zero[:], 0.0).then_inc(zero_s, 1)
            for b in range(B):
                dve.wait_ge(out_s, b + 1)
                x = X[:, TPB * b:TPB * b + TPB, :].rearrange("p t d -> p (t d)")
                nc.vector.tensor_tensor(x, ps[:, b % 2, :], x, ALU.add).then_inc(add_s, 1)


def norm_scale(nc, pool, ch, mv, rstd, half):
    ch.link(nc.gpsimd.tensor_scalar(rstd[:], mv[:, :, 1], EPS_LN, None, ALU.add))
    return nc.gpsimd.tensor_tensor(rstd[:], rstd[:], half[:], ALU.pow)


def build_route(nc, name, X, xn, ident, mv, rstd, stats, half, router_w, router_b, slot_idx, expert, pmax,
                xs_dram, weights):
    with ExitStack() as ctx:
        def sb(n, shape, dt=F32):
            return ctx.enter_context(nc.sbuf_tensor(f"{name}_{n}", shape, dt))

        def sem(n):
            return ctx.enter_context(nc.semaphore(f"{name}_{n}"))

        trp = ctx.enter_context(nc.psum_tensor(f"{name}_trp", [P, 2, T], F32))
        logit_ps = ctx.enter_context(nc.psum_tensor(f"{name}_logit_ps", [P, NT, E], F32))
        cnt_ps = ctx.enter_context(nc.psum_tensor(f"{name}_cnt_ps", [P, 2, 512], F32))
        xT = sb("xT", [P, 2, T])
        rw, rb = sb("rw", [P, E]), sb("rb", [P, E])
        logit, ex, eq, cand = (sb(n, [P, NT, E]) for n in ("logit", "ex", "eq", "cand"))
        best, total = sb("best", [P, NT]), sb("total", [P, NT])
        weight = sb("weight", [P, E])
        hot = sb("hot", [P, E, NT])
        hotb = sb("hotb", [P, E, NT], BF16)
        before, oneb = sb("before", [P, P], BF16), sb("oneb", [P, P], BF16)
        ones = sb("ones", [P, E * NT])
        tot, cum, place = (sb(n, [P, E, NT]) for n in ("tot", "cum", "place"))
        count, tiles, end, off = (sb(n, [P, E]) for n in ("count", "tiles", "end", "off"))
        steps = sb("steps", [P, NT])
        slotno = sb("slotno", [1, SLOTS])
        ended, past = sb("ended", [1, SLOTS, E]), sb("past", [1, SLOTS])
        slotf = sb("slotf", [P, NT])
        r_in, w_in, stat_s, scale_s, xn_s, tr_s, xT_s, logit_s = (sem(n) for n in (
            "router_loaded", "weights_loaded", "stats_done", "scales_done", "xn_ready", "xn_transposed", "xT_ready",
            "logits_ready"))
        const_s, pch, vch, shift_s, exp_s, hot_s, cnt_s, slot_s, sorted_s = (sem(n) for n in (
            "consts", "pool_steps", "dve_steps", "logits_shifted", "exp_done", "hot_ready", "counts_ready",
            "slots_ready", "sorted"))
        block = ctx.enter_context(nc.Block())

        @block.sync
        def _(sp):
            sp.dma_start(rw[:], router_w).then_inc(r_in, 16)
            sp.dma_start(rb[:], router_b.partition_broadcast(P)).then_inc(r_in, 16)
            if weights:
                w1, w2, w1s, w2s = weights
                for e in range(E):
                    sp.dma_start(w1s[:, e, :], w1[e]).then_inc(w_in, 16)
                    sp.dma_start(w2s[:, e, :, :], w2[e].rearrange("(k p) n -> p k n", p=P)).then_inc(w_in, 16)
                sp.wait_ge(w_in, 32 * E)

        @block.gpsimd
        def _(pool):
            ch = Chain(pool, pch)
            ch.link(nc.gpsimd.memset(before[:], 1.0))
            nc.gpsimd.affine_select(out=before[:], in_=before[:], compare_op=ALU.is_gt, fill=0.0, base=0,
                                    pattern=[[1, P]], channel_multiplier=-1).then_inc(const_s, 1)
            nc.gpsimd.memset(oneb[:], 1.0).then_inc(const_s, 1)
            nc.gpsimd.memset(ones[:], 1.0).then_inc(const_s, 1)
            nc.gpsimd.iota(weight[:], [[-1, E]], base=E, channel_multiplier=0,
                           allow_small_or_imprecise_dtypes=True).then_inc(const_s, 1)
            nc.gpsimd.iota(steps[:], [[P, NT]], base=0, channel_multiplier=0,
                           allow_small_or_imprecise_dtypes=True).then_inc(const_s, 1)
            ch.link(nc.gpsimd.iota(slotno[:], [[1, SLOTS]], base=0, channel_multiplier=0,
                                   allow_small_or_imprecise_dtypes=True))
            pool.wait_ge(stat_s, 1)
            norm_scale(nc, pool, ch, mv, rstd, half).then_inc(scale_s, 1)
            pool.wait_ge(slot_s, 1)
            for t in range(NT):
                nc.gpsimd.indirect_dma_start(out=xs_dram, out_offset=bass.IndirectOffsetOnAxis(ap=slot_idx[:, t:t + 1], axis=0),
                                             in_=xn[:, t, :], in_offset=None).then_inc(sorted_s, 16)
            pool.wait_ge(sorted_s, 16 * NT)

        @block.scalar
        def _(act):
            for b in range(B):
                act.wait_ge(tr_s, b + 1)
                if b >= 2:
                    act.wait_ge(logit_s, b - 1)
                nc.scalar.activation(xT[:, b % 2, :], trp[:, b % 2, :], ACT.Copy).then_inc(xT_s, 1)
            act.wait_ge(shift_s, 1)
            nc.scalar.activation(ex[:], ex[:], ACT.Exp).then_inc(exp_s, 1)

        @block.tensor
        def _(pe):
            pe.wait_ge(r_in, 32)
            for b in range(B + 1):
                if b < B:
                    pe.wait_ge(xn_s, b + 1)
                    if b >= 2:
                        pe.wait_ge(xT_s, b - 1)
                    for t in range(TPB):
                        tr = nc.tensor.transpose(trp[:, b % 2, P * t:P * t + P], xn[:, TPB * b + t, :], ident[:])
                    tr.then_inc(tr_s, 1)
                if b:
                    pe.wait_ge(xT_s, b)
                    for t in range(TPB):
                        mm = nc.tensor.matmul(logit_ps[:, TPB * (b - 1) + t, :], xT[:, (b - 1) % 2, P * t:P * t + P],
                                              rw[:], start=True, stop=True)
                    mm.then_inc(logit_s, 1)
            pe.wait_ge(hot_s, 1)
            pe.wait_ge(const_s, 2)
            h = hotb[:].rearrange("p e t -> p (e t)")
            nc.tensor.matmul(cnt_ps[:, 0, 0:E * NT], before[:], h, start=True, stop=True).then_inc(cnt_s, 1)
            nc.tensor.matmul(cnt_ps[:, 1, 0:E * NT], oneb[:], h, start=True, stop=True).then_inc(cnt_s, 1)

        @block.vector
        def _(dve):
            V = nc.vector
            ch = Chain(dve, vch)
            layernorm_stats(nc, ch, X, stats, mv).then_inc(stat_s, 1)
            dve.wait_ge(scale_s, 1)
            for b in range(B):
                for t in range(TPB * b, TPB * b + TPB):
                    k = V.tensor_scalar(xn[:, t, :], X[:, t, :], mv[:, t, 0:1], rstd[:, t:t + 1], ALU.subtract, ALU.mult)
                k.then_inc(xn_s, 1)
            dve.wait_ge(logit_s, B)
            dve.wait_ge(r_in, 32)
            dve.wait_ge(const_s, 5)
            wide = [P, NT, E]
            ch.link(V.tensor_tensor(logit[:], logit_ps[:], rb[:].unsqueeze(1).broadcast_to(wide), ALU.add))
            ch.link(V.tensor_reduce(best[:], logit[:], AX.X, ALU.max))
            top = best[:].unsqueeze(2).broadcast_to(wide)
            V.tensor_tensor(ex[:], logit[:], top, ALU.subtract).then_inc(shift_s, 1)
            ch.link(V.tensor_tensor(eq[:], logit[:], top, ALU.is_equal))
            ch.link(V.tensor_tensor(cand[:], eq[:], weight[:].unsqueeze(1).broadcast_to(wide), ALU.mult))
            ch.link(V.tensor_reduce(total[:], cand[:], AX.X, ALU.max))
            ch.link(V.tensor_tensor(hot[:].rearrange("p e t -> p t e"), cand[:], total[:].unsqueeze(2).broadcast_to(wide),
                                    ALU.is_equal))
            V.tensor_copy(hotb[:], hot[:]).then_inc(hot_s, 1)
            dve.wait_ge(exp_s, 1)
            ch.link(V.tensor_reduce(total[:], ex[:], AX.X, ALU.add))
            ch.link(V.reciprocal(pmax[:], total[:]))
            dve.wait_ge(cnt_s, 2)
            ch.link(V.tensor_copy(tot[:].rearrange("p e t -> p (e t)"), cnt_ps[:, 1, 0:E * NT]))
            ch.link(V.tensor_tensor_scan(cum[:].rearrange("p e t -> p (e t)"), ones[:],
                                         tot[:].rearrange("p e t -> p (e t)"), 0.0, ALU.mult, ALU.add))
            ch.link(V.tensor_reduce(count[:], tot[:], AX.X, ALU.add))
            ch.link(V.tensor_tensor(place[:], count[:].unsqueeze(2).broadcast_to([P, E, NT]),
                                    steps[:].unsqueeze(1).broadcast_to([P, E, NT]), ALU.is_gt))
            ch.link(V.tensor_reduce(tiles[:], place[:], AX.X, ALU.add))
            ch.link(V.tensor_tensor_scan(end[:], ones[:, 0:E], tiles[:], 0.0, ALU.mult, ALU.add))
            ch.link(V.tensor_tensor(off[:], end[:], tiles[:], ALU.subtract))
            ch.link(V.tensor_scalar(off[:], off[:], float(P), None, ALU.mult))
            ch.link(V.tensor_tensor(off[:], off[:], cum[:, :, NT - 1], ALU.subtract))
            ch.link(V.tensor_tensor(off[:], off[:], count[:], ALU.add))
            ch.link(V.tensor_tensor(place[:], cum[:], tot[:], ALU.subtract))
            ch.link(V.tensor_tensor(place[:], place[:], off[:].unsqueeze(2).broadcast_to([P, E, NT]), ALU.add))
            ch.link(V.tensor_tensor(place[:].rearrange("p e t -> p (e t)"), cnt_ps[:, 0, 0:E * NT],
                                    place[:].rearrange("p e t -> p (e t)"), ALU.add))
            ch.link(V.tensor_tensor(place[:], place[:], hot[:], ALU.mult))
            ch.link(V.tensor_reduce(slotf[:], place[:].rearrange("p e t -> p t e"), AX.X, ALU.add))
            V.tensor_copy(slot_idx[:], slotf[:]).then_inc(slot_s, 1)
            dve.wait_ge(pch, 2)
            ch.link(V.tensor_tensor(ended[:], slotno[:].unsqueeze(2).broadcast_to([1, SLOTS, E]),
                                    end[0:1, :].unsqueeze(1).broadcast_to([1, SLOTS, E]), ALU.is_ge))
            ch.link(V.tensor_reduce(past[:], ended[:], AX.X, ALU.add))
            ch.link(V.tensor_scalar(past[:], past[:], float(E - 1), None, ALU.min))
            ch.link(V.tensor_copy(expert[:], past[:]))


def build_experts(nc, name, ident, w1s, w2s, expert, xs_dram, ys_dram):
    R = 3
    with ExitStack() as ctx:
        def sb(n, shape, dt=F32):
            return ctx.enter_context(nc.sbuf_tensor(f"{name}_{n}", shape, dt))

        def sem(n):
            return ctx.enter_context(nc.semaphore(f"{name}_{n}"))

        up = ctx.enter_context(nc.psum_tensor(f"{name}_up", [P, R, 2, FFN], F32))
        hid_ps = ctx.enter_context(nc.psum_tensor(f"{name}_hid_ps", [P, KF, P], F32))
        xT_ps = ctx.enter_context(nc.psum_tensor(f"{name}_xT_ps", [P, P], F32))
        xt, xT = sb("xt", [P, R, P]), sb("xTs", [P, R, P])
        sa, hg, hgT, yo = sb("sa", [P, R, FFN]), sb("hg", [P, R, FFN]), sb("hgT", [P, R, KF, P]), sb("yo", [P, R, P])
        loaded = [sem(f"tile_loaded{u}") for u in range(R)]
        stored = [sem(f"tile_stored{u}") for u in range(R)]
        tr_s, xT_s, a_s, g_s, silu_s, hg_s, hgtr_s, hgT_s, y_s, yo_s, pe_go = (sem(n) for n in (
            "x_transposed", "xT_ready", "a_psum", "g_psum", "silu_done", "hidden_ready", "hidden_transposed",
            "hiddenT_ready", "y_psum", "y_ready", "pe_goes"))
        block = ctx.enter_context(nc.Block())
        xs_v = xs_dram.rearrange("(s p) d -> s p d", p=P)
        ys_v = ys_dram.rearrange("(s p) d -> s p d", p=P)

        @block.sync
        def _(sp):
            with sp.Fori(0, SLOTS // R) as i:
                for u in range(R):
                    s = i * R + u
                    sp.wait_ge(tr_s, i * R)
                    sp.dma_start(xt[:, u, :], xs_v[bass.ds(s, 1)].rearrange("a p d -> p (a d)")).then_inc(loaded[u], 16)

        @block.scalar
        def _(act):
            with act.Fori(0, SLOTS // R) as i:
                for u in range(R):
                    s = i * R + u
                    act.wait_ge(a_s, s + 1)
                    act.wait_ge(hg_s, i * R)
                    nc.scalar.activation(sa[:, u, :], up[:, u, 0, :], ACT.Silu).then_inc(silu_s, 1)
                    act.wait_ge(hgtr_s, s + 1)
                    act.wait_ge(y_s, i * R)
                    nc.scalar.activation(hgT[:, u], hid_ps[:], ACT.Copy).then_inc(hgT_s, 1)
                    act.wait_ge(yo_s, s + 1)
                    act.dma_start(ys_v[bass.ds(s, 1)].rearrange("a p d -> p (a d)"), yo[:, u, :]).then_inc(stored[u], 16)
            for u in range(R):
                act.wait_ge(stored[u], 16 * SLOTS // R)

        @block.vector
        def _(dve):
            with dve.Fori(0, SLOTS // R) as i:
                for u in range(R):
                    s = i * R + u
                    dve.wait_ge(tr_s, s + 1)
                    dve.wait_ge(g_s, i * R)
                    nc.vector.tensor_copy(xT[:, u, :], xT_ps[:]).then_inc(xT_s, 1)
                    dve.wait_ge(silu_s, s + 1)
                    dve.wait_ge(g_s, s + 1)
                    dve.wait_ge(hgtr_s, i * R)
                    nc.vector.tensor_tensor(hg[:, u, :], up[:, u, 1, :], sa[:, u, :], ALU.mult).then_inc(hg_s, 1)
                    dve.wait_ge(y_s, s + 1)
                    dve.wait_ge(stored[u], i * 16)
                    nc.vector.tensor_copy(yo[:, u, :], up[:, u, 0, 0:P]).then_inc(yo_s, 1)

        @block.tensor
        def _(pe):
            with pe.Fori(0, SLOTS // R) as i:
                for u in range(R):
                    s = i * R + u
                    e = pe.value_load(expert[0:1, bass.ds(s, 1)], min_val=0, max_val=E - 1)
                    pe.wait_ge(xT_s, s)
                    pe.wait_ge(loaded[u], i * 16 + 16)
                    pe.sem_inc(pe_go, 1)
                    nc.tensor.transpose(xT_ps[:], xt[:, u, :], ident[:]).then_inc(tr_s, 1)
                    pe.wait_ge(xT_s, s + 1)
                    pe.wait_ge(yo_s, i * R)
                    pe.sem_inc(pe_go, 1)
                    nc.tensor.matmul(up[:, u, 0, :], xT[:, u, :], w1s[:, bass.ds(e, 1), 0:FFN].rearrange("p a n -> p (a n)"),
                                     start=True, stop=True).then_inc(a_s, 1)
                    nc.tensor.matmul(up[:, u, 1, :], xT[:, u, :], w1s[:, bass.ds(e, 1), FFN:].rearrange("p a n -> p (a n)"),
                                     start=True, stop=True).then_inc(g_s, 1)
                    pe.wait_ge(hg_s, s + 1)
                    pe.wait_ge(hgT_s, s)
                    pe.sem_inc(pe_go, 1)
                    for k in range(KF):
                        tr = nc.tensor.transpose(hid_ps[:, k, :], hg[:, u, P * k:P * k + P], ident[:])
                    tr.then_inc(hgtr_s, 1)
                    pe.wait_ge(hgT_s, s + 1)
                    pe.sem_inc(pe_go, 1)
                    for k in range(KF):
                        mm = nc.tensor.matmul(up[:, u, 0, 0:P], hgT[:, u, k, :],
                                              w2s[:, bass.ds(e, 1), k, :].rearrange("p a n -> p (a n)"),
                                              start=k == 0, stop=k == KF - 1)
                    mm.then_inc(y_s, 1)


def build_combine(nc, name, X, yg, slot_idx, pmax, ys_dram, out_tiles):
    with ExitStack() as ctx:
        got, add_s, out_s = (ctx.enter_context(nc.semaphore(f"{name}_{n}")) for n in ("gathered", "added", "out_stored"))
        block = ctx.enter_context(nc.Block())

        @block.gpsimd
        def _(pool):
            for t in range(NT):
                nc.gpsimd.indirect_dma_start(out=yg[:, t, :], out_offset=None, in_=ys_dram,
                                             in_offset=bass.IndirectOffsetOnAxis(ap=slot_idx[:, t:t + 1], axis=0))\
                    .then_inc(got, 16)

        @block.vector
        def _(dve):
            dve.wait_ge(got, 16 * NT)
            for t in range(NT):
                k = nc.vector.scalar_tensor_tensor(X[:, t, :], yg[:, t, :], pmax[:, t:t + 1], X[:, t, :], ALU.mult, ALU.add)
                if t % 8 == 7:
                    k.then_inc(add_s, 1)

        @block.sync
        def _(sp):
            if out_tiles is not None:
                for q in range(NT // 8):
                    sp.wait_ge(add_s, q + 1)
                    sp.dma_start(out_tiles[:, 8 * q:8 * q + 8, :], X[:, 8 * q:8 * q + 8, :]).then_inc(out_s, 16)
                sp.wait_ge(out_s, 16 * (NT // 8))


def build_rwkv(nc, X, xn, ident, mv, rstd, stats, half, time_decay, time_first, mix_k, mix_v, mix_r,
               Wk_b, Wv_b, Wr_b, Wo_b):
    with ExitStack() as ctx:
        def sb(n, shape, dt=F32):
            return ctx.enter_context(nc.sbuf_tensor(f"rwkv_{n}", shape, dt))

        def sem(n):
            return ctx.enter_context(nc.semaphore(f"rwkv_{n}"))

        ps = ctx.enter_context(nc.psum_tensor("rwkv_ps", [P, 2, 3, T], F32))
        ops = ctx.enter_context(nc.psum_tensor("rwkv_out", [P, 2, T], F32))
        wraw = sb("wraw", [P, 4, P])
        wT = sb("wT", [P, 4, P])
        wcur, wold = sb("wcur", [P, 3, P]), sb("wold", [P, 3, P])
        mix, old = sb("mix", [P, 3]), sb("old", [P, 3])
        td, tf, lam = sb("td", [P, 1]), sb("tf", [P, 1]), sb("lam", [P, 1])
        etd, etf = sb("etd", [P, 1]), sb("etf", [P, 1])
        lamw, onew = sb("lamw", [P, T]), sb("onew", [P, T])
        xT = sb("xT", [P, B, 1 + T])
        kmin, kc, kv, er = (sb(n, [P, 2, T]) for n in ("kmin", "kc", "kv", "er"))
        sk, sv = sb("sk", [P, 2, 1 + T]), sb("sv", [P, 2, 1 + T])
        num, dn, rd, o = sb("num", [P, T]), sb("dn", [P, T]), sb("rd", [P, T]), sb("o", [P, 2, T])
        w_in, tr_s, wT_s, w_s, stat_s, scale_s, xn_s, xtr_s, xT_s = (sem(n) for n in (
            "loaded", "w_transposed", "wT_ready", "w_ready", "stats_done", "scales_done", "xn_ready", "x_transposed",
            "xT_ready"))
        k_s, v_s, r_s, kmin_s, kc_s, er_s, o_s, out_s, add_s, pch, vch, ach, lam_s = (sem(n) for n in (
            "k_psum", "v_psum", "r_psum", "k_clamped", "k_exp", "r_exp", "o_ready", "out_psum", "added", "pool_steps",
            "dve_steps", "act_steps", "lam_ready"))
        block = ctx.enter_context(nc.Block())

        @block.sync
        def _(sp):
            for k, w in enumerate((Wk_b, Wv_b, Wr_b, Wo_b)):
                sp.dma_start(wraw[:, k, :], w).then_inc(w_in, 16)
            for k, m in enumerate((mix_k, mix_v, mix_r)):
                sp.dma_start(mix[:, k:k + 1], m.rearrange("a b c -> c (a b)")).then_inc(w_in, 16)
            sp.dma_start(td[:], time_decay).then_inc(w_in, 16)
            sp.dma_start(tf[:], time_first).then_inc(w_in, 16)

        @block.gpsimd
        def _(pool):
            ch = Chain(pool, pch)
            pool.wait_ge(stat_s, 1)
            norm_scale(nc, pool, ch, mv, rstd, half).then_inc(scale_s, 1)

        @block.scalar
        def _(act):
            ch = Chain(act, ach)
            act.wait_ge(w_in, 16 * 9)
            ch.link(nc.scalar.activation(etd[:], td[:], ACT.Exp))
            nc.scalar.activation(etf[:], tf[:], ACT.Exp).then_inc(lam_s, 1)
            nc.scalar.activation(lam[:], etd[:], ACT.Exp, scale=-1.0).then_inc(lam_s, 1)
            for b in range(B):
                act.wait_ge(xtr_s, b + 1)
                nc.scalar.activation(xT[:, b, 1:], ops[:, b % 2, :], ACT.Copy).then_inc(xT_s, 1)
            with act.Fori(0, B // 2) as i:
                for u in range(2):
                    b = i * 2 + u
                    act.wait_ge(kmin_s, b + 1)
                    act.wait_ge(o_s, i * 2)
                    nc.scalar.activation(kc[:, u, :], kmin[:, u, :], ACT.Exp).then_inc(kc_s, 1)
                    act.wait_ge(r_s, b + 1)
                    nc.scalar.activation(er[:, u, :], ps[:, u, 2, :], ACT.Exp, scale=-1.0).then_inc(er_s, 1)

        @block.tensor
        def _(pe):
            pe.wait_ge(w_in, 16 * 9)
            for k in range(4):
                tr = nc.tensor.transpose(ps[:, 0, 0, P * k:P * k + P], wraw[:, k, :], ident[:])
            tr.then_inc(tr_s, 1)
            for b in range(B):
                pe.wait_ge(xn_s, b + 1)
                if b >= 2:
                    pe.wait_ge(xT_s, b - 1)
                for t in range(TPB):
                    tr = nc.tensor.transpose(ops[:, b % 2, P * t:P * t + P], xn[:, TPB * b + t, :], ident[:])
                tr.then_inc(xtr_s, 1)
            pe.wait_ge(w_s, 1)
            pe.wait_ge(xT_s, B)
            with pe.Fori(0, B // 2) as i:
                for u in range(2):
                    b = i * 2 + u
                    pe.wait_ge(o_s, i * 2)
                    for k, s in enumerate((k_s, v_s, r_s)):
                        cur = xT[:, bass.ds(b, 1), 1:].rearrange("p a t -> p (a t)")
                        prev = xT[:, bass.ds(b, 1), 0:T].rearrange("p a t -> p (a t)")
                        nc.tensor.matmul(ps[:, u, k, :], wcur[:, k, :], cur, start=True, stop=False)
                        nc.tensor.matmul(ps[:, u, k, :], wold[:, k, :], prev, start=False, stop=True).then_inc(s, 1)
                    pe.wait_ge(o_s, b + 1)
                    pe.wait_ge(add_s, i * 2)
                    for t in range(TPB):
                        mm = nc.tensor.matmul(ops[:, u, P * t:P * t + P], o[:, u, P * t:P * t + P], wT[:, 3, :],
                                              start=True, stop=True)
                    mm.then_inc(out_s, 1)

        @block.vector
        def _(dve):
            V = nc.vector
            ch = Chain(dve, vch)
            V.memset(xT[:, :, 0], 0.0)
            V.memset(sk[:, :, 0], 0.0)
            V.memset(sv[:, :, 0], 0.0)
            V.memset(onew[:], 1.0)
            layernorm_stats(nc, ch, X, stats, mv).then_inc(stat_s, 1)
            dve.wait_ge(scale_s, 1)
            for b in range(B):
                for t in range(TPB * b, TPB * b + TPB):
                    k = V.tensor_scalar(xn[:, t, :], X[:, t, :], mv[:, t, 0:1], rstd[:, t:t + 1], ALU.subtract, ALU.mult)
                k.then_inc(xn_s, 1)
            dve.wait_ge(w_in, 16 * 9)
            ch.link(V.tensor_scalar(old[:], mix[:], -1.0, 1.0, ALU.mult, ALU.add))
            dve.wait_ge(tr_s, 1)
            ch.link(V.tensor_copy(wT[:].rearrange("p k n -> p (k n)"), ps[:, 0, 0, :]))
            for k in range(3):
                V.tensor_scalar(wcur[:, k, :], wT[:, k, :], mix[:, k:k + 1], None, ALU.mult)
                w = V.tensor_scalar(wold[:, k, :], wT[:, k, :], old[:, k:k + 1], None, ALU.mult)
            w.then_inc(w_s, 1)
            dve.wait_ge(lam_s, 2)
            ch.link(V.tensor_scalar(lamw[:], onew[:], lam[:], None, ALU.mult))
            first = ch.n
            per = 8
            with dve.Fori(0, B // 2) as i:
                ch.at(i * (2 * per) + first)
                for u in range(2):
                    b = i * 2 + u
                    n0 = ch.n
                    dve.wait_ge(k_s, b + 1)
                    V.tensor_scalar(kmin[:, u, :], ps[:, u, 0, :], K_CLAMP, None, ALU.min).then_inc(kmin_s, 1)
                    dve.wait_ge(kc_s, b + 1)
                    dve.wait_ge(v_s, b + 1)
                    ch.link(V.tensor_tensor(kv[:, u, :], ps[:, u, 1, :], kc[:, u, :], ALU.mult))
                    ch.link(V.tensor_tensor_scan(sk[:, u, 1:], lamw[:], kc[:, u, :], 0.0, ALU.mult, ALU.add))
                    ch.link(V.tensor_tensor_scan(sv[:, u, 1:], lamw[:], kv[:, u, :], 0.0, ALU.mult, ALU.add))
                    ch.link(V.scalar_tensor_tensor(num[:], kv[:, u, :], etf[:], sv[:, u, 0:T], ALU.mult, ALU.add))
                    ch.link(V.scalar_tensor_tensor(dn[:], kc[:, u, :], etf[:], sk[:, u, 0:T], ALU.mult, ALU.add))
                    dve.wait_ge(er_s, b + 1)
                    ch.link(V.tensor_scalar(dn[:], dn[:], EPS_RWKV, None, ALU.add))
                    ch.link(V.scalar_tensor_tensor(dn[:], er[:, u, :], 1.0, dn[:], ALU.add, ALU.mult))
                    ch.link(V.reciprocal(rd[:], dn[:]))
                    dve.wait_ge(out_s, i * 2)
                    V.tensor_tensor(o[:, u, :], num[:], rd[:], ALU.mult).then_inc(o_s, 1)
                    dve.wait_ge(out_s, b + 1)
                    x = X[:, bass.ds(b * TPB, TPB), :].rearrange("p t d -> p (t d)")
                    V.tensor_tensor(x, ops[:, u, :], x, ALU.add).then_inc(add_s, 1)
                    assert ch.n - n0 == per


def build_prep(nc, x_tiles, norm_w, Wq, Wk, Wv, Wqf, Wkf, X, ident, identb, mv, rstd, stats, half,
               parts_dram, v_dram):
    with ExitStack() as ctx:
        def sb(name, shape, dt=F32):
            return ctx.enter_context(nc.sbuf_tensor(name, shape, dt))

        def sem(name):
            return ctx.enter_context(nc.semaphore(name))

        ps = ctx.enter_context(nc.psum_tensor("prep_ps", [P, 8, 512], F32))
        wq, wk, wv = sb("wq", [P, P]), sb("wk", [P, P]), sb("wv", [P, P])
        nw = sb("nw", [P, 1])
        wqfT, wkfT = sb("wqfT", [FEAT, HD]), sb("wkfT", [FEAT, HD])
        qrep, krep = sb("qrep", [FEAT, H, HD]), sb("krep", [FEAT, H, HD])
        same = sb("same", [P, P])
        feat = sb("feat", [P, P])
        r2 = sb("r2", [P, NT])
        t1 = sb("t1", [P, NT])
        hs = sb("hs", [P, NT])
        hn = sb("hn", [P, 2, TPB, P])
        xl = sb("xl", [P, NT, P])
        hT = sb("hT", [P, 2, WIN + T])
        kT = sb("kT", [P, 2, T])
        parts = sb("parts", [P, 2, 3, PARTS, T], BF16)
        rem = sb("rem", [P, 3, T])
        vs = sb("vs", [P, 2, NW, P])
        x_in_s, w_in_s = sem("x_loaded"), sem("w_loaded")
        const_s, pch, vch = sem("consts"), sem("pool_steps"), sem("dve_steps")
        stat_s, scale_s = sem("stats_done"), sem("scales_done")
        feat_ps, feat_s = sem("feat_psum"), sem("feat_done")
        hn_s, hnT_s, hT_s = sem("hn_ready"), sem("hnT_psum"), sem("hT_ready")
        q_s, k_s, kT_s, k2_s, v_s = (sem("q_psum"), sem("k_psum"), sem("kT_ready"), sem("k2_psum"),
                                     sem("v_psum"))
        part1_s, split_s, vs_s = sem("first_part"), sem("split_done"), sem("v_ready")
        stored = [sem("stored_even"), sem("stored_odd")]
        block = ctx.enter_context(nc.Block())

        @block.sync
        def _(sp):
            for q in range(4):
                sp.dma_start(X[:, 8 * q:8 * q + 8, :], x_tiles[:, 8 * q:8 * q + 8, :]).then_inc(x_in_s, 16)
            for dst, src in ((wq, Wq), (wk, Wk), (wv, Wv)):
                sp.dma_start(dst[:], src).then_inc(w_in_s, 16)
            sp.dma_start(nw[:], norm_w.rearrange("(p a) -> p a", a=1)).then_inc(w_in_s, 16)
            with nc.allow_non_contiguous_dma("128 numbers"):
                sp.dma_start(wqfT[:], Wqf.rearrange("d f -> f d")).then_inc(w_in_s, 16)
                sp.dma_start(wkfT[:], Wkf.rearrange("d f -> f d")).then_inc(w_in_s, 16)
            with sp.Fori(0, B // 2) as i:
                for u in range(2):
                    b = i * 2 + u
                    sp.wait_ge(split_s, i * 6 + 3 * u + 3)
                    for n in range(3):
                        sp.dma_start(parts_dram[n, bass.ds(b, 1)].rearrange("b c p t -> p (b c) t"), parts[:, u, n])\
                            .then_inc(stored[u], 16)
                    sp.wait_ge(vs_s, i * 4 + 2 * u + 2)
                    sp.dma_start(v_dram[bass.ds(b, 1)].rearrange("b p w n -> p (b w) n"), vs[:, u]).then_inc(stored[u], 16)
            for u in range(2):
                sp.wait_ge(stored[u], 16 * 4 * B // 2)

        @block.gpsimd
        def _(pool):
            ch = Chain(pool, pch)
            nc.gpsimd.memset(half[:], -0.5)
            nc.gpsimd.memset(hT[:, :, 0:WIN], 0.0)
            nc.gpsimd.memset(same[:], 0.5)
            ch.link(nc.gpsimd.memset(ident[:], 0.0))
            nc.gpsimd.affine_select(out=ident[:], in_=ident[:], compare_op=ALU.not_equal, fill=1.0,
                                    base=0, pattern=[[-1, P]], channel_multiplier=1)
            blocks = same[:].rearrange("p (h d) -> p h d", d=HD)
            ch.link(nc.gpsimd.affine_select(out=blocks, in_=blocks, compare_op=ALU.is_ge, fill=0.0, base=0,
                                            pattern=[[-HD, H], [0, HD]], channel_multiplier=1))
            ch.link(nc.gpsimd.affine_select(out=blocks, in_=blocks, compare_op=ALU.is_ge, fill=0.0, base=HD - 1,
                                            pattern=[[HD, H], [0, HD]], channel_multiplier=-1))
            nc.gpsimd.tensor_copy(identb[:], ident[:]).then_inc(const_s, 1)
            pool.wait_ge(stat_s, 1)
            ch.link(nc.gpsimd.tensor_scalar(t1[:], mv[:, :, 1], EPS_LN, None, ALU.add))
            ch.link(nc.gpsimd.tensor_tensor(rstd[:], t1[:], half[:], ALU.pow))
            ch.link(nc.gpsimd.tensor_tensor(t1[:], rstd[:], rstd[:], ALU.mult))
            ch.link(nc.gpsimd.tensor_tensor(t1[:], t1[:], mv[:, :, 1], ALU.mult))
            ch.link(nc.gpsimd.tensor_scalar(t1[:], t1[:], EPS_RMS, None, ALU.add))
            ch.link(nc.gpsimd.tensor_tensor(r2[:], t1[:], half[:], ALU.pow))
            nc.gpsimd.tensor_tensor(hs[:], rstd[:], r2[:], ALU.mult).then_inc(scale_s, 1)
            ch.link(nc.gpsimd.tensor_tensor(xl[:], X[:], mv[:, :, 0:1].broadcast_to([P, NT, P]), ALU.subtract))
            ch.link(nc.gpsimd.tensor_tensor(xl[:], xl[:], rstd[:].unsqueeze(2).broadcast_to([P, NT, P]), ALU.mult))
            pool.wait_ge(hn_s, B)
            nc.gpsimd.tensor_tensor(X[:], X[:], xl[:], ALU.add)

        @block.scalar
        def _(act):
            with act.Fori(0, B // 2) as i:
                for u in range(2):
                    act.wait_ge(hnT_s, i * 2 + u + 1)
                    nc.scalar.activation(hT[:, u, WIN:], ps[:, 0, :], ACT.Copy).then_inc(hT_s, 1)
                    act.wait_ge(k_s, i * 2 + u + 1)
                    nc.scalar.activation(kT[:, u, :], ps[:, 2, :], ACT.Copy).then_inc(kT_s, 1)
                    act.wait_ge(stored[u], i * (16 * 4))
                    act.wait_ge(q_s, i * 2 + u + 1)
                    nc.scalar.activation(parts[:, u, 0, 0, :], ps[:, 1, :], ACT.Copy).then_inc(part1_s, 1)
                    nc.scalar.activation(parts[:, u, 1, 0, :], ps[:, 2, :], ACT.Copy).then_inc(part1_s, 1)
                    act.wait_ge(k2_s, i * 2 + u + 1)
                    nc.scalar.activation(parts[:, u, 2, 0, :], ps[:, 3, :], ACT.Copy).then_inc(part1_s, 1)
                    for q in range(2):
                        act.wait_ge(v_s, i * 4 + 2 * u + q + 1)
                        nc.scalar.activation(vs[:, u, 4 * q:4 * q + 4, :], ps[:, 4 + q, :], ACT.Copy).then_inc(vs_s, 1)

        @block.vector
        def _(dve):
            ch = Chain(dve, vch)
            dve.wait_ge(x_in_s, 64)
            layernorm_stats(nc, ch, X, stats, mv).then_inc(stat_s, 1)
            dve.wait_ge(w_in_s, 96)
            for w in (wq, wk):
                nc.vector.tensor_scalar(w[:], w[:], nw[:], None, ALU.mult)
            nc.vector.tensor_scalar(wv[:], wv[:], nw[:], None, ALU.mult)
            nc.vector.tensor_copy(qrep[:], wqfT[:].rearrange("f (a d) -> f a d", a=1).broadcast_to([FEAT, H, HD]))
            nc.vector.tensor_copy(krep[:], wkfT[:].rearrange("f (a d) -> f a d", a=1).broadcast_to([FEAT, H, HD]))\
                .then_inc(feat_s, 1)
            dve.wait_ge(const_s, 1)
            dve.wait_ge(feat_ps, 1)
            nc.vector.tensor_tensor(feat[:], ps[:, 7, 0:P], same[:], ALU.mult).then_inc(feat_s, 1)
            dve.wait_ge(scale_s, 1)
            first = ch.n
            with dve.Fori(0, B // 2) as i:
                ch.at(first + i * 12)
                for u in range(2):
                    dve.wait_ge(hnT_s, i * 2)
                    for t in range(TPB):
                        k = i * (2 * TPB) + u * TPB + t
                        h = nc.vector.tensor_scalar(hn[:, u, t, :], X[:, k, :],
                                                    mv[:, k, 0:1], hs[:, bass.ds(k, 1)],
                                                    ALU.subtract, ALU.mult)
                    h.then_inc(hn_s, 1)
                    for n in range(3):
                        dve.wait_ge(part1_s, i * 6 + 3 * u + n + 1)
                        ch.link(nc.vector.tensor_tensor(rem[:, n, :], ps[:, 1 + n, :], parts[:, u, n, 0, :], ALU.subtract))
                        ch.link(nc.vector.tensor_copy(parts[:, u, n, 1, :], rem[:, n, :]))
                        nc.vector.tensor_tensor(parts[:, u, n, 2, :], rem[:, n, :], parts[:, u, n, 1, :],
                                                ALU.subtract).then_inc(split_s, 1)

        @block.tensor
        def _(pe):
            pe.wait_ge(feat_s, 1)
            nc.tensor.matmul(ps[:, 7, 0:P], krep[:], qrep[:], start=True, stop=True).then_inc(feat_ps, 1)
            pe.wait_ge(feat_s, 2)
            pe.wait_ge(const_s, 1)
            with pe.Fori(0, B // 2) as i:
                for u in range(2):
                    b = i * 2 + u
                    pe.wait_ge(hn_s, b + 1)
                    pe.wait_ge(hT_s, b)
                    for t in range(TPB):
                        tr = nc.tensor.transpose(ps[:, 0, P * t:P * t + P], hn[:, u, t, :], ident[:])
                    tr.then_inc(hnT_s, 1)
                    pe.wait_ge(hT_s, b + 1)
                    pe.wait_ge(split_s, b * 3)
                    nc.tensor.matmul(ps[:, 2, :], wk[:], hT[:, u, WIN:], start=True, stop=True).then_inc(k_s, 1)
                    nc.tensor.matmul(ps[:, 1, :], wq[:], hT[:, u, WIN:], start=True, stop=True).then_inc(q_s, 1)
                    for q in range(2):
                        pe.wait_ge(vs_s, b * 2 - 1 + q) if q else pe.wait_ge(vs_s, b * 2)
                        for w in range(4):
                            lo = WIN * (4 * q + w)
                            mm = nc.tensor.matmul(ps[:, 4 + q, P * w:P * w + P], hT[:, u, lo:lo + P], wv[:],
                                                  start=True, stop=True)
                        mm.then_inc(v_s, 1)
                    pe.wait_ge(kT_s, b + 1)
                    nc.tensor.matmul(ps[:, 3, :], feat[:], kT[:, u, :], start=True, stop=True).then_inc(k2_s, 1)

_INS = ['L0_attn_a_x','L0_attn_a_norm_w','L0_attn_a_Wq','L0_attn_a_Wk','L0_attn_a_Wv','L0_attn_a_Wqf','L0_attn_a_Wkf','L0_attn_a_Wout','L0_attn_b_xk','L0_attn_b_xv','L0_attn_b_time_decay','L0_attn_b_time_first','L0_attn_b_time_mix_k','L0_attn_b_time_mix_v','L0_attn_b_time_mix_r','L0_attn_b_Wk','L0_attn_b_Wv','L0_attn_b_Wr','L0_attn_b_Wo','L0_ffn_router_w','L0_ffn_router_b','L0_ffn_w1','L0_ffn_w2']

def kernel(**inputs):
    import numpy as _np
    import concourse.bacc as _bacc
    from concourse import mybir as _mybir
    from concourse.bass_utils import run_bass_kernel_spmd as _run
    nc = _bacc.Bacc("TRN2", target_bir_lowering=False, num_devices=1)
    arrays, args = {}, []
    for name in _INS:
        a = _np.ascontiguousarray(inputs[name])
        arrays[f"in_{name}_dram"] = a
        args.append(nc.dram_tensor(f"in_{name}_dram", a.shape, _mybir.dt.from_np(a.dtype), kind="ExternalInput").ap())
    out = nc.dram_tensor("out_dram", (8, 512, 128), _mybir.dt.float32, kind="ExternalOutput").ap()
    build(nc, *args, out)
    r = _run(nc, [arrays], core_ids=[0])
    return r.results[0]["out_dram"]
```

```python
import concourse.bass as bass
from concourse import mybir
from contextlib import ExitStack

F32 = mybir.dt.float32
BF16 = mybir.dt.bfloat16
I32 = mybir.dt.int32
U32 = mybir.dt.uint32
ALU = mybir.AluOpType
ACT = mybir.ActivationFunctionType
AX = mybir.AxisListType

P = 128
B = 8
T = 512
TPB = T // P
NT = B * TPB
H = 16
HD = P // H
FEAT = 16
WIN = 64
NW = T // WIN
NP = H // 2
PARTS = 3
ROWS = 6 * HD
BIAS = 2 * ROWS
SROWS = BIAS + 2 * PARTS
NEG = -1.0e30
E = 8
FFN = 512
KF = FFN // P
ROW = P + 4
SLOTS = NT + E - 1
EPS_LN = 1e-5
EPS_RMS = 1e-6
EPS_LIN = 1e-6
EPS_RWKV = 1e-8
K_CLAMP = 60.0
PRODUCTS = [(0, 0), (0, 1), (0, 2), (1, 0), (1, 1), (2, 0)]


class Chain:

    def __init__(self, engine, sem):
        self.engine, self.sem, self.base, self.n = engine, sem, 0, 0

    def at(self, base):
        self.base, self.n = base, 0

    def link(self, ins):
        self.n += 1
        ins.then_inc(self.sem, 1)
        self.engine.wait_ge(self.sem, self.base + self.n)


def layernorm_stats(nc, ch, x, stats, mv):
    for t in range(NT - 1):
        nc.vector.bn_stats(stats[:, t, :], x[:, t, :])
    ch.link(nc.vector.bn_stats(stats[:, NT - 1, :], x[:, NT - 1, :]))
    for t in range(NT):
        last = nc.vector.bn_aggr(mv[:, t, :], stats[:, t, :])
    return last


def build(nc, x_in, norm_w, Wq, Wk, Wv, Wqf, Wkf, Wout, xk_in, xv_in, time_decay, time_first,
          mix_k, mix_v, mix_r, Wk_b, Wv_b, Wr_b, Wo_b, router_w, router_b, w1, w2, out):
    x_tiles = x_in.rearrange("b (t p) d -> p (b t) d", p=P)
    out_tiles = out.rearrange("b (t p) d -> p (b t) d", p=P)
    parts_dram = nc.dram_tensor("parts_dram", (3, B, PARTS, P, T), BF16).ap()
    v_dram = nc.dram_tensor("v_dram", (B, P, NW, P), F32).ap()
    negmax_dram = nc.dram_tensor("negmax_dram", (B, 2, PARTS, NP * NW, WIN), BF16).ap()
    xs_dram = {name: nc.dram_tensor(f"{name}_xs_dram", (SLOTS * P, ROW), F32).ap() for name in ("ffn1", "ffn2")}
    y_dram = nc.dram_tensor("y_dram", ((NT + SLOTS) * P, P), F32).ap()
    with ExitStack() as ctx:
        def sb(name, shape, dt=F32):
            return ctx.enter_context(nc.sbuf_tensor(name, shape, dt))

        X = sb("X", [P, NT, P])
        ident = sb("ident", [P, P])
        identb = sb("identb", [P, P], BF16)
        mv = sb("mv", [P, NT, 2])
        rstd = sb("rstd", [P, NT])
        stats = sb("stats", [P, NT, 6])
        half = sb("half", [P, NT])
        slot_idx = sb("slot_idx", [P, NT], U32)
        expert = sb("expert", [1, SLOTS], I32)
        pmax = sb("pmax", [P, NT])
        with ExitStack() as attention:
            def at(name, shape, dt=F32):
                return attention.enter_context(nc.sbuf_tensor(name, shape, dt))

            qs = [at(f"qs{u}", [SROWS, 2, NP, T], BF16) for u in range(2)]
            ks = [at(f"ks{u}", [SROWS, WIN + NP * T], BF16) for u in range(2)]
            k2s = [at(f"k2s{u}", [BIAS, NP, T], BF16) for u in range(2)]
            v = [at(f"v{u}", [P, NW, P]) for u in range(2)]
            maskq = at("maskq", [P, NW, P], BF16)
            maskk = at("maskk", [P, NW * 2, WIN], BF16)
            operands = (qs, ks, k2s, v)
            build_prep(nc, x_tiles, norm_w, Wq, Wk, Wv, Wqf, Wkf, X, ident, identb, mv, rstd, stats, half,
                       parts_dram, v_dram, xs_dram, operands, maskq, maskk)
            build_attention(nc, X, ident, identb, Wout, parts_dram, v_dram, negmax_dram, operands, maskq, maskk)
        w1s = sb("w1s", [P, E, 2, FFN])
        w2s = sb("w2s", [P, E, KF, P])
        xn = sb("xn", [P, NT, ROW])
        yg = sb("yg", [P, NT, P])
        first = (w1, w2, w1s, w2s)
        for name in ("ffn1", "ffn2"):
            build_route(nc, name, X, xn, ident, mv, rstd, stats, half, router_w, router_b, slot_idx, expert, pmax,
                        xs_dram[name], first)
            build_experts(nc, name, ident, w1s, w2s, expert, xs_dram[name], y_dram)
            if name == "ffn1":
                build_rwkv(nc, X, yg, y_dram, xn, ident, mv, rstd, stats, half, time_decay, time_first, mix_k, mix_v, mix_r,
                           Wk_b, Wv_b, Wr_b, Wo_b)
            else:
                build_combine(nc, name, X, yg, y_dram, out_tiles)
            first = None


GROUPS = [(kp, sum(k == kp for k, _ in PRODUCTS)) for kp in range(PARTS)]
assert PRODUCTS == [(kp, qp) for kp, n in GROUPS for qp in range(n)]
LOADS = 6 * len(GROUPS) + 1


def load_operands(sp, operands, parts_dram, v_dram, b, u, loaded):
    qs, ks, k2s, v = operands
    for hh in range(2):
        lo = hh * ROWS
        for kp, n in GROUPS:
            rows = slice(lo, lo + n * HD)
            part = parts_dram[:, bass.ds(b, 1)].rearrange("w b c (d x h) t -> w x (b c) d (h t)", x=2, h=NP)[:, hh]
            sp.dma_start(qs[u][rows, hh, :, :].rearrange("r h t -> r (h t)"), part[0, 0:n]).then_inc(loaded, 16)
            for dst, which in ((ks[u][rows, WIN:], 1), (k2s[u][rows, :, :].rearrange("r h t -> r (h t)"), 2)):
                src = part[which, kp:kp + 1].broadcast_to([n, HD, NP * T])
                sp.dma_start(dst, src).then_inc(loaded, 16)
            lo += n * HD
    sp.dma_start(v[u][:], v_dram[bass.ds(b, 1)].rearrange("b p w n -> p (b w) n")).then_inc(loaded, 16)


def build_attention(nc, X, ident, identb, Wout, parts_dram, v_dram, negmax_dram, operands, maskq, maskk):
    LIN = [[(0, 0)], [(1, 0)], [(2, 0), (3, 2 * P)]]
    NL = 4 * len(LIN)
    NU = NL + 4
    MAX_AFTER = (5, 6, 7, 8, 9, 10, 11, 15)
    RP = 4
    LAG = 2
    SUM = 16

    def schedule(first, last, slot):
        jobs = []
        for n in range(NU):
            jobs += [("unit", n, 0), ("unit", n, 1)]
            if n == 0:
                jobs.append(("negmax", 0, 0))
            if not first:
                if n in (1, 3):
                    jobs.append(("norm", n // 2, 0))
                if n == 5:
                    jobs.append(("back", 0, 0))
                if n == 7:
                    jobs.append(("out", 0, 0))
            if n in MAX_AFTER and not last:
                jobs.append(("max", MAX_AFTER.index(n), 0))
        return [(*job, (slot + k) % 2) for k, job in enumerate(jobs)]

    FIRST, EVEN, ODD, LAST = (schedule(*at) for at in ((True, False, 1), (False, False, 1), (False, False, 0), (False, True, 0)))
    assert len(FIRST) % 2 == len(ODD) % 2 == len(EVEN) % 2 == len(LAST) % 2 == 1

    def batches(engine, body):
        body(0, 0, 0, FIRST)
        with engine.Fori(0, B // 2 - 1) as i:
            body(i * 2 + 1, i, 1, ODD)
            body(i * 2 + 2, i + 1, 0, EVEN)
        body(B - 1, B // 2 - 1, 1, LAST)

    with ExitStack() as ctx:
        def sb(name, shape, dt=F32):
            return ctx.enter_context(nc.sbuf_tensor(name, shape, dt))

        def sem(name):
            return ctx.enter_context(nc.semaphore(name))

        def both(name):
            return [sem(name + "_even"), sem(name + "_odd")]

        sc = ctx.enter_context(nc.psum_tensor("scores", [P, 2, 1024], F32))
        acc = ctx.enter_context(nc.psum_tensor("acc", [P, 2, 2, T], F32))
        qs, ks, k2s, v = operands
        qm = sb("qm", [BIAS, NP, NW, 2, WIN], BF16)
        vpad = [sb(f"vpad{u}", [P, NW, H, 32]) for u in range(2)]
        prob = sb("prob", [P, RP, 2, 1024])
        mx = sb("mx", [P, 2, NP, NW])
        nm = sb("nm", [NP * NW, 2, PARTS, P], BF16)
        nr = sb("nr", [NP * NW, P])
        sums_sb = sb("sums_sb", [P, 2, 2, T])
        den, rden = sb("den", [P, TPB * H]), sb("rden", [P, TPB * H])
        ytok = sb("ytok", [P, 2, TPB, P])
        yT = sb("yT", [P, 2, T])
        wo = sb("wo", [P, 2, P])
        loaded, nm_stored, nm_loaded = both("loaded"), both("negmax_stored"), both("negmax_loaded")
        wo_s, pch, vch = (sem(n) for n in ("wout_loaded", "pool_steps", "dve_steps"))
        sp_go, pool_go, pe_go = sem("sp_goes"), sem("pool_goes"), sem("pe_goes")
        vpad_s, masked_s, qm_s = sem("vpad_ready"), sem("lin_masked"), sem("qm_ready")
        mjob, tjob, ujob, njob, bjob, ojob = (sem(n) for n in (
            "max_scores", "negmax_transposed", "unit_scores", "sums_transposed", "y_transposed", "out_ready"))
        maxed, split_s, exped, normed, backed, added = (sem(n) for n in (
            "max_done", "negmax_split", "weights_ready", "normalised", "yT_ready", "out_added"))
        pv_s = sem("unit_summed")
        copied = (sem("lin_sums_copied"), sem("win_sums_copied"))
        block = ctx.enter_context(nc.Block())

        @block.sync
        def _(sp):
            for y in range(2):
                for g in range(4):
                    lo = 64 * y + SUM * g
                    sp.dma_start(wo[lo:lo + SUM, :, :], Wout.rearrange("(k g y r) n -> g y r k n", k=2, g=4, y=2)[g, y])\
                        .then_inc(wo_s, 16)
            load_operands(sp, operands, parts_dram, v_dram, 1, 1, loaded[1])
            with sp.Fori(0, B // 2 - 1) as i:
                for u in range(2):
                    b = i * 2 + u + 1
                    sp.wait_ge(exped, b * (2 * NU))
                    sp.sem_inc(sp_go, 1)
                    load_operands(sp, operands, parts_dram, v_dram, b + 1, u, loaded[u])

        @block.gpsimd
        def _(pool):
            ch = Chain(pool, pch)
            def spread(k, u):
                for s in range(2):
                    nc.gpsimd.tensor_copy(
                        vpad[u][:].rearrange("p w (h s) r -> p (w h) s r", s=2)[:, :, s, SUM * s:SUM * s + HD],
                        v[u][:].rearrange("p w (h s d) -> p (w h) s d", s=2, d=HD)[:, :, s, :]).then_inc(vpad_s, 1)

            for u in range(2):
                ch.link(nc.gpsimd.memset(vpad[u][:], 0.0))
                for s in range(2):
                    ch.link(nc.gpsimd.memset(vpad[u][:].rearrange("p w (h s) r -> p (w h) s r", s=2)
                                             [:, :, s, SUM * s + HD:SUM * s + HD + 1], 1.0))
            spread(0, 0)

            def body(b, k, u, jobs):
                for kind, n, a, slot in jobs:
                    if kind != "unit" or n >= NL:
                        continue
                    pool.wait_ge(exped, b * (2 * NU) + 2 * n + a + 1)
                    pool.sem_inc(pool_go, 1)
                    for kc, col in LIN[n % len(LIN)]:
                        m = prob[:, n % RP, a, :].rearrange("p (h n) -> p h n", h=2)[:, :, col:col + P]
                        sel = nc.gpsimd.affine_select(out=m, in_=m, compare_op=ALU.is_ge, fill=0.0, base=0,
                                                      pattern=[[0, 2], [1, P]], channel_multiplier=-1)
                    sel.then_inc(masked_s, 1)
                if jobs is not LAST:
                    pool.wait_ge(loaded[1 - u], k * (16 * LOADS) + 16 * LOADS)
                    if jobs is not FIRST:
                        pool.sem_inc(pool_go, 1)
                        pool.wait_ge(pv_s, b * NU)
                        pool.sem_inc(pool_go, 1)
                    spread(k, 1 - u)

            batches(pool, body)

        @block.scalar
        def _(act):
            def back(count, slot):
                act.wait_ge(bjob, count)
                nc.scalar.activation(yT[:].rearrange("p k t -> p (k t)"), sc[:, slot, :], ACT.Copy).then_inc(backed, 1)

            def body(b, k, u, jobs):
                for kind, n, a, slot in jobs:
                    if kind == "unit":
                        act.wait_ge(ujob, b * (2 * NU) + 2 * n + a + 1)
                        if jobs is not FIRST or n >= RP:
                            act.wait_ge(pv_s, b * NU + n - RP + 1)
                        if n < NL:
                            w = max(col + (TPB - kc) * P for kc, col in LIN[n % len(LIN)])
                            nc.scalar.activation(prob[:, n % RP, a, :].rearrange("p (h n) -> p h n", h=2)[:, :, 0:w],
                                                 sc[:, slot, :].rearrange("p (h n) -> p h n", h=2)[:, :, 0:w],
                                                 ACT.Square, bias=1.0).then_inc(exped, 1)
                        else:
                            nc.scalar.activation(prob[:, n % RP, a, :], sc[:, slot, :], ACT.Exp,
                                                 scale=float(HD) ** -0.5).then_inc(exped, 1)
                    if kind == "back":
                        back(b, slot)
                    if (kind, n, a) == ("unit", 2, 0):
                        act.wait_ge(split_s, b + 1)
                        for hh in range(2):
                            act.dma_start(negmax_dram[bass.ds(b, 1), hh].rearrange("b c k q -> k (b c) q"),
                                          nm[:, u, :, WIN * hh:WIN * hh + WIN]).then_inc(nm_stored[u], 16)
                    if (kind, n, a) == ("unit", 5, 0):
                        act.wait_ge(nm_stored[u], k * 32 + 32)
                        for hh in range(2):
                            lo = BIAS + PARTS * hh
                            act.dma_start(qs[u][lo:lo + PARTS, hh, :, :].rearrange("c p t -> c (p t)"),
                                          negmax_dram[bass.ds(b, 1), hh].rearrange("b c k q -> (b c) (k q)"))\
                                .then_inc(nm_loaded[u], 16)

            batches(act, body)
            back(B, 1)

        @block.vector
        def _(dve):
            V = nc.vector
            ch = Chain(dve, vch)
            CHAINED = 3 + 2 + 2

            def copy_sums(k, count):
                dve.wait_ge(pv_s, count)
                V.tensor_copy(sums_sb[:, k].rearrange("p y t -> p (y t)"), acc[:, k].rearrange("p y t -> p (y t)"))\
                    .then_inc(copied[k], 1)

            def normalise(k, count, slot):
                dve.wait_ge(njob, count)
                s = sc[:, slot, :].rearrange("p (h r) -> p h r", r=SUM)
                ch.link(V.tensor_scalar(den[:], s[:, :, HD], EPS_LIN if k == 0 else 0.0, None, ALU.add))
                ch.link(V.reciprocal(rden[:], den[:]))
                V.tensor_tensor(ytok[:, k].rearrange("p t (h d) -> p (t h) d", d=HD), s[:, :, 0:HD],
                                rden[:].unsqueeze(2).broadcast_to([P, TPB * H, HD]), ALU.mult).then_inc(normed, 1)

            def q_side_by_side(u):
                for hh in range(2):
                    last = V.tensor_copy(qm[:, :, :, hh, :].rearrange("r p w q -> r (p w) q"),
                                         qs[u][0:BIAS, hh].rearrange("r p (w q) -> r (p w) q", q=WIN))
                last.then_inc(qm_s, 1)

            def maximum(count, u, m, slot):
                dve.wait_ge(mjob, count)
                V.tensor_reduce(mx[:, u, m, :], sc[:, slot, :].rearrange("p (w k) -> p w k", w=NW),
                                AX.X, ALU.max, negate=True).then_inc(maxed, 1)

            def add_out(b, slot):
                x = X[:, bass.ds(b * TPB, TPB), :].rearrange("p t d -> p (t d)")
                V.tensor_tensor(x, sc[:, slot, 0:T], x, ALU.add).then_inc(added, 1)

            q_side_by_side(0)
            for m in range(NP):
                maximum(m + 1, 0, m, (m + 1) % 2)

            def body(b, k, u, jobs):
                ch.at(0 if jobs is FIRST else b * CHAINED - 4)
                for kind, n, a, slot in jobs:
                    if kind == "negmax":
                        dve.wait_ge(tjob, b + 1)
                        tr = sc[0:NP * NW, slot, 0:P]
                        ch.link(V.tensor_copy(nm[:, u, 0, :], tr))
                        ch.link(V.tensor_tensor(nr[:], tr, nm[:, u, 0, :], ALU.subtract))
                        ch.link(V.tensor_copy(nm[:, u, 1, :], nr[:]))
                        V.tensor_tensor(nm[:, u, 2, :], nr[:], nm[:, u, 1, :], ALU.subtract).then_inc(split_s, 1)
                    if kind == "norm":
                        normalise(n, b * 2 - 1 + n, slot)
                    if kind == "out":
                        dve.wait_ge(ojob, b)
                        add_out(b - 1, slot)
                    if kind == "max":
                        if n == 0:
                            dve.wait_ge(loaded[1 - u], k * (16 * LOADS) + 16 * LOADS)
                            q_side_by_side(1 - u)
                        maximum(b * NP + NP + n + 1, 1 - u, n, slot)
                    if (kind, n, a) == ("unit", LAG, 0) and jobs is not FIRST:
                        copy_sums(1, b * NU)
                    if (kind, n, a) == ("unit", NL - 1 + LAG, 1):
                        copy_sums(0, b * NU + NL)

            batches(dve, body)
            ch.at(B * CHAINED - 4)
            copy_sums(1, B * NU)
            normalise(0, 2 * B - 1, 1)
            normalise(1, 2 * B, 0)
            dve.wait_ge(ojob, B)
            add_out(B - 1, 0)

        @block.tensor
        def _(pe):
            free = [None, None]

            def take(slot, reader, value):
                if free[slot]:
                    pe.wait_ge(*free[slot])
                    pe.sem_inc(pe_go, 1)
                free[slot] = (reader, value)

            def lin_scores(u, j, part, a, slot):
                p = j + 4 * a
                for kc, col in LIN[part]:
                    for hh in range(2):
                        at = T * hh + col
                        mm = nc.tensor.matmul(sc[:, slot, at:at + T - P * kc], k2s[u][:, p, P * kc:P * kc + P],
                                              qs[u][0:BIAS, hh, p, P * kc:], start=True, stop=True)
                return mm

            def win_scores(u, j, a, slot):
                p = j + 4 * a
                for f in range(2):
                    nc.tensor.matmul(sc[:, slot, T * f:T * f + T], identb[:], maskk[:, NW * f:NW * f + NW, :],
                                     start=True, stop=False, skip_group_check=True)
                    for w in range(4 * f, 4 * f + 4):
                        mm = nc.tensor.matmul(sc[:, slot, P * w:P * w + P], ks[u][:, T * p + WIN * w:T * p + WIN * w + P],
                                              qs[u][:, :, p, WIN * w:WIN * w + WIN], start=False, stop=True,
                                              skip_group_check=True)
                return mm

            def max_scores(u, m, slot):
                for f in range(2):
                    nc.tensor.matmul(sc[:, slot, T * f:T * f + T], identb[:], maskq[:, 4 * f:4 * f + 4, :],
                                     start=True, stop=False, skip_group_check=True)
                    for w in range(4 * f, 4 * f + 4):
                        mm = nc.tensor.matmul(sc[:, slot, P * w:P * w + P],
                                              qm[:, m, w, :, :].rearrange("r h q -> r (h q)"),
                                              ks[u][0:BIAS, T * m + WIN * w:T * m + WIN * w + P], start=False, stop=True,
                                              skip_group_check=True)
                return mm

            def sums(u, n):
                if n < NL:
                    j, todo = n // len(LIN), [(2 * kc + 1, P * kc, T - P * kc, [T * hh + col for hh in range(2)])
                                              for kc, col in LIN[n % len(LIN)]]
                    k, opens = 0, n % len(LIN) == 0 and j % 2 == 0
                else:
                    j, todo = n - NL, [(w, WIN * w, WIN, [P * w + WIN * hh for hh in range(2)]) for w in range(NW)]
                    k, opens = 1, j % 2 == 0
                for x, (w, col, width, at) in enumerate(todo):
                    for a in range(2):
                        for hh in range(2):
                            g = a + 2 * hh
                            mm = nc.tensor.matmul(acc[32 * g:32 * g + 32, k, j // 2, col:col + width],
                                                  vpad[u][:, w, 4 * g + j, :], prob[:, n % RP, a, at[hh]:at[hh] + width],
                                                  start=opens and x == 0, stop=True, skip_group_check=True)
                return mm

            def norm_job(k, slot):
                for t in range(TPB):
                    for y in range(2):
                        tr = nc.tensor.transpose(sc[:, slot, P * (2 * t + y):P * (2 * t + y) + P],
                                                 sums_sb[:, k, y, P * t:P * t + P], ident[:])
                return tr

            def back_job(slot):
                for k in range(2):
                    for t in range(TPB):
                        at = T * k + P * t
                        tr = nc.tensor.transpose(sc[:, slot, at:at + P], ytok[:, k, t, :], ident[:])
                return tr

            def out_job(slot):
                for t in range(TPB):
                    for k in range(2):
                        mm = nc.tensor.matmul(sc[:, slot, P * t:P * t + P], yT[:, k, P * t:P * t + P], wo[:, k, :],
                                              start=k == 0, stop=k == 1)
                return mm

            pe.wait_ge(wo_s, 8 * 16)
            pe.wait_ge(qm_s, 1)
            for m in range(NP):
                slot = (m + 1) % 2
                take(slot, maxed, m + 1)
                max_scores(0, m, slot).then_inc(mjob, 1)

            def body(b, k, u, jobs):
                if jobs is not FIRST:
                    free[jobs[0][3]] = (exped, b * (2 * NU))
                    free[1 - jobs[0][3]] = (maxed, b * NP + NP)
                for at, (kind, n, a, slot) in enumerate(jobs):
                    if kind == "unit":
                        if n == NL and a == 0:
                            pe.wait_ge(nm_loaded[u], k * 32 + 32)
                        take(slot, exped, b * (2 * NU) + 2 * n + a + 1)
                        if n < NL:
                            lin_scores(u, n // len(LIN), n % len(LIN), a, slot).then_inc(ujob, 1)
                        else:
                            win_scores(u, n - NL, a, slot).then_inc(ujob, 1)
                    if kind == "unit" and a == 0:
                        if n >= LAG:
                            unit_sums(b, u, n - LAG, jobs)
                        elif jobs is not FIRST:
                            unit_sums(b - 1, 1 - u, n + NU - LAG, jobs)
                    if kind == "negmax":
                        take(slot, split_s, b + 1)
                        pe.wait_ge(maxed, b * NP + NP)
                        pe.sem_inc(pe_go, 1)
                        nc.tensor.transpose(sc[0:NP * NW, slot, 0:P], mx[:, u, :, :].rearrange("p m w -> p (m w)"),
                                            ident[:]).then_inc(tjob, 1)
                    if kind == "norm":
                        take(slot, normed, b * 2 - 1 + n)
                        pe.wait_ge(copied[n], b)
                        pe.sem_inc(pe_go, 1)
                        norm_job(n, slot).then_inc(njob, 1)
                    if kind == "back":
                        take(slot, backed, b)
                        pe.wait_ge(normed, b * 2)
                        pe.sem_inc(pe_go, 1)
                        back_job(slot).then_inc(bjob, 1)
                    if kind == "out":
                        take(slot, added, b)
                        pe.wait_ge(backed, b)
                        pe.sem_inc(pe_go, 1)
                        out_job(slot).then_inc(ojob, 1)
                    if kind == "max":
                        take(slot, maxed, b * NP + NP + n + 1)
                        if n == 0:
                            pe.wait_ge(qm_s, b + 2)
                            pe.sem_inc(pe_go, 1)
                        max_scores(1 - u, n, slot).then_inc(mjob, 1)

            def unit_sums(b, u, m, jobs):
                if m == 0:
                    pe.wait_ge(vpad_s, b * 2 + 2)
                    if jobs is not FIRST:
                        pe.wait_ge(copied[0], b)
                if m == NL and jobs is not FIRST:
                    pe.wait_ge(copied[1], b)
                if m < NL:
                    pe.wait_ge(masked_s, b * (2 * NL) + 2 * m + 2)
                else:
                    pe.wait_ge(exped, b * (2 * NU) + 2 * m + 2)
                sums(u, m).then_inc(pv_s, 1)

            batches(pe, body)
            for m in range(NU - LAG, NU):
                unit_sums(B - 1, 1, m, LAST)
            pe.wait_ge(exped, B * 2 * NU - 1)
            pe.wait_ge(copied[0], B)
            norm_job(0, 1).then_inc(njob, 1)
            pe.wait_ge(exped, B * 2 * NU)
            pe.wait_ge(copied[1], B)
            norm_job(1, 0).then_inc(njob, 1)
            pe.wait_ge(normed, 2 * B)
            back_job(1).then_inc(bjob, 1)
            pe.wait_ge(backed, B)
            out_job(0).then_inc(ojob, 1)


LN = 4
LNT = NT // LN


def normalise_tokens(nc, dve, ch, X, xn, stats, mv, rstd, stat_s, scale_s, xn_s, ready=None):
    for q in range(LN + 1):
        if q < LN:
            if ready:
                ready(q)
            for t in range(LNT * q, LNT * q + LNT):
                st = nc.vector.bn_stats(stats[:, t, :], X[:, t, :])
            ch.link(st)
            for t in range(LNT * q, LNT * q + LNT):
                ag = nc.vector.bn_aggr(mv[:, t, :], stats[:, t, :])
            ag.then_inc(stat_s, 1)
        if q:
            dve.wait_ge(scale_s, q)
            for t in range(LNT * (q - 1), LNT * q):
                k = nc.vector.tensor_scalar(xn[:, t, 0:P], X[:, t, :], mv[:, t, 0:1], rstd[:, t:t + 1],
                                            ALU.subtract, ALU.mult)
                if t % TPB == TPB - 1:
                    k.then_inc(xn_s, 1)


def norm_scale(nc, pool, ch, mv, rstd, half, q, stat_s, scale_s):
    part = slice(LNT * q, LNT * q + LNT)
    pool.wait_ge(stat_s, q + 1)
    ch.link(nc.gpsimd.tensor_scalar(rstd[:, part], mv[:, part, 1], EPS_LN, None, ALU.add))
    nc.gpsimd.tensor_tensor(rstd[:, part], rstd[:, part], half[:, part], ALU.pow).then_inc(scale_s, 1)


def build_route(nc, name, X, xn, ident, mv, rstd, stats, half, router_w, router_b, slot_idx, expert, pmax,
                xs_dram, weights):
    with ExitStack() as ctx:
        def sb(n, shape, dt=F32):
            return ctx.enter_context(nc.sbuf_tensor(f"{name}_{n}", shape, dt))

        def sem(n):
            return ctx.enter_context(nc.semaphore(f"{name}_{n}"))

        trp = ctx.enter_context(nc.psum_tensor(f"{name}_trp", [P, 2, T], F32))
        logit_ps = ctx.enter_context(nc.psum_tensor(f"{name}_logit_ps", [P, NT, E], F32))
        cnt_ps = ctx.enter_context(nc.psum_tensor(f"{name}_cnt_ps", [P, 2, 512], F32))
        xT = sb("xT", [P, 2, T])
        rw, rb = sb("rw", [P, E]), sb("rb", [P, E])
        logit, ex, eq, cand = (sb(n, [P, NT, E]) for n in ("logit", "ex", "eq", "cand"))
        best, total = sb("best", [P, NT]), sb("total", [P, NT])
        weight = sb("weight", [P, E])
        hot = sb("hot", [P, E, NT])
        hotb = sb("hotb", [P, E, NT], BF16)
        before, oneb = sb("before", [P, P], BF16), sb("oneb", [P, P], BF16)
        ones = sb("ones", [P, E * NT])
        tot, cum, place = (sb(n, [P, E, NT]) for n in ("tot", "cum", "place"))
        count, tiles, end, off = (sb(n, [P, E]) for n in ("count", "tiles", "end", "off"))
        steps = sb("steps", [P, NT])
        slotno = sb("slotno", [1, SLOTS])
        ended, past = sb("ended", [1, SLOTS, E]), sb("past", [1, SLOTS])
        slotf = sb("slotf", [P, NT])
        r_in, w_in, stat_s, scale_s, xn_s, tr_s, xT_s, logit_s = (sem(n) for n in (
            "router_loaded", "weights_loaded", "stats_done", "scales_done", "xn_ready", "xn_transposed", "xT_ready",
            "logits_ready"))
        fill_s = sem("rows_filled")
        const_s, pch, vch, shift_s, exp_s, hot_s, cnt_s, slot_s, sorted_s = (sem(n) for n in (
            "consts", "pool_steps", "dve_steps", "logits_shifted", "exp_done", "hot_ready", "counts_ready",
            "slots_ready", "sorted"))
        block = ctx.enter_context(nc.Block())

        @block.sync
        def _(sp):
            sp.dma_start(rw[:], router_w).then_inc(r_in, 16)
            sp.dma_start(rb[:], router_b.partition_broadcast(P)).then_inc(r_in, 16)
            if weights:
                w1, w2, w1s, w2s = weights
                for e in range(E):
                    sp.dma_start(w1s[:, e, :, :].rearrange("p a n -> p (a n)"), w1[e]).then_inc(w_in, 16)
                    sp.dma_start(w2s[:, e, :, :], w2[e].rearrange("(k p) n -> p k n", p=P)).then_inc(w_in, 16)
                sp.wait_ge(w_in, 32 * E)

        @block.gpsimd
        def _(pool):
            ch = Chain(pool, pch)
            ch.link(nc.gpsimd.memset(before[:], 1.0))
            nc.gpsimd.affine_select(out=before[:], in_=before[:], compare_op=ALU.is_gt, fill=0.0, base=0,
                                    pattern=[[1, P]], channel_multiplier=-1).then_inc(const_s, 1)
            nc.gpsimd.memset(oneb[:], 1.0).then_inc(const_s, 1)
            nc.gpsimd.memset(ones[:], 1.0).then_inc(const_s, 1)
            nc.gpsimd.iota(weight[:], [[-1, E]], base=E, channel_multiplier=0,
                           allow_small_or_imprecise_dtypes=True).then_inc(const_s, 1)
            nc.gpsimd.iota(steps[:], [[P, NT]], base=0, channel_multiplier=0,
                           allow_small_or_imprecise_dtypes=True).then_inc(const_s, 1)
            ch.link(nc.gpsimd.iota(slotno[:], [[1, SLOTS]], base=0, channel_multiplier=0,
                                   allow_small_or_imprecise_dtypes=True))
            for q in range(LN):
                norm_scale(nc, pool, ch, mv, rstd, half, q, stat_s, scale_s)
            nc.gpsimd.iota(xn[:, :, P].bitcast(U32), [[P, NT]], base=0, channel_multiplier=1).then_inc(fill_s, 1)
            nc.gpsimd.memset(xn[:, :, P + 2:], 0.0).then_inc(fill_s, 1)
            pool.wait_ge(fill_s, 2)
            pool.wait_ge(slot_s, 1)
            for t in range(NT):
                nc.gpsimd.indirect_dma_start(out=xs_dram, out_offset=bass.IndirectOffsetOnAxis(ap=slot_idx[:, t:t + 1], axis=0),
                                             in_=xn[:, t, :], in_offset=None).then_inc(sorted_s, 16)
            pool.wait_ge(sorted_s, 16 * NT)

        @block.scalar
        def _(act):
            for b in range(B):
                act.wait_ge(tr_s, b + 1)
                if b >= 2:
                    act.wait_ge(logit_s, b - 1)
                nc.scalar.activation(xT[:, b % 2, :], trp[:, b % 2, :], ACT.Copy).then_inc(xT_s, 1)
            act.wait_ge(shift_s, 1)
            nc.scalar.activation(ex[:], ex[:], ACT.Exp).then_inc(exp_s, 1)

        @block.tensor
        def _(pe):
            pe.wait_ge(r_in, 32)
            for b in range(B + 1):
                if b < B:
                    pe.wait_ge(xn_s, b + 1)
                    if b >= 2:
                        pe.wait_ge(xT_s, b - 1)
                    for t in range(TPB):
                        tr = nc.tensor.transpose(trp[:, b % 2, P * t:P * t + P], xn[:, TPB * b + t, 0:P], ident[:])
                    tr.then_inc(tr_s, 1)
                if b:
                    pe.wait_ge(xT_s, b)
                    for t in range(TPB):
                        mm = nc.tensor.matmul(logit_ps[:, TPB * (b - 1) + t, :], xT[:, (b - 1) % 2, P * t:P * t + P],
                                              rw[:], start=True, stop=True)
                    mm.then_inc(logit_s, 1)
            pe.wait_ge(hot_s, 1)
            pe.wait_ge(const_s, 2)
            h = hotb[:].rearrange("p e t -> p (e t)")
            nc.tensor.matmul(cnt_ps[:, 0, 0:E * NT], before[:], h, start=True, stop=True).then_inc(cnt_s, 1)
            nc.tensor.matmul(cnt_ps[:, 1, 0:E * NT], oneb[:], h, start=True, stop=True).then_inc(cnt_s, 1)

        @block.vector
        def _(dve):
            V = nc.vector
            ch = Chain(dve, vch)
            normalise_tokens(nc, dve, ch, X, xn, stats, mv, rstd, stat_s, scale_s, xn_s)
            dve.wait_ge(logit_s, B)
            dve.wait_ge(r_in, 32)
            dve.wait_ge(const_s, 5)
            wide = [P, NT, E]
            ch.link(V.tensor_tensor(logit[:], logit_ps[:], rb[:].unsqueeze(1).broadcast_to(wide), ALU.add))
            ch.link(V.tensor_reduce(best[:], logit[:], AX.X, ALU.max))
            top = best[:].unsqueeze(2).broadcast_to(wide)
            V.tensor_tensor(ex[:], logit[:], top, ALU.subtract).then_inc(shift_s, 1)
            ch.link(V.tensor_tensor(eq[:], logit[:], top, ALU.is_equal))
            ch.link(V.tensor_tensor(cand[:], eq[:], weight[:].unsqueeze(1).broadcast_to(wide), ALU.mult))
            ch.link(V.tensor_reduce(total[:], cand[:], AX.X, ALU.max))
            ch.link(V.tensor_tensor(hot[:].rearrange("p e t -> p t e"), cand[:], total[:].unsqueeze(2).broadcast_to(wide),
                                    ALU.is_equal))
            V.tensor_copy(hotb[:], hot[:]).then_inc(hot_s, 1)
            dve.wait_ge(exp_s, 1)
            ch.link(V.tensor_reduce(total[:], ex[:], AX.X, ALU.add))
            ch.link(V.reciprocal(pmax[:], total[:]))
            ch.link(V.tensor_copy(xn[:, :, P + 1], pmax[:]))
            dve.wait_ge(cnt_s, 2)
            ch.link(V.tensor_copy(tot[:].rearrange("p e t -> p (e t)"), cnt_ps[:, 1, 0:E * NT]))
            ch.link(V.tensor_tensor_scan(cum[:].rearrange("p e t -> p (e t)"), ones[:],
                                         tot[:].rearrange("p e t -> p (e t)"), 0.0, ALU.mult, ALU.add))
            ch.link(V.tensor_reduce(count[:], tot[:], AX.X, ALU.add))
            ch.link(V.tensor_tensor(place[:], count[:].unsqueeze(2).broadcast_to([P, E, NT]),
                                    steps[:].unsqueeze(1).broadcast_to([P, E, NT]), ALU.is_gt))
            ch.link(V.tensor_reduce(tiles[:], place[:], AX.X, ALU.add))
            ch.link(V.tensor_tensor_scan(end[:], ones[:, 0:E], tiles[:], 0.0, ALU.mult, ALU.add))
            ch.link(V.tensor_tensor(off[:], end[:], tiles[:], ALU.subtract))
            ch.link(V.tensor_scalar(off[:], off[:], float(P), None, ALU.mult))
            ch.link(V.tensor_tensor(off[:], off[:], cum[:, :, NT - 1], ALU.subtract))
            ch.link(V.tensor_tensor(off[:], off[:], count[:], ALU.add))
            ch.link(V.tensor_tensor(place[:], cum[:], tot[:], ALU.subtract))
            ch.link(V.tensor_tensor(place[:], place[:], off[:].unsqueeze(2).broadcast_to([P, E, NT]), ALU.add))
            ch.link(V.tensor_tensor(place[:].rearrange("p e t -> p (e t)"), cnt_ps[:, 0, 0:E * NT],
                                    place[:].rearrange("p e t -> p (e t)"), ALU.add))
            ch.link(V.tensor_tensor(place[:], place[:], hot[:], ALU.mult))
            ch.link(V.tensor_reduce(slotf[:], place[:].rearrange("p e t -> p t e"), AX.X, ALU.add))
            V.tensor_copy(slot_idx[:], slotf[:]).then_inc(slot_s, 1)
            dve.wait_ge(pch, 2)
            ch.link(V.tensor_tensor(ended[:], slotno[:].unsqueeze(2).broadcast_to([1, SLOTS, E]),
                                    end[0:1, :].unsqueeze(1).broadcast_to([1, SLOTS, E]), ALU.is_ge))
            ch.link(V.tensor_reduce(past[:], ended[:], AX.X, ALU.add))
            ch.link(V.tensor_scalar(past[:], past[:], float(E - 1), None, ALU.min))
            ch.link(V.tensor_copy(expert[:], past[:]))


def build_experts(nc, name, ident, w1s, w2s, expert, xs_dram, y_dram):
    R = 8
    Q = 4
    with ExitStack() as ctx:
        def sb(n, shape, dt=F32):
            return ctx.enter_context(nc.sbuf_tensor(f"{name}_{n}", shape, dt))

        sems = []

        def sem(n):
            sems.append(nc.alloc_semaphore(f"{name}_{n}"))
            return sems[-1]

        ctx.callback(nc.all_engine_barrier)
        ctx.callback(nc.clear_and_free_semaphores, sems)

        up = ctx.enter_context(nc.psum_tensor(f"{name}_up", [P, 2, 2, FFN], F32))
        hid_ps = ctx.enter_context(nc.psum_tensor(f"{name}_hid_ps", [P, KF, P], F32))
        xT_ps = ctx.enter_context(nc.psum_tensor(f"{name}_xT_ps", [P, 512], F32))
        y_ps = ctx.enter_context(nc.psum_tensor(f"{name}_y_ps", [P, 2, 512], F32))
        xt, xT = sb("xt", [P, R, ROW]), sb("xTs", [P, R, P])
        sa, hg, hgT, yo = sb("sa", [P, Q, FFN]), sb("hg", [P, Q, FFN]), sb("hgT", [P, Q, KF, P]), sb("yo", [P, R, P])
        loaded = [sem(f"tile_loaded{u}") for u in range(R)]
        stored = [sem(f"tile_stored{u}") for u in range(R)]
        tr_s, xT_s, a_s, g_s, silu_s, hg_s, hgtr_s, hgT_s, y_s, yo_s, pe_go, pool_go = (sem(n) for n in (
            "x_transposed", "xT_ready", "a_psum", "g_psum", "silu_done", "hidden_ready", "hidden_transposed",
            "hiddenT_ready", "y_psum", "y_ready", "pe_goes", "pool_goes"))
        block = ctx.enter_context(nc.Block())
        xs_v = xs_dram.rearrange("(s p) d -> s p d", p=P)

        def steps(engine, step):
            for i in (0, 1):
                for u in range(R):
                    step(i, u)
            with engine.Fori(2, (SLOTS + 1) // R - 1) as i:
                for u in range(R):
                    step(i, u)
            for u in range(R):
                step((SLOTS + 1) // R - 1, u)
            step((SLOTS + 1) // R, 0)

        def has(s, lo, hi=SLOTS):
            return not isinstance(s, int) or lo <= s < hi

        @block.sync
        def _(sp):
            def load(i, u):
                s = i * R + u
                if has(s, 0):
                    if has(s, R):
                        sp.wait_ge(stored[u], i * 16)
                    sp.dma_start(xt[:, u, :], xs_v[bass.ds(s, 1)].rearrange("a p d -> p (a d)")).then_inc(loaded[u], 16)
            steps(sp, load)

        @block.gpsimd
        def _(pool):
            def store(i, u):
                s = i * R + u
                if has(s, 0):
                    pool.wait_ge(yo_s, s + 1)
                    pool.sem_inc(pool_go, 1)
                    nc.gpsimd.indirect_dma_start(
                        out=y_dram, out_offset=bass.IndirectOffsetOnAxis(ap=xt[:, u, P:P + 1].bitcast(U32), axis=0),
                        in_=yo[:, u, :], in_offset=None).then_inc(stored[u], 16)
            steps(pool, store)
            for u in range(R):
                pool.wait_ge(stored[u], 16 * ((SLOTS - 1 - u) // R + 1))

        @block.scalar
        def _(act):
            def step(i, u):
                s, v = i * R + u, (u - 1) % Q
                if has(s, 0):
                    act.wait_ge(a_s, s + 1)
                    if has(s, Q):
                        act.wait_ge(hg_s, s - Q + 1)
                    nc.scalar.activation(sa[:, u % Q, :], up[:, u % 2, 0, :], ACT.Silu).then_inc(silu_s, 1)
                if has(s, 1, SLOTS + 1):
                    act.wait_ge(hgtr_s, s)
                    if has(s, Q + 1, SLOTS + 1):
                        act.wait_ge(y_s, s - Q)
                    nc.scalar.activation(hgT[:, v], hid_ps[:], ACT.Copy).then_inc(hgT_s, 1)
            steps(act, step)

        @block.vector
        def _(dve):
            def step(i, u):
                s, v, n = i * R + u, (u - 2) % R, (u + 1) % R
                if has(s, 0):
                    dve.wait_ge(g_s, s + 1)
                    dve.wait_ge(silu_s, s + 1)
                    if has(s, Q):
                        dve.wait_ge(hgtr_s, s - Q + 1)
                    nc.vector.tensor_tensor(hg[:, u % Q, :], up[:, u % 2, 1, :], sa[:, u % Q, :], ALU.mult).then_inc(hg_s, 1)
                if has(s, 0, SLOTS - 1):
                    dve.wait_ge(tr_s, s + 2)
                    if has(s, R - 1, SLOTS - 1):
                        dve.wait_ge(g_s, s - R + 2)
                    nc.vector.tensor_copy(xT[:, n, :], xT_ps[:, 0:P]).then_inc(xT_s, 1)
                if has(s, 2, SLOTS + 2):
                    dve.wait_ge(y_s, s - 1)
                    if has(s, R + 2, SLOTS + 2):
                        dve.wait_ge(stored[v], (i - 1) * 16 if u < 2 else i * 16)
                    nc.vector.tensor_scalar(yo[:, v, :], y_ps[:, v % 2, 0:P], xt[:, v, P + 1:P + 2], None, ALU.mult)\
                        .then_inc(yo_s, 1)
            dve.wait_ge(tr_s, 1)
            nc.vector.tensor_copy(xT[:, 0, :], xT_ps[:, 0:P]).then_inc(xT_s, 1)
            steps(dve, step)

        @block.tensor
        def _(pe):
            def transpose_x(u):
                return nc.tensor.transpose(xT_ps[:, 0:P], xt[:, u, 0:P], ident[:])

            def slices(w, u, lo):
                e = pe.snap(number[u], min_val=0, max_val=E - 1)
                return [w[:, bass.ds(e, 1)].rearrange("p a k n -> p (a k) n")[:, k, :] for k in lo]

            number = [pe.alloc_register(f"{name}_expert{u}") for u in range(R)]

            def step(i, u):
                s, d, n = i * R + u, (u - 2) % R, (u + 1) % R
                if has(s, 0):
                    pe.reg_load(number[u], expert[0:1, bass.ds(s, 1)])
                    wa, wg = slices(w1s, u, (0, 1))
                    pe.wait_ge(xT_s, s + 1)
                    if has(s, 2):
                        pe.wait_ge(hg_s, s - 1)
                        pe.sem_inc(pe_go, 1)
                    nc.tensor.matmul(up[:, u % 2, 0, :], xT[:, u, :], wa, start=True, stop=True).then_inc(a_s, 1)
                if has(s, 1, SLOTS + 1):
                    pe.wait_ge(hg_s, s)
                    if has(s, 2, SLOTS + 1):
                        pe.wait_ge(hgT_s, s - 1)
                    pe.sem_inc(pe_go, 1)
                    for k in range(KF):
                        tr = nc.tensor.transpose(hid_ps[:, k, :], hg[:, (u - 1) % Q, P * k:P * k + P], ident[:])
                    tr.then_inc(hgtr_s, 1)
                if has(s, 0):
                    nc.tensor.matmul(up[:, u % 2, 1, :], xT[:, u, :], wg, start=True, stop=True).then_inc(g_s, 1)
                if has(s, 0, SLOTS - 1):
                    pe.wait_ge(loaded[n], (i + (u == R - 1)) * 16 + 16)
                    pe.wait_ge(xT_s, s + 1)
                    pe.sem_inc(pe_go, 1)
                    transpose_x(n).then_inc(tr_s, 1)
                if has(s, 2, SLOTS + 2):
                    wd = slices(w2s, d, range(KF))
                    pe.wait_ge(hgT_s, s - 1)
                    if has(s, 4, SLOTS + 2):
                        pe.wait_ge(yo_s, s - 3)
                    pe.sem_inc(pe_go, 1)
                    for k in range(KF):
                        mm = nc.tensor.matmul(y_ps[:, d % 2, 0:P], hgT[:, d % Q, k, :], wd[k], start=k == 0, stop=k == KF - 1)
                    mm.then_inc(y_s, 1)
            pe.wait_ge(loaded[0], 16)
            transpose_x(0).then_inc(tr_s, 1)
            steps(pe, step)


def build_combine(nc, name, X, yg, y_dram, out_tiles):
    Q = 8
    with ExitStack() as ctx:
        got = [ctx.enter_context(nc.semaphore(f"{name}_gathered{q}")) for q in range(NT // Q)]
        add_s, out_s = (ctx.enter_context(nc.semaphore(f"{name}_{n}")) for n in ("added", "out_stored"))
        block = ctx.enter_context(nc.Block())

        @block.sync
        def _(sp):
            for q in range(NT // Q):
                sp.dma_start(yg[:, Q * q:Q * q + Q, :],
                             y_dram[Q * P * q:Q * P * (q + 1), :].rearrange("(t p) d -> p t d", p=P)).then_inc(got[q], 16)
            for q in range(NT // Q):
                sp.wait_ge(add_s, q + 1)
                sp.dma_start(out_tiles[:, Q * q:Q * q + Q, :], X[:, Q * q:Q * q + Q, :]).then_inc(out_s, 16)
            sp.wait_ge(out_s, 16 * (NT // Q))

        @block.vector
        def _(dve):
            for q in range(NT // Q):
                dve.wait_ge(got[q], 16)
                x = X[:, Q * q:Q * q + Q, :]
                nc.vector.tensor_tensor(x, x, yg[:, Q * q:Q * q + Q, :], ALU.add).then_inc(add_s, 1)


def build_rwkv(nc, X, yg, y_dram, xn, ident, mv, rstd, stats, half, time_decay, time_first, mix_k, mix_v, mix_r,
               Wk_b, Wv_b, Wr_b, Wo_b):
    def batches(engine, body):
        for u in range(2):
            body(u, 0, u, True, False)
        with engine.Fori(1, B // 2 - 1) as i:
            for u in range(2):
                body(i * 2 + u, i, u, False, False)
        for u in range(2):
            body(B - 2 + u, B // 2 - 1, u, False, True)

    with ExitStack() as ctx:
        def sb(n, shape, dt=F32):
            return ctx.enter_context(nc.sbuf_tensor(f"rwkv_{n}", shape, dt))

        def sem(n):
            return ctx.enter_context(nc.semaphore(f"rwkv_{n}"))

        ps = ctx.enter_context(nc.psum_tensor("rwkv_ps", [P, 2, 3, T], F32))
        ops = ctx.enter_context(nc.psum_tensor("rwkv_out", [P, 2, T], F32))
        wraw = sb("wraw", [P, 4, P])
        wT = sb("wT", [P, 4, P])
        wcur, wold = sb("wcur", [P, 3, P]), sb("wold", [P, 3, P])
        mix, old = sb("mix", [P, 3]), sb("old", [P, 3])
        td, tf, lam = sb("td", [P, 1]), sb("tf", [P, 1]), sb("lam", [P, 1])
        etd, etf = sb("etd", [P, 1]), sb("etf", [P, 1])
        lamw, onew = sb("lamw", [P, T]), sb("onew", [P, T])
        xT = sb("xT", [P, B, 1 + T])
        kmin, kc, kv, fkv = (sb(n, [P, 2, T]) for n in ("kmin", "kc", "kv", "fkv"))
        er, er1, num, rd, o = (sb(n, [P, 2, T]) for n in ("er", "er1", "num", "rd", "o"))
        sk, sv = sb("sk", [P, 2, 1 + T]), sb("sv", [P, 2, 1 + T])
        dn, dr = sb("dn", [P, T]), sb("dr", [P, T])
        w_in, tr_s, wT_s, w_s, stat_s, scale_s, xn_s, xtr_s, xT_s = (sem(n) for n in (
            "loaded", "w_transposed", "wT_ready", "w_ready", "stats_done", "scales_done", "xn_ready", "x_transposed",
            "xT_ready"))
        got = [sem(f"gathered{q}") for q in range(LN)]
        k_s, v_s, r_s, kmin_s, kc_s, er_s, er1_s, kv_s, fkv_s, sv_s, num_s, rd_s, o_s, out_s, add_s, x_s = (
            sem(n) for n in ("k_psum", "v_psum", "r_psum", "k_clamped", "k_exp", "r_exp", "r_exp_plus_one", "kv_ready",
                             "first_kv", "kv_scanned", "numerator", "reciprocal", "o_ready", "out_psum", "added",
                             "experts_added"))
        pch, vch, ach, lam_s = (sem(n) for n in ("pool_steps", "dve_steps", "act_steps", "lam_ready"))
        pool_go = sem("pool_goes")
        block = ctx.enter_context(nc.Block())

        @block.sync
        def _(sp):
            for q in range(LN):
                sp.dma_start(yg[:, LNT * q:LNT * q + LNT, :],
                             y_dram[LNT * P * q:LNT * P * (q + 1), :].rearrange("(t p) d -> p t d", p=P)).then_inc(got[q], 16)
            for k, w in enumerate((Wk_b, Wv_b, Wr_b, Wo_b)):
                sp.dma_start(wraw[:, k, :], w).then_inc(w_in, 16)
            for k, m in enumerate((mix_k, mix_v, mix_r)):
                sp.dma_start(mix[:, k:k + 1], m.rearrange("a b c -> c (a b)")).then_inc(w_in, 16)
            sp.dma_start(td[:], time_decay).then_inc(w_in, 16)
            sp.dma_start(tf[:], time_first).then_inc(w_in, 16)

        @block.gpsimd
        def _(pool):
            ch = Chain(pool, pch)
            for q in range(LN + 1):
                if q < LN:
                    pool.wait_ge(got[q], 16)
                    x = X[:, LNT * q:LNT * q + LNT, :]
                    nc.gpsimd.tensor_tensor(x, x, yg[:, LNT * q:LNT * q + LNT, :], ALU.add).then_inc(x_s, 1)
                if q:
                    norm_scale(nc, pool, ch, mv, rstd, half, q - 1, stat_s, scale_s)

            def body(b, k, u, first, last):
                pool.wait_ge(fkv_s, b + 1)
                pool.wait_ge(sv_s, b + 1)
                pool.sem_inc(pool_go, 1)
                nc.gpsimd.tensor_tensor(num[:, u, :], fkv[:, u, :], sv[:, u, 0:T], ALU.add).then_inc(num_s, 1)
                pool.wait_ge(num_s, b + 1)
                pool.wait_ge(rd_s, b + 1)
                if not first:
                    pool.wait_ge(out_s, b - 1)
                pool.sem_inc(pool_go, 1)
                nc.gpsimd.tensor_tensor(o[:, u, :], num[:, u, :], rd[:, u, :], ALU.mult).then_inc(o_s, 1)

            batches(pool, body)

        @block.scalar
        def _(act):
            ch = Chain(act, ach)
            act.wait_ge(w_in, 16 * 9)
            ch.link(nc.scalar.activation(etd[:], td[:], ACT.Exp))
            nc.scalar.activation(etf[:], tf[:], ACT.Exp).then_inc(lam_s, 1)
            nc.scalar.activation(lam[:], etd[:], ACT.Exp, scale=-1.0).then_inc(lam_s, 1)
            for b in range(B):
                act.wait_ge(xtr_s, b + 1)
                nc.scalar.activation(xT[:, b, 1:], ops[:, b % 2, :], ACT.Copy).then_inc(xT_s, 1)
            act.wait_ge(lam_s, 2)

            def body(b, k, u, first, last):
                act.wait_ge(kmin_s, b + 1)
                if not first:
                    act.wait_ge(rd_s, b - 1)
                nc.scalar.activation(kc[:, u, :], kmin[:, u, :], ACT.Exp).then_inc(kc_s, 1)
                act.wait_ge(r_s, b + 1)
                nc.scalar.activation(er[:, u, :], ps[:, u, 2, :], ACT.Exp, scale=-1.0).then_inc(er_s, 1)
                act.wait_ge(er_s, b + 1)
                nc.scalar.activation(er1[:, u, :], er[:, u, :], ACT.Copy, bias=1.0).then_inc(er1_s, 1)
                act.wait_ge(kv_s, b + 1)
                if not first:
                    act.wait_ge(num_s, b - 1)
                nc.scalar.activation(fkv[:, u, :], kv[:, u, :], ACT.Copy, scale=etf[:]).then_inc(fkv_s, 1)

            batches(act, body)

        @block.tensor
        def _(pe):
            pe.wait_ge(w_in, 16 * 9)
            for k in range(4):
                tr = nc.tensor.transpose(ps[:, 0, 0, P * k:P * k + P], wraw[:, k, :], ident[:])
            tr.then_inc(tr_s, 1)
            for b in range(B):
                pe.wait_ge(xn_s, b + 1)
                if b >= 2:
                    pe.wait_ge(xT_s, b - 1)
                for t in range(TPB):
                    tr = nc.tensor.transpose(ops[:, b % 2, P * t:P * t + P], xn[:, TPB * b + t, 0:P], ident[:])
                tr.then_inc(xtr_s, 1)

            def products(b, u):
                for k, s in enumerate((k_s, v_s, r_s)):
                    cur = xT[:, bass.ds(b, 1), 1:].rearrange("p a t -> p (a t)")
                    prev = xT[:, bass.ds(b, 1), 0:T].rearrange("p a t -> p (a t)")
                    nc.tensor.matmul(ps[:, u, k, :], wcur[:, k, :], cur, start=True, stop=False)
                    nc.tensor.matmul(ps[:, u, k, :], wold[:, k, :], prev, start=False, stop=True).then_inc(s, 1)

            def body(b, k, u, first, last):
                if not (last and u == 1):
                    if not (first and u == 0):
                        pe.wait_ge(kv_s, b)
                        pe.wait_ge(er_s, b)
                    products(b + 1, 1 - u)
                pe.wait_ge(o_s, b + 1)
                if not first:
                    pe.wait_ge(add_s, b - 1)
                for t in range(TPB):
                    mm = nc.tensor.matmul(ops[:, u, P * t:P * t + P], o[:, u, P * t:P * t + P], wT[:, 3, :],
                                          start=True, stop=True)
                mm.then_inc(out_s, 1)

            pe.wait_ge(w_s, 1)
            pe.wait_ge(xT_s, B)
            products(0, 0)
            batches(pe, body)

        @block.vector
        def _(dve):
            V = nc.vector
            ch = Chain(dve, vch)
            V.memset(xT[:, :, 0], 0.0)
            V.memset(sk[:, :, 0], 0.0)
            V.memset(sv[:, :, 0], 0.0)
            V.memset(onew[:], 1.0)
            normalise_tokens(nc, dve, ch, X, xn, stats, mv, rstd, stat_s, scale_s, xn_s,
                             lambda q: dve.wait_ge(x_s, q + 1))
            dve.wait_ge(w_in, 16 * 9)
            ch.link(V.tensor_scalar(old[:], mix[:], -1.0, 1.0, ALU.mult, ALU.add))
            dve.wait_ge(tr_s, 1)
            ch.link(V.tensor_copy(wT[:].rearrange("p k n -> p (k n)"), ps[:, 0, 0, :]))
            for k in range(3):
                V.tensor_scalar(wcur[:, k, :], wT[:, k, :], mix[:, k:k + 1], None, ALU.mult)
                w = V.tensor_scalar(wold[:, k, :], wT[:, k, :], old[:, k:k + 1], None, ALU.mult)
            w.then_inc(w_s, 1)
            dve.wait_ge(lam_s, 2)
            ch.link(V.tensor_scalar(lamw[:], onew[:], lam[:], None, ALU.mult))
            done = ch.n
            CHAINED = 3

            def add_out(b, u):
                dve.wait_ge(out_s, b + 1)
                x = X[:, bass.ds(b * TPB, TPB), :].rearrange("p t d -> p (t d)")
                V.tensor_tensor(x, ops[:, u, :], x, ALU.add).then_inc(add_s, 1)

            def body(b, k, u, first, last):
                ch.at(done + b * CHAINED)
                dve.wait_ge(k_s, b + 1)
                V.tensor_scalar(kmin[:, u, :], ps[:, u, 0, :], K_CLAMP, None, ALU.min).then_inc(kmin_s, 1)
                if not first:
                    add_out(b - 2, u)
                    dve.wait_ge(num_s, b - 1)
                dve.wait_ge(kc_s, b + 1)
                dve.wait_ge(v_s, b + 1)
                V.tensor_tensor(kv[:, u, :], ps[:, u, 1, :], kc[:, u, :], ALU.mult).then_inc(kv_s, 1)
                ch.link(V.tensor_tensor_scan(sk[:, u, 1:], lamw[:], kc[:, u, :], 0.0, ALU.mult, ALU.add))
                dve.wait_ge(kv_s, b + 1)
                V.tensor_tensor_scan(sv[:, u, 1:], lamw[:], kv[:, u, :], 0.0, ALU.mult, ALU.add).then_inc(sv_s, 1)
                ch.link(V.scalar_tensor_tensor(dn[:], kc[:, u, :], etf[:], sk[:, u, 0:T], ALU.mult, ALU.add))
                dve.wait_ge(er1_s, b + 1)
                ch.link(V.scalar_tensor_tensor(dr[:], dn[:], EPS_RWKV, er1[:, u, :], ALU.add, ALU.mult))
                if not first:
                    dve.wait_ge(o_s, b - 1)
                V.reciprocal(rd[:, u, :], dr[:]).then_inc(rd_s, 1)

            batches(dve, body)
            for u in range(2):
                add_out(B - 2 + u, u)


def build_prep(nc, x_tiles, norm_w, Wq, Wk, Wv, Wqf, Wkf, X, ident, identb, mv, rstd, stats, half,
               parts_dram, v_dram, xs_dram, operands, maskq, maskk):
    def batches(engine, body):
        for u in range(2):
            body(u, 0, u, True, False)
        with engine.Fori(1, B // 2 - 1) as i:
            for u in range(2):
                body(i * 2 + u, i, u, False, False)
        for u in range(2):
            body(B - 2 + u, B // 2 - 1, u, False, True)

    with ExitStack() as ctx:
        def sb(name, shape, dt=F32):
            return ctx.enter_context(nc.sbuf_tensor(name, shape, dt))

        def sem(name):
            return ctx.enter_context(nc.semaphore(name))

        ps = ctx.enter_context(nc.psum_tensor("prep_ps", [P, 8, 512], F32))
        wq, wk, wv = sb("wq", [P, P]), sb("wk", [P, P]), sb("wv", [P, P])
        nw = sb("nw", [P, 1])
        wqfT, wkfT = sb("wqfT", [FEAT, HD]), sb("wkfT", [FEAT, HD])
        qrep, krep = sb("qrep", [FEAT, HD, H]), sb("krep", [FEAT, HD, H])
        wqp, wkp = sb("wqp", [P, P]), sb("wkp", [P, P])
        same = sb("same", [P, H])
        feat = sb("feat", [P, P])
        r2 = sb("r2", [P, NT])
        t1 = sb("t1", [P, NT])
        hs = sb("hs", [P, NT])
        hn = sb("hn", [P, 2, TPB, P])
        xl = sb("xl", [P, NT, P])
        hT = sb("hT", [P, 2, WIN + T])
        kT = sb("kT", [P, 2, T])
        parts = sb("parts", [P, 2, 3, PARTS, T], BF16)
        rem = sb("rem", [P, 3, T])
        vs = sb("vs", [P, 2, NW, P])
        empty = sb("empty", [P, SLOTS, ROW])
        empty_s, cleared = sem("empty_tile"), sem("slots_cleared")
        x_in_s, w_in_s = sem("x_loaded"), sem("w_loaded")
        const_s, pch, vch = sem("consts"), sem("pool_steps"), sem("dve_steps")
        stat_s, scale_s = sem("stats_done"), sem("scales_done")
        feat_ps, feat_s = sem("feat_psum"), sem("feat_done")
        hn_s, hnT_s, hT_s = sem("hn_ready"), sem("hnT_psum"), sem("hT_ready")
        q_s, k_s, kT_s, k2_s, v_s = (sem("q_psum"), sem("k_psum"), sem("kT_ready"), sem("k2_psum"),
                                     sem("v_psum"))
        part1_s, split_s, vs_s = sem("first_part"), sem("split_done"), sem("v_ready")
        stored = [sem("stored_even"), sem("stored_odd")]
        pads_s, loaded_s = sem("pads_ready"), sem("first_loaded")
        sp_go, pe_go = sem("prep_sp_goes"), sem("prep_pe_goes")
        qs, ks, k2s, v = operands
        block = ctx.enter_context(nc.Block())

        @block.sync
        def _(sp):
            for q in range(4):
                sp.dma_start(X[:, 8 * q:8 * q + 8, :], x_tiles[:, 8 * q:8 * q + 8, :]).then_inc(x_in_s, 16)
            for dst, src in ((wq, Wq), (wk, Wk), (wv, Wv)):
                sp.dma_start(dst[:], src).then_inc(w_in_s, 16)
            sp.dma_start(nw[:], norm_w.rearrange("(p a) -> p a", a=1)).then_inc(w_in_s, 16)
            with nc.allow_non_contiguous_dma("128 numbers"):
                sp.dma_start(wqfT[:], Wqf.rearrange("d f -> f d")).then_inc(w_in_s, 16)
                sp.dma_start(wkfT[:], Wkf.rearrange("d f -> f d")).then_inc(w_in_s, 16)
            sp.wait_ge(empty_s, 1)
            for xs in xs_dram.values():
                sp.dma_start(xs.rearrange("(s p) d -> p s d", p=P), empty[:]).then_inc(cleared, 16)

            def store(i):
                for u in range(2):
                    b = i * 2 + u
                    for x, n in enumerate((1, 0, 2)):
                        sp.wait_ge(split_s, b * 3 + x + 1)
                        sp.sem_inc(sp_go, 1)
                        sp.dma_start(parts_dram[n, bass.ds(b, 1)].rearrange("b c p t -> p (b c) t"), parts[:, u, n])\
                            .then_inc(stored[u], 16)
                    sp.wait_ge(vs_s, b * 2 + 2)
                    sp.sem_inc(sp_go, 1)
                    sp.dma_start(v_dram[bass.ds(b, 1)].rearrange("b p w n -> p (b w) n"), vs[:, u]).then_inc(stored[u], 16)

            store(0)
            sp.wait_ge(stored[0], 16 * 4)
            sp.wait_ge(pads_s, 1)
            load_operands(sp, operands, parts_dram, v_dram, 0, 0, loaded_s)
            with sp.Fori(1, B // 2) as i:
                store(i)
            for u in range(2):
                sp.wait_ge(stored[u], 16 * 4 * B // 2)
            sp.wait_ge(cleared, 32)
            sp.wait_ge(loaded_s, 16 * LOADS)

        @block.gpsimd
        def _(pool):
            ch = Chain(pool, pch)
            nc.gpsimd.memset(half[:], -0.5)
            nc.gpsimd.memset(hT[:, :, 0:WIN], 0.0)
            ch.link(nc.gpsimd.memset(same[:], 0.0))
            ch.link(nc.gpsimd.memset(ident[:], 0.0))
            nc.gpsimd.affine_select(out=ident[:], in_=ident[:], compare_op=ALU.not_equal, fill=1.0,
                                    base=0, pattern=[[-1, P]], channel_multiplier=1)
            for d in range(HD):
                ch.link(nc.gpsimd.affine_select(out=same[:], in_=same[:], compare_op=ALU.not_equal, fill=0.5,
                                                base=-H * d, pattern=[[-1, H]], channel_multiplier=1))
            nc.gpsimd.tensor_copy(identb[:], ident[:]).then_inc(const_s, 1)
            ch.link(nc.gpsimd.memset(empty[:], 0.0))
            nc.gpsimd.iota(empty[:, :, P].bitcast(U32), [[P, SLOTS]], base=NT * P, channel_multiplier=1).then_inc(empty_s, 1)
            pool.wait_ge(stat_s, 1)
            ch.link(nc.gpsimd.tensor_scalar(t1[:], mv[:, :, 1], EPS_LN, None, ALU.add))
            ch.link(nc.gpsimd.tensor_tensor(rstd[:], t1[:], half[:], ALU.pow))
            ch.link(nc.gpsimd.tensor_tensor(t1[:], rstd[:], rstd[:], ALU.mult))
            ch.link(nc.gpsimd.tensor_tensor(t1[:], t1[:], mv[:, :, 1], ALU.mult))
            ch.link(nc.gpsimd.tensor_scalar(t1[:], t1[:], EPS_RMS, None, ALU.add))
            ch.link(nc.gpsimd.tensor_tensor(r2[:], t1[:], half[:], ALU.pow))
            nc.gpsimd.tensor_tensor(hs[:], rstd[:], r2[:], ALU.mult).then_inc(scale_s, 1)
            for u in range(2):
                ch.link(nc.gpsimd.memset(qs[u][:], 0.0))
                ch.link(nc.gpsimd.memset(ks[u][0:BIAS, 0:WIN], 0.0))
                ch.link(nc.gpsimd.memset(ks[u][BIAS:SROWS, :], 1.0))
            pool.sem_inc(pads_s, 1)
            ch.link(nc.gpsimd.memset(maskq[:], 0.0))
            ch.link(nc.gpsimd.memset(maskk[:], 0.0))
            for lo in (0, WIN):
                m = maskq[lo:lo + WIN, :, :]
                ch.link(nc.gpsimd.affine_select(out=m, in_=m, compare_op=ALU.is_ge, fill=NEG, base=0,
                                                pattern=[[0, NW], [1, P]], channel_multiplier=-1))
                ch.link(nc.gpsimd.affine_select(out=m, in_=m, compare_op=ALU.is_ge, fill=NEG, base=WIN,
                                                pattern=[[0, NW], [-1, P]], channel_multiplier=1))
            ch.link(nc.gpsimd.affine_select(out=maskk[:], in_=maskk[:], compare_op=ALU.is_ge, fill=NEG, base=0,
                                            pattern=[[0, NW * 2], [-1, WIN]], channel_multiplier=1))
            ch.link(nc.gpsimd.affine_select(out=maskk[:], in_=maskk[:], compare_op=ALU.is_ge, fill=NEG, base=WIN,
                                            pattern=[[0, NW * 2], [1, WIN]], channel_multiplier=-1))
            ch.link(nc.gpsimd.memset(maskq[:, 0, 0:WIN], NEG))
            ch.link(nc.gpsimd.memset(maskk[0:WIN, 0:2, :], NEG))
            ch.link(nc.gpsimd.tensor_tensor(xl[:], X[:], mv[:, :, 0:1].broadcast_to([P, NT, P]), ALU.subtract))
            ch.link(nc.gpsimd.tensor_tensor(xl[:], xl[:], rstd[:].unsqueeze(2).broadcast_to([P, NT, P]), ALU.mult))
            pool.wait_ge(hn_s, B)
            nc.gpsimd.tensor_tensor(X[:], X[:], xl[:], ALU.add)

        @block.scalar
        def _(act):
            def transposed(b, u):
                act.wait_ge(hnT_s, b + 1)
                nc.scalar.activation(hT[:, u, WIN:], ps[:, 0, :], ACT.Copy).then_inc(hT_s, 1)

            def body(b, k, u, first, last):
                act.wait_ge(k_s, b + 1)
                nc.scalar.activation(kT[:, u, :], ps[:, 2, :], ACT.Copy).then_inc(kT_s, 1)
                if not first:
                    act.wait_ge(stored[u], k * (16 * 4))
                nc.scalar.activation(parts[:, u, 1, 0, :], ps[:, 2, :], ACT.Copy).then_inc(part1_s, 1)
                act.wait_ge(q_s, b + 1)
                nc.scalar.activation(parts[:, u, 0, 0, :], ps[:, 1, :], ACT.Copy).then_inc(part1_s, 1)
                if not (last and u == 1):
                    transposed(b + 1, 1 - u)
                act.wait_ge(k2_s, b + 1)
                nc.scalar.activation(parts[:, u, 2, 0, :], ps[:, 3, :], ACT.Copy).then_inc(part1_s, 1)
                for q in range(2):
                    act.wait_ge(v_s, b * 2 + q + 1)
                    nc.scalar.activation(vs[:, u, 4 * q:4 * q + 4, :], ps[:, 4 + q, :], ACT.Copy).then_inc(vs_s, 1)

            transposed(0, 0)
            batches(act, body)

        @block.vector
        def _(dve):
            ch = Chain(dve, vch)
            dve.wait_ge(x_in_s, 64)
            layernorm_stats(nc, ch, X, stats, mv).then_inc(stat_s, 1)
            dve.wait_ge(w_in_s, 96)
            for dst, w in ((wqp, wq), (wkp, wk)):
                nc.vector.tensor_scalar(dst[:].rearrange("p (d h) -> p h d", h=H), w[:].rearrange("p (h d) -> p h d", d=HD),
                                        nw[:], None, ALU.mult)
            nc.vector.tensor_scalar(wv[:], wv[:], nw[:], None, ALU.mult)
            nc.vector.tensor_copy(qrep[:], wqfT[:].unsqueeze(2).broadcast_to([FEAT, HD, H]))
            nc.vector.tensor_copy(krep[:], wkfT[:].unsqueeze(2).broadcast_to([FEAT, HD, H]))\
                .then_inc(feat_s, 1)
            dve.wait_ge(const_s, 1)
            dve.wait_ge(feat_ps, 1)
            nc.vector.tensor_tensor(feat[:].rearrange("p (d h) -> p d h", h=H), ps[:, 7, 0:P].rearrange("p (d h) -> p d h", h=H),
                                    same[:].unsqueeze(1).broadcast_to([P, HD, H]), ALU.mult).then_inc(feat_s, 1)
            dve.wait_ge(scale_s, 1)
            done = ch.n

            def normalise(b, u):
                for t in range(TPB):
                    k = b * TPB + t
                    h = nc.vector.tensor_scalar(hn[:, u, t, :], X[:, k, :], mv[:, k, 0:1], hs[:, bass.ds(k, 1)],
                                                ALU.subtract, ALU.mult)
                h.then_inc(hn_s, 1)

            def body(b, k, u, first, last):
                ch.at(done + b * 6)
                for x, n in enumerate((1, 0, 2)):
                    dve.wait_ge(part1_s, b * 3 + x + 1)
                    ch.link(nc.vector.tensor_tensor(rem[:, n, :], ps[:, 1 + n, :], parts[:, u, n, 0, :], ALU.subtract))
                    ch.link(nc.vector.tensor_copy(parts[:, u, n, 1, :], rem[:, n, :]))
                    nc.vector.tensor_tensor(parts[:, u, n, 2, :], rem[:, n, :], parts[:, u, n, 1, :],
                                            ALU.subtract).then_inc(split_s, 1)
                    if n == 0 and not last:
                        dve.wait_ge(hnT_s, b + 1)
                        normalise(b + 2, u)

            normalise(0, 0)
            normalise(1, 1)
            batches(dve, body)

        @block.tensor
        def _(pe):
            def transpose(b, u):
                pe.wait_ge(hn_s, b + 1)
                pe.sem_inc(pe_go, 1)
                for t in range(TPB):
                    tr = nc.tensor.transpose(ps[:, 0, P * t:P * t + P], hn[:, u, t, :], ident[:])
                tr.then_inc(hnT_s, 1)

            def body(b, k, u, first, last):
                first = first and u == 0
                pe.wait_ge(hT_s, b + 1)
                if not first:
                    pe.wait_ge(split_s, b * 3 - 2)
                nc.tensor.matmul(ps[:, 2, :], wkp[:], hT[:, u, WIN:], start=True, stop=True).then_inc(k_s, 1)
                if not first:
                    pe.wait_ge(split_s, b * 3 - 1)
                nc.tensor.matmul(ps[:, 1, :], wqp[:], hT[:, u, WIN:], start=True, stop=True).then_inc(q_s, 1)
                if not (last and u == 1):
                    transpose(b + 1, 1 - u)
                pe.wait_ge(kT_s, b + 1)
                if not first:
                    pe.wait_ge(split_s, b * 3)
                nc.tensor.matmul(ps[:, 3, :], feat[:], kT[:, u, :], start=True, stop=True).then_inc(k2_s, 1)
                for q in range(2):
                    if not first:
                        pe.wait_ge(vs_s, b * 2 - 1 + q)
                    for w in range(4):
                        lo = WIN * (4 * q + w)
                        mm = nc.tensor.matmul(ps[:, 4 + q, P * w:P * w + P], hT[:, u, lo:lo + P], wv[:],
                                              start=True, stop=True)
                    mm.then_inc(v_s, 1)

            pe.wait_ge(feat_s, 1)
            nc.tensor.matmul(ps[:, 7, 0:P], krep[:].rearrange("f d h -> f (d h)"), qrep[:].rearrange("f d h -> f (d h)"), start=True, stop=True).then_inc(feat_ps, 1)
            pe.wait_ge(feat_s, 2)
            pe.wait_ge(const_s, 1)
            transpose(0, 0)
            batches(pe, body)


_INS = ['L0_attn_a_x','L0_attn_a_norm_w','L0_attn_a_Wq','L0_attn_a_Wk','L0_attn_a_Wv','L0_attn_a_Wqf','L0_attn_a_Wkf','L0_attn_a_Wout','L0_attn_b_xk','L0_attn_b_xv','L0_attn_b_time_decay','L0_attn_b_time_first','L0_attn_b_time_mix_k','L0_attn_b_time_mix_v','L0_attn_b_time_mix_r','L0_attn_b_Wk','L0_attn_b_Wv','L0_attn_b_Wr','L0_attn_b_Wo','L0_ffn_router_w','L0_ffn_router_b','L0_ffn_w1','L0_ffn_w2']

def kernel(**inputs):
    import numpy as _np
    import concourse.bacc as _bacc
    from concourse import mybir as _mybir
    from concourse.bass_utils import run_bass_kernel_spmd as _run
    nc = _bacc.Bacc("TRN2", target_bir_lowering=False, num_devices=1)
    arrays, args = {}, []
    for name in _INS:
        a = _np.ascontiguousarray(inputs[name])
        arrays[f"in_{name}_dram"] = a
        args.append(nc.dram_tensor(f"in_{name}_dram", a.shape, _mybir.dt.from_np(a.dtype), kind="ExternalInput").ap())
    out = nc.dram_tensor("out_dram", (8, 512, 128), _mybir.dt.float32, kind="ExternalOutput").ap()
    build(nc, *args, out)
    r = _run(nc, [arrays], core_ids=[0])
    return r.results[0]["out_dram"]
```

```python
import concourse.bass as bass
from concourse import mybir
from contextlib import ExitStack

F32 = mybir.dt.float32
BF16 = mybir.dt.bfloat16
I32 = mybir.dt.int32
U32 = mybir.dt.uint32
ALU = mybir.AluOpType
ACT = mybir.ActivationFunctionType
AX = mybir.AxisListType

P = 128
B = 8
T = 512
TPB = T // P
NT = B * TPB
H = 16
HD = P // H
FEAT = 16
WIN = 64
NW = T // WIN
NP = H // 2
PARTS = 3
ROWS = 6 * HD
BIAS = 2 * ROWS
SROWS = BIAS + 2 * PARTS
NEG = -1.0e30
E = 8
FFN = 512
KF = FFN // P
ROW = P + 1
SLOTS = NT + E - 1
EPS_LN = 1e-5
EPS_RMS = 1e-6
EPS_LIN = 1e-6
EPS_RWKV = 1e-8
K_CLAMP = 60.0
PRODUCTS = [(0, 0), (0, 1), (0, 2), (1, 0), (1, 1), (2, 0)]


class Chain:

    def __init__(self, engine, sem):
        self.engine, self.sem, self.base, self.n = engine, sem, 0, 0

    def at(self, base):
        self.base, self.n = base, 0

    def link(self, ins):
        self.n += 1
        ins.then_inc(self.sem, 1)
        self.engine.wait_ge(self.sem, self.base + self.n)


LN = 4
LNT = NT // LN
assert LNT >= 2 * TPB


def part_stats(nc, ch, x, stats, mv, q):
    for t in range(LNT * q, LNT * q + LNT):
        st = nc.vector.bn_stats(stats[:, t, :], x[:, t, :])
    ch.link(st)
    for t in range(LNT * q, LNT * q + LNT):
        last = nc.vector.bn_aggr(mv[:, t, :], stats[:, t, :])
    return last


def build(nc, x_in, norm_w, Wq, Wk, Wv, Wqf, Wkf, Wout, xk_in, xv_in, time_decay, time_first,
          mix_k, mix_v, mix_r, Wk_b, Wv_b, Wr_b, Wo_b, router_w, router_b, w1, w2, out):
    x_tiles = x_in.rearrange("b (t p) d -> p (b t) d", p=P)
    out_tiles = out.rearrange("b (t p) d -> p (b t) d", p=P)
    parts_dram = nc.dram_tensor("parts_dram", (3, B, PARTS, P, T), BF16).ap()
    v_dram = nc.dram_tensor("v_dram", (B, P, NW, P), F32).ap()
    negmax_dram = nc.dram_tensor("negmax_dram", (B, 2, PARTS, NP * NW, WIN), BF16).ap()
    xn_dram = {name: nc.dram_tensor(f"{name}_xn_dram", (NT * P, ROW), F32).ap() for name in ("ffn1", "ffn2")}
    y_dram = nc.dram_tensor("y_dram", ((NT + SLOTS) * P, P), F32).ap()
    with ExitStack() as ctx:
        def sb(name, shape, dt=F32):
            return ctx.enter_context(nc.sbuf_tensor(name, shape, dt))

        X = sb("X", [P, NT, P])
        ident = sb("ident", [P, P])
        identb = sb("identb", [P, P], BF16)
        mv = sb("mv", [P, NT, 2])
        rstd = sb("rstd", [P, NT])
        stats = sb("stats", [P, NT, 6])
        half = sb("half", [P, NT])
        tokens = sb("tokens", [P, SLOTS, 2], U32)
        expert = sb("expert", [1, SLOTS], I32)
        pmax = sb("pmax", [P, NT])
        with ExitStack() as attention:
            def at(name, shape, dt=F32):
                return attention.enter_context(nc.sbuf_tensor(name, shape, dt))

            qs = [at(f"qs{u}", [SROWS, 2, NP, T], BF16) for u in range(2)]
            ks = [at(f"ks{u}", [SROWS, WIN + NP * T], BF16) for u in range(2)]
            k2s = [at(f"k2s{u}", [BIAS, NP, T], BF16) for u in range(2)]
            v = [at(f"v{u}", [P, NW, P]) for u in range(2)]
            maskq = at("maskq", [P, NW, P], BF16)
            maskk = at("maskk", [P, NW * 2, WIN], BF16)
            operands = (qs, ks, k2s, v)
            build_prep(nc, x_tiles, norm_w, Wq, Wk, Wv, Wqf, Wkf, X, ident, identb, mv, rstd, stats, half,
                       parts_dram, v_dram, operands, maskq, maskk)
            build_attention(nc, X, ident, identb, Wout, parts_dram, v_dram, negmax_dram, operands, maskq, maskk)
        w1s = sb("w1s", [P, E, 2, FFN])
        w2s = sb("w2s", [P, E, KF, P])
        xn = sb("xn", [P, NT, ROW])
        yg = sb("yg", [P, NT, P])
        first = (w1, w2, w1s, w2s)
        for name in ("ffn1", "ffn2"):
            build_route(nc, name, X, xn, ident, mv, rstd, stats, half, router_w, router_b, tokens, expert,
                        pmax, xn_dram[name], first)
            build_experts(nc, name, ident, w1s, w2s, expert, tokens, xn_dram[name], y_dram)
            if name == "ffn1":
                build_rwkv(nc, X, yg, y_dram, xn, ident, mv, rstd, stats, half, time_decay, time_first, mix_k, mix_v, mix_r,
                           Wk_b, Wv_b, Wr_b, Wo_b)
            else:
                build_combine(nc, name, X, yg, y_dram, out_tiles)
            first = None


GROUPS = [(kp, sum(k == kp for k, _ in PRODUCTS)) for kp in range(PARTS)]
assert PRODUCTS == [(kp, qp) for kp, n in GROUPS for qp in range(n)]
LOADS = 6 * len(GROUPS) + 1


def load_operands(sp, operands, parts_dram, v_dram, b, u, loaded):
    qs, ks, k2s, v = operands
    for hh in range(2):
        lo = hh * ROWS
        for kp, n in GROUPS:
            rows = slice(lo, lo + n * HD)
            part = parts_dram[:, bass.ds(b, 1)].rearrange("w b c (d x h) t -> w x (b c) d (h t)", x=2, h=NP)[:, hh]
            sp.dma_start(qs[u][rows, hh, :, :].rearrange("r h t -> r (h t)"), part[0, 0:n]).then_inc(loaded, 16)
            for dst, which in ((ks[u][rows, WIN:], 1), (k2s[u][rows, :, :].rearrange("r h t -> r (h t)"), 2)):
                src = part[which, kp:kp + 1].broadcast_to([n, HD, NP * T])
                sp.dma_start(dst, src).then_inc(loaded, 16)
            lo += n * HD
    sp.dma_start(v[u][:], v_dram[bass.ds(b, 1)].rearrange("b p w n -> p (b w) n")).then_inc(loaded, 16)


def build_attention(nc, X, ident, identb, Wout, parts_dram, v_dram, negmax_dram, operands, maskq, maskk):
    LIN = [[(0, 0)], [(1, 0)], [(2, 0), (3, 2 * P)]]
    NL = 4 * len(LIN)
    NU = NL + 4
    MAX_AFTER = (5, 6, 7, 8, 9, 10, 11, 15)
    RP = 4
    LAG = 3
    SUM = 16

    def schedule(first, last, slot):
        jobs = []
        for n in range(NU):
            jobs += [("unit", n, 0), ("unit", n, 1)]
            if n == 0:
                jobs.append(("negmax", 0, 0))
            if not first:
                if n in (1, 3):
                    jobs.append(("norm", n // 2, 0))
                if n == 5:
                    jobs.append(("back", 0, 0))
                if n == 7:
                    jobs.append(("out", 0, 0))
            if n in MAX_AFTER and not last:
                jobs.append(("max", MAX_AFTER.index(n), 0))
        return [(*job, (slot + k) % 2) for k, job in enumerate(jobs)]

    FIRST, EVEN, ODD, LAST = (schedule(*at) for at in ((True, False, 1), (False, False, 1), (False, False, 0), (False, True, 0)))
    assert len(FIRST) % 2 == len(ODD) % 2 == len(EVEN) % 2 == len(LAST) % 2 == 1

    def batches(engine, body):
        body(0, 0, 0, FIRST)
        with engine.Fori(0, B // 2 - 1) as i:
            body(i * 2 + 1, i, 1, ODD)
            body(i * 2 + 2, i + 1, 0, EVEN)
        body(B - 1, B // 2 - 1, 1, LAST)

    with ExitStack() as ctx:
        def sb(name, shape, dt=F32):
            return ctx.enter_context(nc.sbuf_tensor(name, shape, dt))

        def sem(name):
            return ctx.enter_context(nc.semaphore(name))

        def both(name):
            return [sem(name + "_even"), sem(name + "_odd")]

        sc = ctx.enter_context(nc.psum_tensor("scores", [P, 2, 1024], F32))
        acc = ctx.enter_context(nc.psum_tensor("acc", [P, 2, 2, T], F32))
        qs, ks, k2s, v = operands
        qm = sb("qm", [BIAS, NP, NW, 2, WIN], BF16)
        vpad = [sb(f"vpad{u}", [P, NW, H, 32]) for u in range(2)]
        prob = sb("prob", [P, RP, 2, 1024])
        mx = sb("mx", [P, 2, NP, NW])
        nm = sb("nm", [NP * NW, 2, PARTS, P], BF16)
        nr = sb("nr", [NP * NW, P])
        sums_sb = sb("sums_sb", [P, 2, 2, T])
        den, rden = sb("den", [P, TPB * H]), sb("rden", [P, TPB * H])
        ytok = sb("ytok", [P, 2, TPB, P])
        yT = sb("yT", [P, 2, T])
        wo = sb("wo", [P, 2, P])
        loaded, nm_stored, nm_loaded = both("loaded"), both("negmax_stored"), both("negmax_loaded")
        wo_s, pch, vch = (sem(n) for n in ("wout_loaded", "pool_steps", "dve_steps"))
        sp_go, pool_go, pe_go = sem("sp_goes"), sem("pool_goes"), sem("pe_goes")
        vpad_s, masked_s, qm_s = sem("vpad_ready"), sem("lin_masked"), sem("qm_ready")
        mjob, tjob, ujob, njob, bjob, ojob = (sem(n) for n in (
            "max_scores", "negmax_transposed", "unit_scores", "sums_transposed", "y_transposed", "out_ready"))
        maxed, split_s, exped, normed, backed, added = (sem(n) for n in (
            "max_done", "negmax_split", "weights_ready", "normalised", "yT_ready", "out_added"))
        pv_s = sem("unit_summed")
        copied = (sem("lin_sums_copied"), sem("win_sums_copied"))
        block = ctx.enter_context(nc.Block())

        @block.sync
        def _(sp):
            for y in range(2):
                for g in range(4):
                    lo = 64 * y + SUM * g
                    sp.dma_start(wo[lo:lo + SUM, :, :], Wout.rearrange("(k g y r) n -> g y r k n", k=2, g=4, y=2)[g, y])\
                        .then_inc(wo_s, 16)
            load_operands(sp, operands, parts_dram, v_dram, 1, 1, loaded[1])
            with sp.Fori(0, B // 2 - 1) as i:
                for u in range(2):
                    b = i * 2 + u + 1
                    sp.wait_ge(exped, b * (2 * NU))
                    sp.sem_inc(sp_go, 1)
                    load_operands(sp, operands, parts_dram, v_dram, b + 1, u, loaded[u])

        @block.gpsimd
        def _(pool):
            ch = Chain(pool, pch)
            def spread(k, u):
                for s in range(2):
                    nc.gpsimd.tensor_copy(
                        vpad[u][:].rearrange("p w (h s) r -> p (w h) s r", s=2)[:, :, s, SUM * s:SUM * s + HD],
                        v[u][:].rearrange("p w (h s d) -> p (w h) s d", s=2, d=HD)[:, :, s, :]).then_inc(vpad_s, 1)

            for u in range(2):
                ch.link(nc.gpsimd.memset(vpad[u][:], 0.0))
                for s in range(2):
                    ch.link(nc.gpsimd.memset(vpad[u][:].rearrange("p w (h s) r -> p (w h) s r", s=2)
                                             [:, :, s, SUM * s + HD:SUM * s + HD + 1], 1.0))
            spread(0, 0)

            def body(b, k, u, jobs):
                for kind, n, a, slot in jobs:
                    if kind != "unit" or n >= NL:
                        continue
                    pool.wait_ge(exped, b * (2 * NU) + 2 * n + a + 1)
                    pool.sem_inc(pool_go, 1)
                    for kc, col in LIN[n % len(LIN)]:
                        m = prob[:, n % RP, a, :].rearrange("p (h n) -> p h n", h=2)[:, :, col:col + P]
                        sel = nc.gpsimd.affine_select(out=m, in_=m, compare_op=ALU.is_ge, fill=0.0, base=0,
                                                      pattern=[[0, 2], [1, P]], channel_multiplier=-1)
                    sel.then_inc(masked_s, 1)
                if jobs is not LAST:
                    pool.wait_ge(loaded[1 - u], k * (16 * LOADS) + 16 * LOADS)
                    if jobs is not FIRST:
                        pool.sem_inc(pool_go, 1)
                        pool.wait_ge(pv_s, b * NU)
                        pool.sem_inc(pool_go, 1)
                    spread(k, 1 - u)

            batches(pool, body)

        @block.scalar
        def _(act):
            def back(count, slot):
                act.wait_ge(bjob, count)
                nc.scalar.activation(yT[:].rearrange("p k t -> p (k t)"), sc[:, slot, :], ACT.Copy).then_inc(backed, 1)

            def body(b, k, u, jobs):
                for kind, n, a, slot in jobs:
                    if kind == "unit":
                        act.wait_ge(ujob, b * (2 * NU) + 2 * n + a + 1)
                        if jobs is not FIRST or n >= RP:
                            act.wait_ge(pv_s, b * NU + n - RP + 1)
                        if n < NL:
                            w = max(col + (TPB - kc) * P for kc, col in LIN[n % len(LIN)])
                            nc.scalar.activation(prob[:, n % RP, a, :].rearrange("p (h n) -> p h n", h=2)[:, :, 0:w],
                                                 sc[:, slot, :].rearrange("p (h n) -> p h n", h=2)[:, :, 0:w],
                                                 ACT.Square, bias=1.0).then_inc(exped, 1)
                        else:
                            nc.scalar.activation(prob[:, n % RP, a, :], sc[:, slot, :], ACT.Exp,
                                                 scale=float(HD) ** -0.5).then_inc(exped, 1)
                    if kind == "back":
                        back(b, slot)
                    if (kind, n, a) == ("unit", 2, 0):
                        act.wait_ge(split_s, b + 1)
                        for hh in range(2):
                            act.dma_start(negmax_dram[bass.ds(b, 1), hh].rearrange("b c k q -> k (b c) q"),
                                          nm[:, u, :, WIN * hh:WIN * hh + WIN]).then_inc(nm_stored[u], 16)
                    if (kind, n, a) == ("unit", 5, 0):
                        act.wait_ge(nm_stored[u], k * 32 + 32)
                        for hh in range(2):
                            lo = BIAS + PARTS * hh
                            act.dma_start(qs[u][lo:lo + PARTS, hh, :, :].rearrange("c p t -> c (p t)"),
                                          negmax_dram[bass.ds(b, 1), hh].rearrange("b c k q -> (b c) (k q)"))\
                                .then_inc(nm_loaded[u], 16)

            batches(act, body)
            back(B, 1)

        @block.vector
        def _(dve):
            V = nc.vector
            ch = Chain(dve, vch)
            CHAINED = 3 + 2 + 2

            def copy_sums(k, count):
                dve.wait_ge(pv_s, count)
                V.tensor_copy(sums_sb[:, k].rearrange("p y t -> p (y t)"), acc[:, k].rearrange("p y t -> p (y t)"))\
                    .then_inc(copied[k], 1)

            def normalise(k, count, slot):
                dve.wait_ge(njob, count)
                s = sc[:, slot, :].rearrange("p (h r) -> p h r", r=SUM)
                ch.link(V.tensor_scalar(den[:], s[:, :, HD], EPS_LIN if k == 0 else 0.0, None, ALU.add))
                ch.link(V.reciprocal(rden[:], den[:]))
                V.tensor_tensor(ytok[:, k].rearrange("p t (h d) -> p (t h) d", d=HD), s[:, :, 0:HD],
                                rden[:].unsqueeze(2).broadcast_to([P, TPB * H, HD]), ALU.mult).then_inc(normed, 1)

            def q_side_by_side(u):
                for hh in range(2):
                    last = V.tensor_copy(qm[:, :, :, hh, :].rearrange("r p w q -> r (p w) q"),
                                         qs[u][0:BIAS, hh].rearrange("r p (w q) -> r (p w) q", q=WIN))
                last.then_inc(qm_s, 1)

            def maximum(count, u, m, slot):
                dve.wait_ge(mjob, count)
                V.tensor_reduce(mx[:, u, m, :], sc[:, slot, :].rearrange("p (w k) -> p w k", w=NW),
                                AX.X, ALU.max, negate=True).then_inc(maxed, 1)

            def add_out(b, slot):
                x = X[:, bass.ds(b * TPB, TPB), :].rearrange("p t d -> p (t d)")
                V.tensor_tensor(x, sc[:, slot, 0:T], x, ALU.add).then_inc(added, 1)

            q_side_by_side(0)
            for m in range(NP):
                maximum(m + 1, 0, m, (m + 1) % 2)

            def body(b, k, u, jobs):
                ch.at(0 if jobs is FIRST else b * CHAINED - 4)
                for kind, n, a, slot in jobs:
                    if kind == "negmax":
                        dve.wait_ge(tjob, b + 1)
                        tr = sc[0:NP * NW, slot, 0:P]
                        ch.link(V.tensor_copy(nm[:, u, 0, :], tr))
                        ch.link(V.tensor_tensor(nr[:], tr, nm[:, u, 0, :], ALU.subtract))
                        ch.link(V.tensor_copy(nm[:, u, 1, :], nr[:]))
                        V.tensor_tensor(nm[:, u, 2, :], nr[:], nm[:, u, 1, :], ALU.subtract).then_inc(split_s, 1)
                    if kind == "norm":
                        normalise(n, b * 2 - 1 + n, slot)
                    if kind == "out":
                        dve.wait_ge(ojob, b)
                        add_out(b - 1, slot)
                    if kind == "max":
                        if n == 0:
                            dve.wait_ge(loaded[1 - u], k * (16 * LOADS) + 16 * LOADS)
                            q_side_by_side(1 - u)
                        maximum(b * NP + NP + n + 1, 1 - u, n, slot)
                    if (kind, n, a) == ("unit", LAG, 0) and jobs is not FIRST:
                        copy_sums(1, b * NU)
                    if (kind, n, a) == ("unit", NL - 1 + LAG, 1):
                        copy_sums(0, b * NU + NL)

            batches(dve, body)
            ch.at(B * CHAINED - 4)
            copy_sums(1, B * NU)
            normalise(0, 2 * B - 1, 1)
            normalise(1, 2 * B, 0)
            dve.wait_ge(ojob, B)
            add_out(B - 1, 0)

        @block.tensor
        def _(pe):
            free = [None, None]

            def take(slot, reader, value):
                if free[slot]:
                    pe.wait_ge(*free[slot])
                    pe.sem_inc(pe_go, 1)
                free[slot] = (reader, value)

            def lin_scores(u, j, part, a, slot):
                p = j + 4 * a
                for kc, col in LIN[part]:
                    for hh in range(2):
                        at = T * hh + col
                        mm = nc.tensor.matmul(sc[:, slot, at:at + T - P * kc], k2s[u][:, p, P * kc:P * kc + P],
                                              qs[u][0:BIAS, hh, p, P * kc:], start=True, stop=True)
                return mm

            def win_scores(u, j, a, slot):
                p = j + 4 * a
                for f in range(2):
                    nc.tensor.matmul(sc[:, slot, T * f:T * f + T], identb[:], maskk[:, NW * f:NW * f + NW, :],
                                     start=True, stop=False, skip_group_check=True)
                    for w in range(4 * f, 4 * f + 4):
                        mm = nc.tensor.matmul(sc[:, slot, P * w:P * w + P], ks[u][:, T * p + WIN * w:T * p + WIN * w + P],
                                              qs[u][:, :, p, WIN * w:WIN * w + WIN], start=False, stop=True,
                                              skip_group_check=True)
                return mm

            def max_scores(u, m, slot):
                for f in range(2):
                    nc.tensor.matmul(sc[:, slot, T * f:T * f + T], identb[:], maskq[:, 4 * f:4 * f + 4, :],
                                     start=True, stop=False, skip_group_check=True)
                    for w in range(4 * f, 4 * f + 4):
                        mm = nc.tensor.matmul(sc[:, slot, P * w:P * w + P],
                                              qm[:, m, w, :, :].rearrange("r h q -> r (h q)"),
                                              ks[u][0:BIAS, T * m + WIN * w:T * m + WIN * w + P], start=False, stop=True,
                                              skip_group_check=True)
                return mm

            def sums(u, n):
                if n < NL:
                    j, todo = n // len(LIN), [(2 * kc + 1, P * kc, T - P * kc, [T * hh + col for hh in range(2)])
                                              for kc, col in LIN[n % len(LIN)]]
                    k, opens = 0, n % len(LIN) == 0 and j % 2 == 0
                else:
                    j, todo = n - NL, [(w, WIN * w, WIN, [P * w + WIN * hh for hh in range(2)]) for w in range(NW)]
                    k, opens = 1, j % 2 == 0
                for x, (w, col, width, at) in enumerate(todo):
                    for a in range(2):
                        for hh in range(2):
                            g = a + 2 * hh
                            mm = nc.tensor.matmul(acc[32 * g:32 * g + 32, k, j // 2, col:col + width],
                                                  vpad[u][:, w, 4 * g + j, :], prob[:, n % RP, a, at[hh]:at[hh] + width],
                                                  start=opens and x == 0, stop=True, skip_group_check=True)
                return mm

            def norm_job(k, slot):
                for t in range(TPB):
                    for y in range(2):
                        tr = nc.tensor.transpose(sc[:, slot, P * (2 * t + y):P * (2 * t + y) + P],
                                                 sums_sb[:, k, y, P * t:P * t + P], ident[:])
                return tr

            def back_job(slot):
                for k in range(2):
                    for t in range(TPB):
                        at = T * k + P * t
                        tr = nc.tensor.transpose(sc[:, slot, at:at + P], ytok[:, k, t, :], ident[:])
                return tr

            def out_job(slot):
                for t in range(TPB):
                    for k in range(2):
                        mm = nc.tensor.matmul(sc[:, slot, P * t:P * t + P], yT[:, k, P * t:P * t + P], wo[:, k, :],
                                              start=k == 0, stop=k == 1)
                return mm

            pe.wait_ge(wo_s, 8 * 16)
            pe.wait_ge(qm_s, 1)
            for m in range(NP):
                slot = (m + 1) % 2
                take(slot, maxed, m + 1)
                max_scores(0, m, slot).then_inc(mjob, 1)

            def body(b, k, u, jobs):
                if jobs is not FIRST:
                    free[jobs[0][3]] = (exped, b * (2 * NU))
                    free[1 - jobs[0][3]] = (maxed, b * NP + NP)
                for at, (kind, n, a, slot) in enumerate(jobs):
                    if kind == "unit":
                        if n == NL and a == 0:
                            pe.wait_ge(nm_loaded[u], k * 32 + 32)
                        take(slot, exped, b * (2 * NU) + 2 * n + a + 1)
                        if n < NL:
                            lin_scores(u, n // len(LIN), n % len(LIN), a, slot).then_inc(ujob, 1)
                        else:
                            win_scores(u, n - NL, a, slot).then_inc(ujob, 1)
                    if kind == "unit" and a == 0:
                        if n >= LAG:
                            unit_sums(b, u, n - LAG, jobs)
                        elif jobs is not FIRST:
                            unit_sums(b - 1, 1 - u, n + NU - LAG, jobs)
                    if kind == "negmax":
                        take(slot, split_s, b + 1)
                        pe.wait_ge(maxed, b * NP + NP)
                        pe.sem_inc(pe_go, 1)
                        nc.tensor.transpose(sc[0:NP * NW, slot, 0:P], mx[:, u, :, :].rearrange("p m w -> p (m w)"),
                                            ident[:]).then_inc(tjob, 1)
                    if kind == "norm":
                        take(slot, normed, b * 2 - 1 + n)
                        pe.wait_ge(copied[n], b)
                        pe.sem_inc(pe_go, 1)
                        norm_job(n, slot).then_inc(njob, 1)
                    if kind == "back":
                        take(slot, backed, b)
                        pe.wait_ge(normed, b * 2)
                        pe.sem_inc(pe_go, 1)
                        back_job(slot).then_inc(bjob, 1)
                    if kind == "out":
                        take(slot, added, b)
                        pe.wait_ge(backed, b)
                        pe.sem_inc(pe_go, 1)
                        out_job(slot).then_inc(ojob, 1)
                    if kind == "max":
                        take(slot, maxed, b * NP + NP + n + 1)
                        if n == 0:
                            pe.wait_ge(qm_s, b + 2)
                            pe.sem_inc(pe_go, 1)
                        max_scores(1 - u, n, slot).then_inc(mjob, 1)

            def unit_sums(b, u, m, jobs):
                if m == 0:
                    pe.wait_ge(vpad_s, b * 2 + 2)
                    if jobs is not FIRST:
                        pe.wait_ge(copied[0], b)
                if m == NL and jobs is not FIRST:
                    pe.wait_ge(copied[1], b)
                if m < NL:
                    pe.wait_ge(masked_s, b * (2 * NL) + 2 * m + 2)
                else:
                    pe.wait_ge(exped, b * (2 * NU) + 2 * m + 2)
                sums(u, m).then_inc(pv_s, 1)

            batches(pe, body)
            for m in range(NU - LAG, NU):
                unit_sums(B - 1, 1, m, LAST)
            pe.wait_ge(exped, B * 2 * NU - 1)
            pe.wait_ge(copied[0], B)
            norm_job(0, 1).then_inc(njob, 1)
            pe.wait_ge(exped, B * 2 * NU)
            pe.wait_ge(copied[1], B)
            norm_job(1, 0).then_inc(njob, 1)
            pe.wait_ge(normed, 2 * B)
            back_job(1).then_inc(bjob, 1)
            pe.wait_ge(backed, B)
            out_job(0).then_inc(ojob, 1)


def normalise_tokens(nc, dve, ch, X, xn, stats, mv, rstd, stat_s, scale_s, xn_s, ready=None):
    for q in range(LN + 1):
        if q < LN:
            if ready:
                ready(q)
            part_stats(nc, ch, X, stats, mv, q).then_inc(stat_s, 1)
        if q:
            dve.wait_ge(scale_s, q)
            for t in range(LNT * (q - 1), LNT * q):
                k = nc.vector.tensor_scalar(xn[:, t, 0:P], X[:, t, :], mv[:, t, 0:1], rstd[:, t:t + 1],
                                            ALU.subtract, ALU.mult)
                if t % TPB == TPB - 1:
                    k.then_inc(xn_s, 1)


def norm_scale(nc, pool, ch, mv, rstd, half, q, stat_s, scale_s):
    part = slice(LNT * q, LNT * q + LNT)
    pool.wait_ge(stat_s, q + 1)
    ch.link(nc.gpsimd.tensor_scalar(rstd[:, part], mv[:, part, 1], EPS_LN, None, ALU.add))
    nc.gpsimd.tensor_tensor(rstd[:, part], rstd[:, part], half[:, part], ALU.pow).then_inc(scale_s, 1)


def build_route(nc, name, X, xn, ident, mv, rstd, stats, half, router_w, router_b, tokens, expert,
                pmax, xn_dram, weights):
    with ExitStack() as ctx:
        def sb(n, shape, dt=F32):
            return ctx.enter_context(nc.sbuf_tensor(f"{name}_{n}", shape, dt))

        def sem(n):
            return ctx.enter_context(nc.semaphore(f"{name}_{n}"))

        trp = ctx.enter_context(nc.psum_tensor(f"{name}_trp", [P, 2, T], F32))
        logit_ps = ctx.enter_context(nc.psum_tensor(f"{name}_logit_ps", [P, NT, E], F32))
        cnt_ps = ctx.enter_context(nc.psum_tensor(f"{name}_cnt_ps", [P, 2, 512], F32))
        token_ps = ctx.enter_context(nc.psum_tensor(f"{name}_token_ps", [P, 3, SLOTS], F32))
        xT = sb("xT", [P, 2, T])
        rw, rb = sb("rw", [P, E]), sb("rb", [P, E])
        logit, ex, eq, cand = (sb(n, [P, NT, E]) for n in ("logit", "ex", "eq", "cand"))
        best, total = sb("best", [P, NT]), sb("total", [P, NT])
        weight = sb("weight", [P, E])
        hot = sb("hot", [P, E, NT])
        hotb = sb("hotb", [P, E, NT], BF16)
        before, oneb = sb("before", [P, P], BF16), sb("oneb", [P, P], BF16)
        ones = sb("ones", [P, E * NT])
        tot, cum, place = (sb(n, [P, E, NT]) for n in ("tot", "cum", "place"))
        count, tiles, end, off = (sb(n, [P, E]) for n in ("count", "tiles", "end", "off"))
        steps = sb("steps", [P, NT])
        slotno = sb("slotno", [1, SLOTS])
        ended, past = sb("ended", [1, SLOTS, E]), sb("past", [1, SLOTS])
        slotf, lane = sb("slotf", [P, NT]), sb("lane", [P, NT])
        edge = sb("edge", [P, SLOTS + 1])
        reached = sb("reached", [P, NT, SLOTS + 1], BF16)
        intile = sb("intile", [P, NT, 3, SLOTS], BF16)
        lanes = sb("lanes", [P, P])
        atlane = sb("atlane", [P, NT, P], BF16)
        tileno, part = sb("tileno", [P, NT], BF16), sb("part", [P, 1])
        token, found, back = sb("token", [P, SLOTS]), sb("found", [P, 3, SLOTS]), sb("back", [P, SLOTS])
        spare = sb("spare", [P, SLOTS])
        r_in, w_in, stat_s, scale_s, xn_s, tr_s, xT_s, logit_s = (sem(n) for n in (
            "router_loaded", "weights_loaded", "stats_done", "scales_done", "xn_ready", "xn_transposed", "xT_ready",
            "logits_ready"))
        tile_s, lane_s, token_s, pmax_s, xn_out = (sem(n) for n in (
            "tiles_marked", "lanes_marked", "tokens_psum", "pmax_ready", "tokens_stored"))
        const_s, pch, vch, shift_s, exp_s, hot_s, cnt_s = (sem(n) for n in (
            "consts", "pool_steps", "dve_steps", "logits_shifted", "exp_done", "hot_ready", "counts_ready"))
        block = ctx.enter_context(nc.Block())

        @block.sync
        def _(sp):
            sp.dma_start(rw[:], router_w).then_inc(r_in, 16)
            sp.dma_start(rb[:], router_b.partition_broadcast(P)).then_inc(r_in, 16)
            if weights:
                w1, w2, w1s, w2s = weights
                for e in range(E):
                    sp.dma_start(w1s[:, e, :, :].rearrange("p a n -> p (a n)"), w1[e]).then_inc(w_in, 16)
                    sp.dma_start(w2s[:, e, :, :], w2[e].rearrange("(k p) n -> p k n", p=P)).then_inc(w_in, 16)
            sp.wait_ge(pmax_s, 1)
            for q in range(LN):
                sp.dma_start(xn_dram[LNT * P * q:LNT * P * (q + 1), :].rearrange("(t p) d -> p t d", p=P),
                             xn[:, LNT * q:LNT * q + LNT, :]).then_inc(xn_out, 16)
            if weights:
                sp.wait_ge(w_in, 32 * E)
            sp.wait_ge(xn_out, 16 * LN)

        @block.gpsimd
        def _(pool):
            ch = Chain(pool, pch)
            ch.link(nc.gpsimd.memset(before[:], 1.0))
            nc.gpsimd.affine_select(out=before[:], in_=before[:], compare_op=ALU.is_gt, fill=0.0, base=0,
                                    pattern=[[1, P]], channel_multiplier=-1).then_inc(const_s, 1)
            nc.gpsimd.memset(oneb[:], 1.0).then_inc(const_s, 1)
            nc.gpsimd.memset(ones[:], 1.0).then_inc(const_s, 1)
            nc.gpsimd.iota(weight[:], [[-1, E]], base=E, channel_multiplier=0,
                           allow_small_or_imprecise_dtypes=True).then_inc(const_s, 1)
            nc.gpsimd.iota(steps[:], [[P, NT]], base=0, channel_multiplier=0,
                           allow_small_or_imprecise_dtypes=True).then_inc(const_s, 1)
            ch.link(nc.gpsimd.iota(slotno[:], [[1, SLOTS]], base=0, channel_multiplier=0,
                                   allow_small_or_imprecise_dtypes=True))
            for dst, step, base, mul in ((edge, P, 0, 0), (lanes, 1, -P, 0), (tileno, 1, 0, 0), (part, 1, 0, 1),
                                         (spare, P, NT * P, 1)):
                nc.gpsimd.iota(dst[:], [[step, dst.shape[-1]]], base=base, channel_multiplier=mul,
                               allow_small_or_imprecise_dtypes=True).then_inc(const_s, 1)
            for q in range(LN):
                norm_scale(nc, pool, ch, mv, rstd, half, q, stat_s, scale_s)

        @block.scalar
        def _(act):
            for b in range(B):
                act.wait_ge(tr_s, b + 1)
                if b >= 2:
                    act.wait_ge(logit_s, b - 1)
                nc.scalar.activation(xT[:, b % 2, :], trp[:, b % 2, :], ACT.Copy).then_inc(xT_s, 1)
            act.wait_ge(shift_s, 1)
            nc.scalar.activation(ex[:], ex[:], ACT.Exp).then_inc(exp_s, 1)
            act.wait_ge(tile_s, 1)
            act.wait_ge(const_s, 10)
            nc.scalar.activation(intile[:, :, 1, :], intile[:, :, 2, :], ACT.Copy, scale=part[:]).then_inc(lane_s, 1)

        @block.tensor
        def _(pe):
            pe.wait_ge(r_in, 32)
            for b in range(B + 1):
                if b < B:
                    pe.wait_ge(xn_s, b + 1)
                    if b >= 2:
                        pe.wait_ge(xT_s, b - 1)
                    for t in range(TPB):
                        tr = nc.tensor.transpose(trp[:, b % 2, P * t:P * t + P], xn[:, TPB * b + t, 0:P], ident[:])
                    tr.then_inc(tr_s, 1)
                if b:
                    pe.wait_ge(xT_s, b)
                    for t in range(TPB):
                        mm = nc.tensor.matmul(logit_ps[:, TPB * (b - 1) + t, :], xT[:, (b - 1) % 2, P * t:P * t + P],
                                              rw[:], start=True, stop=True)
                    mm.then_inc(logit_s, 1)
            pe.wait_ge(hot_s, 1)
            pe.wait_ge(const_s, 2)
            h = hotb[:].rearrange("p e t -> p (e t)")
            nc.tensor.matmul(cnt_ps[:, 0, 0:E * NT], before[:], h, start=True, stop=True).then_inc(cnt_s, 1)
            nc.tensor.matmul(cnt_ps[:, 1, 0:E * NT], oneb[:], h, start=True, stop=True).then_inc(cnt_s, 1)
            pe.wait_ge(tile_s, 2)
            pe.wait_ge(lane_s, 1)
            for t in range(NT):
                if t % TPB == 0:
                    pe.wait_ge(tile_s, 3 + t // TPB)
                mm = nc.tensor.matmul(token_ps[:].rearrange("p a s -> p (a s)"), atlane[:, t, :],
                                      intile[:, t, :, :].rearrange("p a s -> p (a s)"), start=t == 0, stop=t == NT - 1)
            mm.then_inc(token_s, 1)

        @block.vector
        def _(dve):
            V = nc.vector
            ch = Chain(dve, vch)
            normalise_tokens(nc, dve, ch, X, xn, stats, mv, rstd, stat_s, scale_s, xn_s)
            dve.wait_ge(logit_s, B)
            dve.wait_ge(r_in, 32)
            dve.wait_ge(const_s, 10)
            wide = [P, NT, E]
            ch.link(V.tensor_tensor(logit[:], logit_ps[:], rb[:].unsqueeze(1).broadcast_to(wide), ALU.add))
            ch.link(V.tensor_reduce(best[:], logit[:], AX.X, ALU.max))
            top = best[:].unsqueeze(2).broadcast_to(wide)
            V.tensor_tensor(ex[:], logit[:], top, ALU.subtract).then_inc(shift_s, 1)
            ch.link(V.tensor_tensor(eq[:], logit[:], top, ALU.is_equal))
            ch.link(V.tensor_tensor(cand[:], eq[:], weight[:].unsqueeze(1).broadcast_to(wide), ALU.mult))
            ch.link(V.tensor_reduce(total[:], cand[:], AX.X, ALU.max))
            ch.link(V.tensor_tensor(hot[:].rearrange("p e t -> p t e"), cand[:], total[:].unsqueeze(2).broadcast_to(wide),
                                    ALU.is_equal))
            V.tensor_copy(hotb[:], hot[:]).then_inc(hot_s, 1)
            dve.wait_ge(exp_s, 1)
            ch.link(V.tensor_reduce(total[:], ex[:], AX.X, ALU.add))
            ch.link(V.reciprocal(pmax[:], total[:]))
            V.tensor_copy(xn[:, :, P], pmax[:]).then_inc(pmax_s, 1)
            dve.wait_ge(cnt_s, 2)
            ch.link(V.tensor_copy(tot[:].rearrange("p e t -> p (e t)"), cnt_ps[:, 1, 0:E * NT]))
            ch.link(V.tensor_tensor_scan(cum[:].rearrange("p e t -> p (e t)"), ones[:],
                                         tot[:].rearrange("p e t -> p (e t)"), 0.0, ALU.mult, ALU.add))
            ch.link(V.tensor_reduce(count[:], tot[:], AX.X, ALU.add))
            ch.link(V.tensor_tensor(place[:], count[:].unsqueeze(2).broadcast_to([P, E, NT]),
                                    steps[:].unsqueeze(1).broadcast_to([P, E, NT]), ALU.is_gt))
            ch.link(V.tensor_reduce(tiles[:], place[:], AX.X, ALU.add))
            ch.link(V.tensor_tensor_scan(end[:], ones[:, 0:E], tiles[:], 0.0, ALU.mult, ALU.add))
            ch.link(V.tensor_tensor(off[:], end[:], tiles[:], ALU.subtract))
            ch.link(V.tensor_scalar(off[:], off[:], float(P), None, ALU.mult))
            ch.link(V.tensor_tensor(off[:], off[:], cum[:, :, NT - 1], ALU.subtract))
            ch.link(V.tensor_tensor(off[:], off[:], count[:], ALU.add))
            ch.link(V.tensor_tensor(place[:], cum[:], tot[:], ALU.subtract))
            ch.link(V.tensor_tensor(place[:], place[:], off[:].unsqueeze(2).broadcast_to([P, E, NT]), ALU.add))
            ch.link(V.tensor_tensor(place[:].rearrange("p e t -> p (e t)"), cnt_ps[:, 0, 0:E * NT],
                                    place[:].rearrange("p e t -> p (e t)"), ALU.add))
            ch.link(V.tensor_tensor(place[:], place[:], hot[:], ALU.mult))
            ch.link(V.tensor_reduce(slotf[:], place[:].rearrange("p e t -> p t e"), AX.X, ALU.add))
            edges = [P, NT, SLOTS + 1]
            ch.link(V.tensor_tensor(reached[:], slotf[:].unsqueeze(2).broadcast_to(edges),
                                    edge[:].unsqueeze(1).broadcast_to(edges), ALU.is_ge))
            V.tensor_tensor(intile[:, :, 2, :], reached[:, :, 0:SLOTS], reached[:, :, 1:], ALU.subtract).then_inc(tile_s, 1)
            dve.wait_ge(tile_s, 1)
            V.tensor_tensor(intile[:, :, 0, :], intile[:, :, 2, :], tileno[:].unsqueeze(2).broadcast_to([P, NT, SLOTS]),
                            ALU.mult).then_inc(tile_s, 1)
            ch.link(V.tensor_reduce(lane[:], reached[:], AX.X, ALU.add))
            ch.link(V.scalar_tensor_tensor(lane[:], lane[:], -float(P), slotf[:], ALU.mult, ALU.add))
            for t in range(NT):
                at = V.tensor_scalar(atlane[:, t, :], lanes[:], lane[:, t:t + 1], None, ALU.is_equal)
                if t % TPB == TPB - 1:
                    at.then_inc(tile_s, 1)
            dve.wait_ge(pch, 2)
            ch.link(V.tensor_tensor(ended[:], slotno[:].unsqueeze(2).broadcast_to([1, SLOTS, E]),
                                    end[0:1, :].unsqueeze(1).broadcast_to([1, SLOTS, E]), ALU.is_ge))
            ch.link(V.tensor_reduce(past[:], ended[:], AX.X, ALU.add))
            ch.link(V.tensor_scalar(past[:], past[:], float(E - 1), None, ALU.min))
            ch.link(V.tensor_copy(expert[:], past[:]))
            dve.wait_ge(token_s, 1)
            ch.link(V.tensor_copy(found[:], token_ps[:]))
            ch.link(V.scalar_tensor_tensor(token[:], found[:, 0, :], float(P), found[:, 1, :], ALU.mult, ALU.add))
            V.tensor_copy(tokens[:, :, 0], token[:])
            ch.link(V.scalar_tensor_tensor(back[:], found[:, 2, :], -1.0, spare[:], ALU.add, ALU.mult))
            V.tensor_tensor(tokens[:, :, 1], token[:], back[:], ALU.subtract)


def build_experts(nc, name, ident, w1s, w2s, expert, tokens, xn_dram, y_dram):
    R = 8
    Q = 4
    AHEAD = 4
    with ExitStack() as ctx:
        def sb(n, shape, dt=F32):
            return ctx.enter_context(nc.sbuf_tensor(f"{name}_{n}", shape, dt))

        sems = []

        def sem(n):
            sems.append(nc.alloc_semaphore(f"{name}_{n}"))
            return sems[-1]

        ctx.callback(nc.all_engine_barrier)
        ctx.callback(nc.clear_and_free_semaphores, sems)

        up = ctx.enter_context(nc.psum_tensor(f"{name}_up", [P, 2, 2, FFN], F32))
        hid_ps = ctx.enter_context(nc.psum_tensor(f"{name}_hid_ps", [P, KF, P], F32))
        xT_ps = ctx.enter_context(nc.psum_tensor(f"{name}_xT_ps", [P, 512], F32))
        y_ps = ctx.enter_context(nc.psum_tensor(f"{name}_y_ps", [P, 2, 512], F32))
        xt, xT = sb("xt", [P, R, ROW]), sb("xTs", [P, R, P])
        index = sb("index", [P, R, 2], U32)
        sa, hg, hgT, yo = sb("sa", [P, Q, FFN]), sb("hg", [P, Q, FFN]), sb("hgT", [P, Q, KF, P]), sb("yo", [P, R, P])
        loaded = [sem(f"tile_loaded{u}") for u in range(R)]
        stored = [sem(f"tile_stored{u}") for u in range(R)]
        tr_s, xT_s, a_s, g_s, silu_s, hg_s, hgtr_s, hgT_s, y_s, yo_s, pch, pe_go, pool_go = (sem(n) for n in (
            "x_transposed", "xT_ready", "a_psum", "g_psum", "silu_done", "hidden_ready", "hidden_transposed",
            "hiddenT_ready", "y_psum", "y_ready", "pool_steps", "pe_goes", "pool_goes"))
        block = ctx.enter_context(nc.Block())

        def steps(engine, step):
            for i in (0, 1):
                for u in range(R):
                    step(i, u)
            with engine.Fori(2, (SLOTS + 1) // R - 1) as i:
                for u in range(R):
                    step(i, u)
            for u in range(R):
                step((SLOTS + 1) // R - 1, u)
            step((SLOTS + 1) // R, 0)

        def has(s, lo, hi=SLOTS):
            return not isinstance(s, int) or lo <= s < hi

        @block.gpsimd
        def _(pool):
            ch = Chain(pool, pch)

            def load(s, u):
                ch.link(nc.gpsimd.tensor_copy(index[:, u:u + 1, :], tokens[:, bass.ds(s, 1), :]))
                pool.sem_inc(pool_go, 1)
                nc.gpsimd.indirect_dma_start(
                    out=xt[:, u, :], out_offset=None, in_=xn_dram,
                    in_offset=bass.IndirectOffsetOnAxis(ap=index[:, u, 0:1], axis=0)).then_inc(loaded[u], 16)

            def step(i, u):
                s, a = i * R + u, (u + AHEAD) % R
                if has(s + AHEAD, 0):
                    if has(s + AHEAD, R):
                        pool.wait_ge(stored[a], (i + (u + AHEAD) // R) * 16)
                        pool.sem_inc(pool_go, 1)
                    ch.at(s + AHEAD)
                    load(s + AHEAD, a)
                if has(s, 0):
                    pool.wait_ge(yo_s, s + 1)
                    pool.sem_inc(pool_go, 1)
                    nc.gpsimd.indirect_dma_start(
                        out=y_dram, out_offset=bass.IndirectOffsetOnAxis(ap=index[:, u, 1:2], axis=0),
                        in_=yo[:, u, :], in_offset=None).then_inc(stored[u], 16)

            for s in range(AHEAD):
                load(s, s)
            steps(pool, step)
            for u in range(R):
                pool.wait_ge(stored[u], 16 * ((SLOTS - 1 - u) // R + 1))

        @block.scalar
        def _(act):
            def step(i, u):
                s, v = i * R + u, (u - 1) % Q
                if has(s, 0):
                    act.wait_ge(a_s, s + 1)
                    if has(s, Q):
                        act.wait_ge(hg_s, s - Q + 1)
                    nc.scalar.activation(sa[:, u % Q, :], up[:, u % 2, 0, :], ACT.Silu).then_inc(silu_s, 1)
                if has(s, 1, SLOTS + 1):
                    act.wait_ge(hgtr_s, s)
                    if has(s, Q + 1, SLOTS + 1):
                        act.wait_ge(y_s, s - Q)
                    nc.scalar.activation(hgT[:, v], hid_ps[:], ACT.Copy).then_inc(hgT_s, 1)
            steps(act, step)

        @block.vector
        def _(dve):
            def step(i, u):
                s, v, n = i * R + u, (u - 2) % R, (u + 1) % R
                if has(s, 0):
                    dve.wait_ge(g_s, s + 1)
                    dve.wait_ge(silu_s, s + 1)
                    if has(s, Q):
                        dve.wait_ge(hgtr_s, s - Q + 1)
                    nc.vector.tensor_tensor(hg[:, u % Q, :], up[:, u % 2, 1, :], sa[:, u % Q, :], ALU.mult).then_inc(hg_s, 1)
                if has(s, 0, SLOTS - 1):
                    dve.wait_ge(tr_s, s + 2)
                    if has(s, R - 1, SLOTS - 1):
                        dve.wait_ge(g_s, s - R + 2)
                    nc.vector.tensor_copy(xT[:, n, :], xT_ps[:, 0:P]).then_inc(xT_s, 1)
                if has(s, 2, SLOTS + 2):
                    dve.wait_ge(y_s, s - 1)
                    if has(s, R + 2, SLOTS + 2):
                        dve.wait_ge(stored[v], (i - 1) * 16 if u < 2 else i * 16)
                    nc.vector.tensor_scalar(yo[:, v, :], y_ps[:, v % 2, 0:P], xt[:, v, P:P + 1], None, ALU.mult)\
                        .then_inc(yo_s, 1)
            dve.wait_ge(tr_s, 1)
            nc.vector.tensor_copy(xT[:, 0, :], xT_ps[:, 0:P]).then_inc(xT_s, 1)
            steps(dve, step)

        @block.tensor
        def _(pe):
            def transpose_x(u):
                return nc.tensor.transpose(xT_ps[:, 0:P], xt[:, u, 0:P], ident[:])

            def slices(w, u, lo):
                e = pe.snap(number[u], min_val=0, max_val=E - 1)
                return [w[:, bass.ds(e, 1)].rearrange("p a k n -> p (a k) n")[:, k, :] for k in lo]

            number = [pe.alloc_register(f"{name}_expert{u}") for u in range(R)]

            def step(i, u):
                s, d, n = i * R + u, (u - 2) % R, (u + 1) % R
                if has(s, 0):
                    pe.reg_load(number[u], expert[0:1, bass.ds(s, 1)])
                    wa, wg = slices(w1s, u, (0, 1))
                    pe.wait_ge(xT_s, s + 1)
                    if has(s, 2):
                        pe.wait_ge(hg_s, s - 1)
                        pe.sem_inc(pe_go, 1)
                    nc.tensor.matmul(up[:, u % 2, 0, :], xT[:, u, :], wa, start=True, stop=True).then_inc(a_s, 1)
                if has(s, 1, SLOTS + 1):
                    pe.wait_ge(hg_s, s)
                    if has(s, 2, SLOTS + 1):
                        pe.wait_ge(hgT_s, s - 1)
                    pe.sem_inc(pe_go, 1)
                    for k in range(KF):
                        tr = nc.tensor.transpose(hid_ps[:, k, :], hg[:, (u - 1) % Q, P * k:P * k + P], ident[:])
                    tr.then_inc(hgtr_s, 1)
                if has(s, 0):
                    nc.tensor.matmul(up[:, u % 2, 1, :], xT[:, u, :], wg, start=True, stop=True).then_inc(g_s, 1)
                if has(s, 0, SLOTS - 1):
                    pe.wait_ge(loaded[n], (i + (u == R - 1)) * 16 + 16)
                    pe.wait_ge(xT_s, s + 1)
                    pe.sem_inc(pe_go, 1)
                    transpose_x(n).then_inc(tr_s, 1)
                if has(s, 2, SLOTS + 2):
                    wd = slices(w2s, d, range(KF))
                    pe.wait_ge(hgT_s, s - 1)
                    if has(s, 4, SLOTS + 2):
                        pe.wait_ge(yo_s, s - 3)
                    pe.sem_inc(pe_go, 1)
                    for k in range(KF):
                        mm = nc.tensor.matmul(y_ps[:, d % 2, 0:P], hgT[:, d % Q, k, :], wd[k], start=k == 0, stop=k == KF - 1)
                    mm.then_inc(y_s, 1)
            pe.wait_ge(loaded[0], 16)
            transpose_x(0).then_inc(tr_s, 1)
            steps(pe, step)


def build_combine(nc, name, X, yg, y_dram, out_tiles):
    Q = 8
    with ExitStack() as ctx:
        got = [ctx.enter_context(nc.semaphore(f"{name}_gathered{q}")) for q in range(NT // Q)]
        add_s, out_s = (ctx.enter_context(nc.semaphore(f"{name}_{n}")) for n in ("added", "out_stored"))
        block = ctx.enter_context(nc.Block())

        @block.sync
        def _(sp):
            for q in range(NT // Q):
                sp.dma_start(yg[:, Q * q:Q * q + Q, :],
                             y_dram[Q * P * q:Q * P * (q + 1), :].rearrange("(t p) d -> p t d", p=P)).then_inc(got[q], 16)
            for q in range(NT // Q):
                sp.wait_ge(add_s, q + 1)
                sp.dma_start(out_tiles[:, Q * q:Q * q + Q, :], X[:, Q * q:Q * q + Q, :]).then_inc(out_s, 16)
            sp.wait_ge(out_s, 16 * (NT // Q))

        @block.vector
        def _(dve):
            for q in range(NT // Q):
                dve.wait_ge(got[q], 16)
                x = X[:, Q * q:Q * q + Q, :]
                nc.vector.tensor_tensor(x, x, yg[:, Q * q:Q * q + Q, :], ALU.add).then_inc(add_s, 1)


def build_rwkv(nc, X, yg, y_dram, xn, ident, mv, rstd, stats, half, time_decay, time_first, mix_k, mix_v, mix_r,
               Wk_b, Wv_b, Wr_b, Wo_b):
    def batches(engine, body):
        for u in range(2):
            body(u, 0, u, True, False)
        with engine.Fori(1, B // 2 - 1) as i:
            for u in range(2):
                body(i * 2 + u, i, u, False, False)
        for u in range(2):
            body(B - 2 + u, B // 2 - 1, u, False, True)

    with ExitStack() as ctx:
        def sb(n, shape, dt=F32):
            return ctx.enter_context(nc.sbuf_tensor(f"rwkv_{n}", shape, dt))

        sems = []

        def sem(n):
            sems.append(nc.alloc_semaphore(f"rwkv_{n}"))
            return sems[-1]

        ctx.callback(nc.all_engine_barrier)
        ctx.callback(nc.clear_and_free_semaphores, sems)

        ps = ctx.enter_context(nc.psum_tensor("rwkv_ps", [P, 2, 3, T], F32))
        ops = ctx.enter_context(nc.psum_tensor("rwkv_out", [P, 2, T], F32))
        wraw = sb("wraw", [P, 4, P])
        wT = sb("wT", [P, 4, P])
        wcur, wold = sb("wcur", [P, 3, P]), sb("wold", [P, 3, P])
        mix, old = sb("mix", [P, 3]), sb("old", [P, 3])
        td, tf, lam = sb("td", [P, 1]), sb("tf", [P, 1]), sb("lam", [P, 1])
        etd, etf = sb("etd", [P, 1]), sb("etf", [P, 1])
        lamw, onew = sb("lamw", [P, T]), sb("onew", [P, T])
        xT = sb("xT", [P, B, 1 + T])
        kmin, kc, kv, fkc, fkv = (sb(n, [P, 2, T]) for n in ("kmin", "kc", "kv", "fkc", "fkv"))
        er, er1, num, rd, o = (sb(n, [P, 2, T]) for n in ("er", "er1", "num", "rd", "o"))
        sk, sv = sb("sk", [P, 2, 1 + T]), sb("sv", [P, 2, 1 + T])
        dn, dr = sb("dn", [P, 2, T]), sb("dr", [P, 2, T])
        w_in, tr_s, w_s, stat_s, scale_s, xn_s, xtr_s, xT_s = (sem(n) for n in (
            "loaded", "w_transposed", "w_ready", "stats_done", "scales_done", "xn_ready", "x_transposed",
            "xT_ready"))
        got = [sem(f"gathered{q}") for q in range(LN)]
        k_s, v_s, r_s, kmin_s, kc_s, er_s, er1_s, kv_s, fkc_s, fkv_s, sk_s, sv_s, num_s, dr_s, rd_s, o_s, out_s, add_s, x_s = (
            sem(n) for n in ("k_psum", "v_psum", "r_psum", "k_clamped", "k_exp", "r_exp", "r_exp_plus_one", "kv_ready",
                             "first_k", "first_kv", "k_scanned", "kv_scanned", "numerator", "denominator", "reciprocal", "o_ready", "out_psum", "added",
                             "experts_added"))
        pch, vch, ach, lam_s = (sem(n) for n in ("pool_steps", "dve_steps", "act_steps", "lam_ready"))
        pool_go = sem("pool_goes")
        block = ctx.enter_context(nc.Block())

        @block.sync
        def _(sp):
            for q in range(LN):
                sp.dma_start(yg[:, LNT * q:LNT * q + LNT, :],
                             y_dram[LNT * P * q:LNT * P * (q + 1), :].rearrange("(t p) d -> p t d", p=P)).then_inc(got[q], 16)
            for k, w in enumerate((Wk_b, Wv_b, Wr_b, Wo_b)):
                sp.dma_start(wraw[:, k, :], w).then_inc(w_in, 16)
            for k, m in enumerate((mix_k, mix_v, mix_r)):
                sp.dma_start(mix[:, k:k + 1], m.rearrange("a b c -> c (a b)")).then_inc(w_in, 16)
            sp.dma_start(td[:], time_decay).then_inc(w_in, 16)
            sp.dma_start(tf[:], time_first).then_inc(w_in, 16)

        @block.gpsimd
        def _(pool):
            ch = Chain(pool, pch)
            for q in range(LN + 1):
                if q < LN:
                    pool.wait_ge(got[q], 16)
                    x = X[:, LNT * q:LNT * q + LNT, :]
                    nc.gpsimd.tensor_tensor(x, x, yg[:, LNT * q:LNT * q + LNT, :], ALU.add).then_inc(x_s, 1)
                if q:
                    norm_scale(nc, pool, ch, mv, rstd, half, q - 1, stat_s, scale_s)

            done = ch.n
            CHAINED = 2

            def output(b, u):
                pool.wait_ge(rd_s, b + 1)
                pool.sem_inc(pool_go, 1)
                nc.gpsimd.tensor_tensor(o[:, u, :], num[:, u, :], rd[:, u, :], ALU.mult).then_inc(o_s, 1)

            def body(b, k, u, first, last):
                ch.at(done + b * CHAINED)
                pool.wait_ge(fkc_s, b + 1)
                pool.wait_ge(sk_s, b + 1)
                if not first:
                    pool.wait_ge(dr_s, b - 1)
                pool.sem_inc(pool_go, 1)
                ch.link(nc.gpsimd.tensor_tensor(dn[:, u, :], fkc[:, u, :], sk[:, u, 0:T], ALU.add))
                pool.sem_inc(pool_go, 1)
                ch.link(nc.gpsimd.tensor_scalar(dn[:, u, :], dn[:, u, :], EPS_RWKV, None, ALU.add))
                pool.wait_ge(er1_s, b + 1)
                if not first:
                    pool.wait_ge(rd_s, b - 1)
                pool.sem_inc(pool_go, 1)
                nc.gpsimd.tensor_tensor(dr[:, u, :], dn[:, u, :], er1[:, u, :], ALU.mult).then_inc(dr_s, 1)
                pool.wait_ge(fkv_s, b + 1)
                if not first:
                    pool.wait_ge(o_s, b - 1)
                pool.wait_ge(sv_s, b + 1)
                pool.sem_inc(pool_go, 1)
                nc.gpsimd.tensor_tensor(num[:, u, :], fkv[:, u, :], sv[:, u, 0:T], ALU.add).then_inc(num_s, 1)
                if not (first and u == 0):
                    output(b - 1, 1 - u)

            batches(pool, body)
            pool.wait_ge(num_s, B)
            output(B - 1, 1)

        @block.scalar
        def _(act):
            ch = Chain(act, ach)
            act.wait_ge(w_in, 16 * 9)
            ch.link(nc.scalar.activation(etd[:], td[:], ACT.Exp))
            nc.scalar.activation(etf[:], tf[:], ACT.Exp).then_inc(lam_s, 1)
            nc.scalar.activation(lam[:], etd[:], ACT.Exp, scale=-1.0).then_inc(lam_s, 1)
            for b in range(B):
                act.wait_ge(xtr_s, b + 1)
                nc.scalar.activation(xT[:, b, 1:], ops[:, b % 2, :], ACT.Copy).then_inc(xT_s, 1)
            act.wait_ge(lam_s, 2)

            def body(b, k, u, first, last):
                act.wait_ge(kmin_s, b + 1)
                if not first:
                    act.wait_ge(sv_s, b - 1)
                nc.scalar.activation(kc[:, u, :], kmin[:, u, :], ACT.Exp).then_inc(kc_s, 1)
                act.wait_ge(kc_s, b + 1)
                if not first:
                    act.wait_ge(dr_s, b - 1)
                nc.scalar.activation(fkc[:, u, :], kc[:, u, :], ACT.Copy, scale=etf[:]).then_inc(fkc_s, 1)
                act.wait_ge(r_s, b + 1)
                nc.scalar.activation(er[:, u, :], ps[:, u, 2, :], ACT.Exp, scale=-1.0).then_inc(er_s, 1)
                act.wait_ge(er_s, b + 1)
                nc.scalar.activation(er1[:, u, :], er[:, u, :], ACT.Copy, bias=1.0).then_inc(er1_s, 1)
                act.wait_ge(kv_s, b + 1)
                if not first:
                    act.wait_ge(num_s, b - 1)
                nc.scalar.activation(fkv[:, u, :], kv[:, u, :], ACT.Copy, scale=etf[:]).then_inc(fkv_s, 1)

            batches(act, body)

        @block.tensor
        def _(pe):
            pe.wait_ge(w_in, 16 * 9)
            for k in range(4):
                tr = nc.tensor.transpose(ps[:, 0, 0, P * k:P * k + P], wraw[:, k, :], ident[:])
            tr.then_inc(tr_s, 1)
            for b in range(B):
                pe.wait_ge(xn_s, b + 1)
                if b >= 2:
                    pe.wait_ge(xT_s, b - 1)
                for t in range(TPB):
                    tr = nc.tensor.transpose(ops[:, b % 2, P * t:P * t + P], xn[:, TPB * b + t, 0:P], ident[:])
                tr.then_inc(xtr_s, 1)

            def products(b, u):
                for k, s in enumerate((k_s, v_s, r_s)):
                    cur = xT[:, bass.ds(b, 1), 1:].rearrange("p a t -> p (a t)")
                    prev = xT[:, bass.ds(b, 1), 0:T].rearrange("p a t -> p (a t)")
                    nc.tensor.matmul(ps[:, u, k, :], wcur[:, k, :], cur, start=True, stop=False)
                    nc.tensor.matmul(ps[:, u, k, :], wold[:, k, :], prev, start=False, stop=True).then_inc(s, 1)

            def body(b, k, u, first, last):
                if not last:
                    pe.wait_ge(kv_s, b + 1)
                    pe.wait_ge(er_s, b + 1)
                    products(b + 2, u)
                pe.wait_ge(o_s, b + 1)
                if not first:
                    pe.wait_ge(add_s, b - 1)
                for t in range(TPB):
                    mm = nc.tensor.matmul(ops[:, u, P * t:P * t + P], o[:, u, P * t:P * t + P], wT[:, 3, :],
                                          start=True, stop=True)
                mm.then_inc(out_s, 1)

            pe.wait_ge(w_s, 1)
            pe.wait_ge(xT_s, B)
            products(0, 0)
            products(1, 1)
            batches(pe, body)

        @block.vector
        def _(dve):
            V = nc.vector
            ch = Chain(dve, vch)
            V.memset(xT[:, :, 0], 0.0)
            V.memset(sk[:, :, 0], 0.0)
            V.memset(sv[:, :, 0], 0.0)
            V.memset(onew[:], 1.0)
            normalise_tokens(nc, dve, ch, X, xn, stats, mv, rstd, stat_s, scale_s, xn_s,
                             lambda q: dve.wait_ge(x_s, q + 1))
            dve.wait_ge(w_in, 16 * 9)
            ch.link(V.tensor_scalar(old[:], mix[:], -1.0, 1.0, ALU.mult, ALU.add))
            dve.wait_ge(tr_s, 1)
            ch.link(V.tensor_copy(wT[:].rearrange("p k n -> p (k n)"), ps[:, 0, 0, :]))
            for k in range(3):
                V.tensor_scalar(wcur[:, k, :], wT[:, k, :], mix[:, k:k + 1], None, ALU.mult)
                w = V.tensor_scalar(wold[:, k, :], wT[:, k, :], old[:, k:k + 1], None, ALU.mult)
            w.then_inc(w_s, 1)
            dve.wait_ge(lam_s, 2)
            ch.link(V.tensor_scalar(lamw[:], onew[:], lam[:], None, ALU.mult))

            def clamp(b, u):
                dve.wait_ge(k_s, b + 1)
                V.tensor_scalar(kmin[:, u, :], ps[:, u, 0, :], K_CLAMP, None, ALU.min).then_inc(kmin_s, 1)

            def reciprocal(b, u):
                dve.wait_ge(dr_s, b + 1)
                V.reciprocal(rd[:, u, :], dr[:, u, :]).then_inc(rd_s, 1)

            def add_out(b, u):
                dve.wait_ge(out_s, b + 1)
                x = X[:, bass.ds(b * TPB, TPB), :].rearrange("p t d -> p (t d)")
                V.tensor_tensor(x, ops[:, u, :], x, ALU.add).then_inc(add_s, 1)

            def body(b, k, u, first, last):
                if not first:
                    dve.wait_ge(num_s, b - 1)
                dve.wait_ge(kc_s, b + 1)
                dve.wait_ge(v_s, b + 1)
                V.tensor_tensor(kv[:, u, :], ps[:, u, 1, :], kc[:, u, :], ALU.mult).then_inc(kv_s, 1)
                V.tensor_tensor_scan(sk[:, u, 1:], lamw[:], kc[:, u, :], 0.0, ALU.mult, ALU.add).then_inc(sk_s, 1)
                dve.wait_ge(kv_s, b + 1)
                V.tensor_tensor_scan(sv[:, u, 1:], lamw[:], kv[:, u, :], 0.0, ALU.mult, ALU.add).then_inc(sv_s, 1)
                if not (first and u == 0):
                    reciprocal(b - 1, 1 - u)
                if not (last and u == 1):
                    clamp(b + 1, 1 - u)
                if not first:
                    add_out(b - 2, u)

            clamp(0, 0)
            batches(dve, body)
            reciprocal(B - 1, 1)
            add_out(B - 2, 0)
            add_out(B - 1, 1)


def build_prep(nc, x_tiles, norm_w, Wq, Wk, Wv, Wqf, Wkf, X, ident, identb, mv, rstd, stats, half,
               parts_dram, v_dram, operands, maskq, maskk):
    def batches(engine, body):
        for u in range(2):
            body(u, 0, u, True, False)
        with engine.Fori(1, B // 2 - 1) as i:
            for u in range(2):
                body(i * 2 + u, i, u, False, False)
        for u in range(2):
            body(B - 2 + u, B // 2 - 1, u, False, True)

    with ExitStack() as ctx:
        def sb(name, shape, dt=F32):
            return ctx.enter_context(nc.sbuf_tensor(name, shape, dt))

        def sem(name):
            return ctx.enter_context(nc.semaphore(name))

        ps = ctx.enter_context(nc.psum_tensor("prep_ps", [P, 8, 512], F32))
        wq, wk, wv = sb("wq", [P, P]), sb("wk", [P, P]), sb("wv", [P, P])
        nw = sb("nw", [P, 1])
        wqfT, wkfT = sb("wqfT", [FEAT, HD]), sb("wkfT", [FEAT, HD])
        qrep, krep = sb("qrep", [FEAT, HD, H]), sb("krep", [FEAT, HD, H])
        wqp, wkp = sb("wqp", [P, P]), sb("wkp", [P, P])
        same = sb("same", [P, H])
        feat = sb("feat", [P, P])
        r2 = sb("r2", [P, NT])
        t1 = sb("t1", [P, NT])
        hs = sb("hs", [P, NT])
        hn = sb("hn", [P, 2, TPB, P])
        xl = sb("xl", [P, NT, P])
        hT = sb("hT", [P, 2, WIN + T])
        kT = sb("kT", [P, 2, T])
        parts = sb("parts", [P, 2, 3, PARTS, T], BF16)
        rem = sb("rem", [P, 3, T])
        vs = sb("vs", [P, 2, NW, P])
        x_in_s, w_in_s = [sem(f"x_loaded{q}") for q in range(LN)], sem("w_loaded")
        const_s, pch, vch = sem("consts"), sem("pool_steps"), sem("dve_steps")
        stat_s, scale_s = sem("stats_done"), sem("scales_done")
        feat_ps, feat_s = sem("feat_psum"), sem("feat_done")
        hn_s, hnT_s, hT_s = sem("hn_ready"), sem("hnT_psum"), sem("hT_ready")
        q_s, k_s, kT_s, k2_s, v_s = (sem("q_psum"), sem("k_psum"), sem("kT_ready"), sem("k2_psum"),
                                     sem("v_psum"))
        part1_s, split_s, vs_s = sem("first_part"), sem("split_done"), sem("v_ready")
        stored = [sem("stored_even"), sem("stored_odd")]
        pads_s, loaded_s = sem("pads_ready"), sem("first_loaded")
        sp_go, pe_go = sem("prep_sp_goes"), sem("prep_pe_goes")
        qs, ks, k2s, v = operands
        block = ctx.enter_context(nc.Block())

        @block.sync
        def _(sp):
            for q in range(LN):
                sp.dma_start(X[:, LNT * q:LNT * q + LNT, :], x_tiles[:, LNT * q:LNT * q + LNT, :]).then_inc(x_in_s[q], 16)
            for dst, src in ((wq, Wq), (wk, Wk), (wv, Wv)):
                sp.dma_start(dst[:], src).then_inc(w_in_s, 16)
            sp.dma_start(nw[:], norm_w.rearrange("(p a) -> p a", a=1)).then_inc(w_in_s, 16)
            with nc.allow_non_contiguous_dma("128 numbers"):
                sp.dma_start(wqfT[:], Wqf.rearrange("d f -> f d")).then_inc(w_in_s, 16)
                sp.dma_start(wkfT[:], Wkf.rearrange("d f -> f d")).then_inc(w_in_s, 16)

            def store(i):
                for u in range(2):
                    b = i * 2 + u
                    for x, n in enumerate((1, 0, 2)):
                        sp.wait_ge(split_s, b * 3 + x + 1)
                        sp.sem_inc(sp_go, 1)
                        sp.dma_start(parts_dram[n, bass.ds(b, 1)].rearrange("b c p t -> p (b c) t"), parts[:, u, n])\
                            .then_inc(stored[u], 16)
                    sp.wait_ge(vs_s, b * 2 + 2)
                    sp.sem_inc(sp_go, 1)
                    sp.dma_start(v_dram[bass.ds(b, 1)].rearrange("b p w n -> p (b w) n"), vs[:, u]).then_inc(stored[u], 16)

            for i in range(2):
                store(i)
            sp.wait_ge(stored[0], 16 * 4)
            sp.wait_ge(pads_s, 1)
            load_operands(sp, operands, parts_dram, v_dram, 0, 0, loaded_s)
            with sp.Fori(2, B // 2) as i:
                store(i)
            for u in range(2):
                sp.wait_ge(stored[u], 16 * 4 * B // 2)
            sp.wait_ge(loaded_s, 16 * LOADS)

        @block.gpsimd
        def _(pool):
            ch = Chain(pool, pch)
            nc.gpsimd.memset(half[:], -0.5)
            nc.gpsimd.memset(hT[:, :, 0:WIN], 0.0)
            ch.link(nc.gpsimd.memset(same[:], 0.0))
            ch.link(nc.gpsimd.memset(ident[:], 0.0))
            nc.gpsimd.affine_select(out=ident[:], in_=ident[:], compare_op=ALU.not_equal, fill=1.0,
                                    base=0, pattern=[[-1, P]], channel_multiplier=1)
            for d in range(HD):
                ch.link(nc.gpsimd.affine_select(out=same[:], in_=same[:], compare_op=ALU.not_equal, fill=0.5,
                                                base=-H * d, pattern=[[-1, H]], channel_multiplier=1))
            nc.gpsimd.tensor_copy(identb[:], ident[:]).then_inc(const_s, 1)
            for q in range(LN):
                part = slice(LNT * q, LNT * q + LNT)
                pool.wait_ge(stat_s, q + 1)
                ch.link(nc.gpsimd.tensor_scalar(t1[:, part], mv[:, part, 1], EPS_LN, None, ALU.add))
                ch.link(nc.gpsimd.tensor_tensor(rstd[:, part], t1[:, part], half[:, part], ALU.pow))
                ch.link(nc.gpsimd.tensor_tensor(t1[:, part], rstd[:, part], rstd[:, part], ALU.mult))
                ch.link(nc.gpsimd.tensor_tensor(t1[:, part], t1[:, part], mv[:, part, 1], ALU.mult))
                ch.link(nc.gpsimd.tensor_scalar(t1[:, part], t1[:, part], EPS_RMS, None, ALU.add))
                ch.link(nc.gpsimd.tensor_tensor(r2[:, part], t1[:, part], half[:, part], ALU.pow))
                nc.gpsimd.tensor_tensor(hs[:, part], rstd[:, part], r2[:, part], ALU.mult).then_inc(scale_s, 1)
            for u in range(2):
                ch.link(nc.gpsimd.memset(qs[u][:], 0.0))
                ch.link(nc.gpsimd.memset(ks[u][0:BIAS, 0:WIN], 0.0))
                ch.link(nc.gpsimd.memset(ks[u][BIAS:SROWS, :], 1.0))
            pool.sem_inc(pads_s, 1)
            ch.link(nc.gpsimd.memset(maskq[:], 0.0))
            ch.link(nc.gpsimd.memset(maskk[:], 0.0))
            for lo in (0, WIN):
                m = maskq[lo:lo + WIN, :, :]
                ch.link(nc.gpsimd.affine_select(out=m, in_=m, compare_op=ALU.is_ge, fill=NEG, base=0,
                                                pattern=[[0, NW], [1, P]], channel_multiplier=-1))
                ch.link(nc.gpsimd.affine_select(out=m, in_=m, compare_op=ALU.is_ge, fill=NEG, base=WIN,
                                                pattern=[[0, NW], [-1, P]], channel_multiplier=1))
            ch.link(nc.gpsimd.affine_select(out=maskk[:], in_=maskk[:], compare_op=ALU.is_ge, fill=NEG, base=0,
                                            pattern=[[0, NW * 2], [-1, WIN]], channel_multiplier=1))
            ch.link(nc.gpsimd.affine_select(out=maskk[:], in_=maskk[:], compare_op=ALU.is_ge, fill=NEG, base=WIN,
                                            pattern=[[0, NW * 2], [1, WIN]], channel_multiplier=-1))
            ch.link(nc.gpsimd.memset(maskq[:, 0, 0:WIN], NEG))
            ch.link(nc.gpsimd.memset(maskk[0:WIN, 0:2, :], NEG))
            ch.link(nc.gpsimd.tensor_tensor(xl[:], X[:], mv[:, :, 0:1].broadcast_to([P, NT, P]), ALU.subtract))
            ch.link(nc.gpsimd.tensor_tensor(xl[:], xl[:], rstd[:].unsqueeze(2).broadcast_to([P, NT, P]), ALU.mult))
            for q in range(LN):
                part = slice(LNT * q, LNT * q + LNT)
                pool.wait_ge(hn_s, (q + 1) * (LNT // TPB))
                nc.gpsimd.tensor_tensor(X[:, part, :], X[:, part, :], xl[:, part, :], ALU.add)

        @block.scalar
        def _(act):
            def transposed(b, u):
                act.wait_ge(hnT_s, b + 1)
                nc.scalar.activation(hT[:, u, WIN:], ps[:, 0, :], ACT.Copy).then_inc(hT_s, 1)

            def body(b, k, u, first, last):
                act.wait_ge(k_s, b + 1)
                nc.scalar.activation(kT[:, u, :], ps[:, 2, :], ACT.Copy).then_inc(kT_s, 1)
                if not first:
                    act.wait_ge(stored[u], k * (16 * 4))
                nc.scalar.activation(parts[:, u, 1, 0, :], ps[:, 2, :], ACT.Copy).then_inc(part1_s, 1)
                act.wait_ge(q_s, b + 1)
                nc.scalar.activation(parts[:, u, 0, 0, :], ps[:, 1, :], ACT.Copy).then_inc(part1_s, 1)
                if not (last and u == 1):
                    transposed(b + 1, 1 - u)
                act.wait_ge(k2_s, b + 1)
                nc.scalar.activation(parts[:, u, 2, 0, :], ps[:, 3, :], ACT.Copy).then_inc(part1_s, 1)
                for q in range(2):
                    act.wait_ge(v_s, b * 2 + q + 1)
                    nc.scalar.activation(vs[:, u, 4 * q:4 * q + 4, :], ps[:, 4 + q, :], ACT.Copy).then_inc(vs_s, 1)

            transposed(0, 0)
            batches(act, body)

        @block.vector
        def _(dve):
            ch = Chain(dve, vch)
            for q in range(LN):
                dve.wait_ge(x_in_s[q], 16)
                part_stats(nc, ch, X, stats, mv, q).then_inc(stat_s, 1)
            dve.wait_ge(w_in_s, 96)
            for dst, w in ((wqp, wq), (wkp, wk)):
                nc.vector.tensor_scalar(dst[:].rearrange("p (d h) -> p h d", h=H), w[:].rearrange("p (h d) -> p h d", d=HD),
                                        nw[:], None, ALU.mult)
            nc.vector.tensor_scalar(wv[:], wv[:], nw[:], None, ALU.mult)
            nc.vector.tensor_copy(qrep[:], wqfT[:].unsqueeze(2).broadcast_to([FEAT, HD, H]))
            nc.vector.tensor_copy(krep[:], wkfT[:].unsqueeze(2).broadcast_to([FEAT, HD, H]))\
                .then_inc(feat_s, 1)
            dve.wait_ge(const_s, 1)
            dve.wait_ge(feat_ps, 1)
            nc.vector.tensor_tensor(feat[:].rearrange("p (d h) -> p d h", h=H), ps[:, 7, 0:P].rearrange("p (d h) -> p d h", h=H),
                                    same[:].unsqueeze(1).broadcast_to([P, HD, H]), ALU.mult).then_inc(feat_s, 1)
            dve.wait_ge(scale_s, 1)
            done = ch.n

            def normalise(b, u):
                for t in range(TPB):
                    k = b * TPB + t
                    h = nc.vector.tensor_scalar(hn[:, u, t, :], X[:, k, :], mv[:, k, 0:1], hs[:, bass.ds(k, 1)],
                                                ALU.subtract, ALU.mult)
                h.then_inc(hn_s, 1)

            def body(b, k, u, first, last):
                ch.at(done + b * 6)
                for x, n in enumerate((1, 0, 2)):
                    dve.wait_ge(part1_s, b * 3 + x + 1)
                    ch.link(nc.vector.tensor_tensor(rem[:, n, :], ps[:, 1 + n, :], parts[:, u, n, 0, :], ALU.subtract))
                    ch.link(nc.vector.tensor_copy(parts[:, u, n, 1, :], rem[:, n, :]))
                    nc.vector.tensor_tensor(parts[:, u, n, 2, :], rem[:, n, :], parts[:, u, n, 1, :],
                                            ALU.subtract).then_inc(split_s, 1)
                    if n == 0 and not last:
                        dve.wait_ge(hnT_s, b + 1)
                        normalise(b + 2, u)

            normalise(0, 0)
            normalise(1, 1)
            dve.wait_ge(scale_s, LN)
            batches(dve, body)

        @block.tensor
        def _(pe):
            def transpose(b, u):
                pe.wait_ge(hn_s, b + 1)
                pe.sem_inc(pe_go, 1)
                for t in range(TPB):
                    tr = nc.tensor.transpose(ps[:, 0, P * t:P * t + P], hn[:, u, t, :], ident[:])
                tr.then_inc(hnT_s, 1)

            def body(b, k, u, first, last):
                first = first and u == 0
                pe.wait_ge(hT_s, b + 1)
                if not first:
                    pe.wait_ge(split_s, b * 3 - 2)
                nc.tensor.matmul(ps[:, 2, :], wkp[:], hT[:, u, WIN:], start=True, stop=True).then_inc(k_s, 1)
                if not first:
                    pe.wait_ge(split_s, b * 3 - 1)
                nc.tensor.matmul(ps[:, 1, :], wqp[:], hT[:, u, WIN:], start=True, stop=True).then_inc(q_s, 1)
                if not (last and u == 1):
                    transpose(b + 1, 1 - u)
                pe.wait_ge(kT_s, b + 1)
                if not first:
                    pe.wait_ge(split_s, b * 3)
                nc.tensor.matmul(ps[:, 3, :], feat[:], kT[:, u, :], start=True, stop=True).then_inc(k2_s, 1)
                for q in range(2):
                    if not first:
                        pe.wait_ge(vs_s, b * 2 - 1 + q)
                    for w in range(4):
                        lo = WIN * (4 * q + w)
                        mm = nc.tensor.matmul(ps[:, 4 + q, P * w:P * w + P], hT[:, u, lo:lo + P], wv[:],
                                              start=True, stop=True)
                    mm.then_inc(v_s, 1)

            pe.wait_ge(feat_s, 1)
            nc.tensor.matmul(ps[:, 7, 0:P], krep[:].rearrange("f d h -> f (d h)"), qrep[:].rearrange("f d h -> f (d h)"), start=True, stop=True).then_inc(feat_ps, 1)
            pe.wait_ge(feat_s, 2)
            pe.wait_ge(const_s, 1)
            transpose(0, 0)
            batches(pe, body)


_INS = ['L0_attn_a_x','L0_attn_a_norm_w','L0_attn_a_Wq','L0_attn_a_Wk','L0_attn_a_Wv','L0_attn_a_Wqf','L0_attn_a_Wkf','L0_attn_a_Wout','L0_attn_b_xk','L0_attn_b_xv','L0_attn_b_time_decay','L0_attn_b_time_first','L0_attn_b_time_mix_k','L0_attn_b_time_mix_v','L0_attn_b_time_mix_r','L0_attn_b_Wk','L0_attn_b_Wv','L0_attn_b_Wr','L0_attn_b_Wo','L0_ffn_router_w','L0_ffn_router_b','L0_ffn_w1','L0_ffn_w2']

def kernel(**inputs):
    import numpy as _np
    import concourse.bacc as _bacc
    from concourse import mybir as _mybir
    from concourse.bass_utils import run_bass_kernel_spmd as _run
    nc = _bacc.Bacc("TRN2", target_bir_lowering=False, num_devices=1)
    arrays, args = {}, []
    for name in _INS:
        a = _np.ascontiguousarray(inputs[name])
        arrays[f"in_{name}_dram"] = a
        args.append(nc.dram_tensor(f"in_{name}_dram", a.shape, _mybir.dt.from_np(a.dtype), kind="ExternalInput").ap())
    out = nc.dram_tensor("out_dram", (8, 512, 128), _mybir.dt.float32, kind="ExternalOutput").ap()
    build(nc, *args, out)
    r = _run(nc, [arrays], core_ids=[0])
    return r.results[0]["out_dram"]
```
